# Optimizing a Trainium2 kernel written in Bass

```python
import numpy as np
import jax
import jax.numpy as jnp

def _softmax(x, axis=-1):
    return jax.nn.softmax(x, axis=axis)

def _gelu(x):
    return jax.nn.gelu(x, approximate=True)

def _silu(x):
    return jax.nn.silu(x)

def _sigmoid(x):
    return jax.nn.sigmoid(x)

def _layernorm(x, axis=-1, eps=1e-05):
    m = jnp.mean(x, axis=axis, keepdims=True)
    v = jnp.var(x, axis=axis, keepdims=True)
    return (x - m) / jnp.sqrt(v + eps)

def _scatter_add(tgt, idx, src, axis=0):
    return tgt.at[idx].add(src)

def _segment_sum(src, seg, n):
    return jax.ops.segment_sum(src, seg, n)
kernel_name = 'mk_recurrent_d2_jaxref_r8_63f2a5'

def setup_inputs(seed: int=0):
    np.random.seed(seed)
    _w = jnp.asarray

    def _L0_attn_setup():
        import jax, jax.numpy as jnp
        import numpy as np
        EMB = 512
        HEADS = 32
        SCALE = 4
        D = EMB // HEADS
        HKV = HEADS // SCALE
        B, S = (2, 256)
        key = jax.random.key(seed)
        ks = jax.random.split(key, 7)
        std = 0.02
        return {'x': jax.random.normal(ks[0], (B, S, EMB), jnp.float32), 'Wq': jax.random.normal(ks[1], (EMB, D, HEADS), jnp.float32) * std, 'bq': jnp.zeros((D, HEADS), jnp.float32), 'Wk': jax.random.normal(ks[2], (EMB, D, HKV), jnp.float32) * std, 'bk': jnp.zeros((D, HKV), jnp.float32), 'Wv': jax.random.normal(ks[3], (EMB, D, HKV), jnp.float32) * std, 'bv': jnp.zeros((D, HKV), jnp.float32)}
    _L0_attn_in = _L0_attn_setup()

    def _L0_ffn_setup():
        import jax, jax.numpy as jnp
        import numpy as np
        B, S, D = (4, 256, 512)
        NUM_EXPERTS, TOP_K = (3, 2)

        def _expert_outputs(h, w1, b1, w2, b2):
            pre = jnp.einsum('bsd,edf->ebsf', h, w1) + b1[:, None, None, :]
            act = jnp.stack([jnp.tanh(pre[0]), jax.nn.gelu(pre[1], approximate=False), jax.nn.silu(pre[2])])
            return jnp.einsum('ebsf,efd->ebsd', act, w2) + b2[:, None, None, :]
        key = jax.random.key(seed)
        ks = jax.random.split(key, 8)
        scale_in = 1.0 / np.sqrt(D)
        scale_gate = 1.0 / np.sqrt(D + 1)
        return {'h': jax.random.normal(ks[0], (B, S, D), dtype=jnp.float32), 'gate_w': jax.random.uniform(ks[1], (D + 1, NUM_EXPERTS), minval=-scale_gate, maxval=scale_gate, dtype=jnp.float32), 'gate_b': jnp.zeros((NUM_EXPERTS,), dtype=jnp.float32), 'w1': jax.random.uniform(ks[2], (NUM_EXPERTS, D, D), minval=-scale_in, maxval=scale_in, dtype=jnp.float32), 'b1': jnp.zeros((NUM_EXPERTS, D), dtype=jnp.float32), 'w2': jax.random.uniform(ks[3], (NUM_EXPERTS, D, D), minval=-scale_in, maxval=scale_in, dtype=jnp.float32), 'b2': jnp.zeros((NUM_EXPERTS, D), dtype=jnp.float32)}
    _L0_ffn_in = _L0_ffn_setup()

    def _L1_attn_setup():
        import math
        import jax, jax.numpy as jnp
        import numpy as np
        B, T, E = (2, 256, 512)
        H, HKV = (32, 8)
        DH = E // H
        G = H // HKV
        ROPE_THETA = 500000.0
        ROPE_FACTOR = 32.0
        HI_FREQ_FACTOR = 4.0
        LO_FREQ_FACTOR = 1.0
        ORIG_CTX = 1024

        def _rope_cos_sin(t_len):
            inv_freq = 1.0 / ROPE_THETA ** (jnp.arange(0, DH, 2, dtype=jnp.float32) / DH)
            wavelen = 2.0 * math.pi / inv_freq
            cut_lo = ORIG_CTX / HI_FREQ_FACTOR
            cut_hi = ORIG_CTX / LO_FREQ_FACTOR
            inv_freq = jnp.where(wavelen > cut_hi, inv_freq / ROPE_FACTOR, inv_freq)
            smooth = (ORIG_CTX / wavelen - LO_FREQ_FACTOR) / (HI_FREQ_FACTOR - LO_FREQ_FACTOR)
            smoothed = (1.0 - smooth) * inv_freq / ROPE_FACTOR + smooth * inv_freq
            is_medium = ~(wavelen < cut_hi) & ~(wavelen > cut_lo)
            inv_freq = jnp.where(is_medium, smoothed, inv_freq)
            pos = jnp.arange(t_len, dtype=jnp.float32)
            freqs = pos[:, None] * inv_freq[None, :]
            emb = jnp.concatenate([freqs, freqs], axis=-1)
            return (jnp.cos(emb), jnp.sin(emb))

        def _rotate_half(x):
            x1, x2 = jnp.split(x, 2, axis=-1)
            return jnp.concatenate([-x2, x1], axis=-1)
        key = jax.random.key(seed)
        kx, kq, kk, kv, ko = jax.random.split(key, 5)
        w = lambda k, shape: jax.random.normal(k, shape, jnp.float32) * 0.02
        return {'x': jax.random.normal(kx, (B, T, E), jnp.float32), 'Wq': w(kq, (E, E)), 'Wk': w(kk, (HKV * DH, E)), 'Wv': w(kv, (HKV * DH, E)), 'Wo': w(ko, (E, E))}
    _L1_attn_in = _L1_attn_setup()

    def _L1_ffn_setup():
        import jax, jax.numpy as jnp
        import numpy as np
        HIDDEN = 512
        INTER = 1376
        GROUP = 128
        B, S = (4, 256)
        NIB = jnp.uint32(15)

        def _pack_rows(nib):
            r = nib.reshape(-1, 8, nib.shape[-1])
            shifts = (jnp.arange(8, dtype=jnp.uint32) * 4)[None, :, None]
            return jnp.sum(r << shifts, axis=1, dtype=jnp.uint32)

        def _pack_cols(nib):
            r = nib.reshape(nib.shape[0], -1, 8)
            shifts = (jnp.arange(8, dtype=jnp.uint32) * 4)[None, None, :]
            return jnp.sum(r << shifts, axis=2, dtype=jnp.uint32)

        def _dequant(qw, qz, sc, g_idx):
            shifts = jnp.arange(8, dtype=jnp.uint32) * 4
            wq = qw[:, None, :] >> shifts[None, :, None] & NIB
            wq = wq.reshape(-1, qw.shape[1]).astype(jnp.float32)
            zq = qz[:, :, None] >> shifts[None, None, :] & NIB
            zq = zq.reshape(qz.shape[0], -1).astype(jnp.float32) + 1.0
            return sc[g_idx] * (wq - zq[g_idx])
        key = jax.random.key(seed)
        ks = jax.random.split(key, 7)
        n_groups = HIDDEN // GROUP
        n_groups_d = INTER // GROUP
        x = jax.random.normal(ks[0], (B, S, HIDDEN), jnp.float32)
        nib_w_gu = jax.random.randint(ks[1], (HIDDEN, 2 * INTER), 0, 16).astype(jnp.uint32)
        nib_z_gu = jax.random.randint(ks[2], (n_groups, 2 * INTER), 0, 15).astype(jnp.uint32)
        qweight_gu = _pack_rows(nib_w_gu)
        qzeros_gu = _pack_cols(nib_z_gu)
        scales_gu = jax.random.uniform(ks[3], (n_groups, 2 * INTER), jnp.float32, 0.005, 0.02)
        g_idx_gu = jnp.arange(HIDDEN, dtype=jnp.int32) // GROUP
        nib_w_d = jax.random.randint(ks[4], (INTER, HIDDEN), 0, 16).astype(jnp.uint32)
        nib_z_d = jax.random.randint(ks[5], (n_groups_d, HIDDEN), 0, 15).astype(jnp.uint32)
        qweight_down = _pack_rows(nib_w_d)
        qzeros_down = _pack_cols(nib_z_d)
        scales_down = jax.random.uniform(ks[6], (n_groups_d, HIDDEN), jnp.float32, 0.005, 0.02)
        g_idx_down = jnp.arange(INTER, dtype=jnp.int32) // GROUP
        return {'x': x, 'qweight_gu': qweight_gu, 'qzeros_gu': qzeros_gu, 'scales_gu': scales_gu, 'g_idx_gu': g_idx_gu, 'qweight_down': qweight_down, 'qzeros_down': qzeros_down, 'scales_down': scales_down, 'g_idx_down': g_idx_down}
    _L1_ffn_in = _L1_ffn_setup()
    _d = {'L0_attn_x': _L0_attn_in['x'], 'L0_attn_Wq': _L0_attn_in['Wq'], 'L0_attn_bq': _L0_attn_in['bq'], 'L0_attn_Wk': _L0_attn_in['Wk'], 'L0_attn_bk': _L0_attn_in['bk'], 'L0_attn_Wv': _L0_attn_in['Wv'], 'L0_attn_bv': _L0_attn_in['bv'], 'L0_ffn_gate_w': _L0_ffn_in['gate_w'], 'L0_ffn_gate_b': _L0_ffn_in['gate_b'], 'L0_ffn_w1': _L0_ffn_in['w1'], 'L0_ffn_b1': _L0_ffn_in['b1'], 'L0_ffn_w2': _L0_ffn_in['w2'], 'L0_ffn_b2': _L0_ffn_in['b2'], 'L1_attn_Wq': _L1_attn_in['Wq'], 'L1_attn_Wk': _L1_attn_in['Wk'], 'L1_attn_Wv': _L1_attn_in['Wv'], 'L1_attn_Wo': _L1_attn_in['Wo'], 'L1_ffn_qweight_gu': _L1_ffn_in['qweight_gu'], 'L1_ffn_qzeros_gu': _L1_ffn_in['qzeros_gu'], 'L1_ffn_scales_gu': _L1_ffn_in['scales_gu'], 'L1_ffn_g_idx_gu': _L1_ffn_in['g_idx_gu'], 'L1_ffn_qweight_down': _L1_ffn_in['qweight_down'], 'L1_ffn_qzeros_down': _L1_ffn_in['qzeros_down'], 'L1_ffn_scales_down': _L1_ffn_in['scales_down'], 'L1_ffn_g_idx_down': _L1_ffn_in['g_idx_down']}
    _x0 = _d['L0_attn_x']
    _d['L0_attn_x'] = jax.random.normal(jax.random.fold_in(jax.random.key(seed), 1), (2, 1024, 512), dtype=_x0.dtype)
    del _x0
    return _d

def reference(L0_attn_x, L0_attn_Wq, L0_attn_bq, L0_attn_Wk, L0_attn_bk, L0_attn_Wv, L0_attn_bv, L0_ffn_gate_w, L0_ffn_gate_b, L0_ffn_w1, L0_ffn_b1, L0_ffn_w2, L0_ffn_b2, L1_attn_Wq, L1_attn_Wk, L1_attn_Wv, L1_attn_Wo, L1_ffn_qweight_gu, L1_ffn_qzeros_gu, L1_ffn_scales_gu, L1_ffn_g_idx_gu, L1_ffn_qweight_down, L1_ffn_qzeros_down, L1_ffn_scales_down, L1_ffn_g_idx_down):

    def _L0_attn_ref(x, Wq, bq, Wk, bk, Wv, bv):
        import jax, jax.numpy as jnp
        import numpy as np
        EMB = 512
        HEADS = 32
        SCALE = 4
        D = EMB // HEADS
        HKV = HEADS // SCALE
        B, S = (2, 256)
        q = jnp.einsum('bse,edh->bsdh', x, Wq) + bq
        k = jnp.einsum('bse,edh->bsdh', x, Wk) + bk
        v = jnp.einsum('bse,edh->bsdh', x, Wv) + bv
        k = jnp.repeat(k, SCALE, axis=-1)
        v = jnp.repeat(v, SCALE, axis=-1)
        scores = jnp.einsum('bsdh,bseh->bsde', q, k) / np.float32(np.sqrt(D))
        attn = jax.nn.softmax(scores, axis=-1)
        out = jnp.einsum('bsde,bseh->bsdh', attn, v)
        return out.reshape(x.shape[:-1] + (EMB,))

    def _L0_ffn_ref(h, gate_w, gate_b, w1, b1, w2, b2):
        import jax, jax.numpy as jnp
        import numpy as np
        B, S, D = (4, 256, 512)
        NUM_EXPERTS, TOP_K = (3, 2)

        def _expert_outputs(h, w1, b1, w2, b2):
            pre = jnp.einsum('bsd,edf->ebsf', h, w1) + b1[:, None, None, :]
            act = jnp.stack([jnp.tanh(pre[0]), jax.nn.gelu(pre[1], approximate=False), jax.nn.silu(pre[2])])
            return jnp.einsum('ebsf,efd->ebsd', act, w2) + b2[:, None, None, :]
        b, s, d = h.shape
        vision_len = int(s * 0.3)
        text_strength = jnp.mean(jnp.abs(h[:, vision_len:, :]), axis=(1, 2), keepdims=True)
        vision_strength = jnp.mean(jnp.abs(h[:, :vision_len, :]), axis=(1, 2), keepdims=True)
        modality_ratio = text_strength / (vision_strength + 1e-08)
        modality_ratio = jnp.broadcast_to(modality_ratio, (b, s, 1))
        router_input = jnp.concatenate([h, modality_ratio], axis=-1)
        gate_logits = router_input @ gate_w + gate_b
        gate_scores = jax.nn.softmax(gate_logits, axis=-1)
        top_val, top_idx = jax.lax.top_k(gate_scores, TOP_K)
        top_val = top_val / (jnp.sum(top_val, axis=-1, keepdims=True) + 1e-08)
        expert_out = _expert_outputs(h, w1, b1, w2, b2)
        moe_out = jnp.zeros_like(h)
        batch_idx = jnp.arange(b)
        for i in range(TOP_K):
            j = top_idx[:, 0, i]
            out_i = expert_out[j, batch_idx]
            moe_out = moe_out + top_val[..., i:i + 1] * out_i
        return moe_out

    def _L1_attn_ref(x, Wq, Wk, Wv, Wo):
        import math
        import jax, jax.numpy as jnp
        import numpy as np
        B, T, E = (2, 256, 512)
        H, HKV = (32, 8)
        DH = E // H
        G = H // HKV
        ROPE_THETA = 500000.0
        ROPE_FACTOR = 32.0
        HI_FREQ_FACTOR = 4.0
        LO_FREQ_FACTOR = 1.0
        ORIG_CTX = 1024

        def _rope_cos_sin(t_len):
            inv_freq = 1.0 / ROPE_THETA ** (jnp.arange(0, DH, 2, dtype=jnp.float32) / DH)
            wavelen = 2.0 * math.pi / inv_freq
            cut_lo = ORIG_CTX / HI_FREQ_FACTOR
            cut_hi = ORIG_CTX / LO_FREQ_FACTOR
            inv_freq = jnp.where(wavelen > cut_hi, inv_freq / ROPE_FACTOR, inv_freq)
            smooth = (ORIG_CTX / wavelen - LO_FREQ_FACTOR) / (HI_FREQ_FACTOR - LO_FREQ_FACTOR)
            smoothed = (1.0 - smooth) * inv_freq / ROPE_FACTOR + smooth * inv_freq
            is_medium = ~(wavelen < cut_hi) & ~(wavelen > cut_lo)
            inv_freq = jnp.where(is_medium, smoothed, inv_freq)
            pos = jnp.arange(t_len, dtype=jnp.float32)
            freqs = pos[:, None] * inv_freq[None, :]
            emb = jnp.concatenate([freqs, freqs], axis=-1)
            return (jnp.cos(emb), jnp.sin(emb))

        def _rotate_half(x):
            x1, x2 = jnp.split(x, 2, axis=-1)
            return jnp.concatenate([-x2, x1], axis=-1)
        b, t, _ = x.shape
        q = (x @ Wq.T).reshape(b, t, H, DH).transpose(0, 2, 1, 3)
        k = (x @ Wk.T).reshape(b, t, HKV, DH).transpose(0, 2, 1, 3)
        v = (x @ Wv.T).reshape(b, t, HKV, DH).transpose(0, 2, 1, 3)
        cos, sin = _rope_cos_sin(t)
        cos = cos.astype(x.dtype)[None, None]
        sin = sin.astype(x.dtype)[None, None]
        q = q * cos + _rotate_half(q) * sin
        k = k * cos + _rotate_half(k) * sin
        qg = q.reshape(b, HKV, G, t, DH)
        scores = jnp.einsum('bhgtd,bhkd->bhgtk', qg.astype(jnp.float32), k.astype(jnp.float32)) / math.sqrt(DH)
        causal = jnp.tril(jnp.ones((t, t), dtype=bool))
        scores = jnp.where(causal[None, None, None], scores, jnp.finfo(jnp.float32).min)
        attn = jax.nn.softmax(scores, axis=-1).astype(x.dtype)
        ctx = jnp.einsum('bhgtk,bhkd->bhgtd', attn, v)
        out = ctx.reshape(b, H, t, DH).transpose(0, 2, 1, 3).reshape(b, t, E)
        return out @ Wo.T

    def _L1_ffn_ref(x, qweight_gu, qzeros_gu, scales_gu, g_idx_gu, qweight_down, qzeros_down, scales_down, g_idx_down):
        import jax, jax.numpy as jnp
        import numpy as np
        HIDDEN = 512
        INTER = 1376
        GROUP = 128
        B, S = (4, 256)
        NIB = jnp.uint32(15)

        def _pack_rows(nib):
            r = nib.reshape(-1, 8, nib.shape[-1])
            shifts = (jnp.arange(8, dtype=jnp.uint32) * 4)[None, :, None]
            return jnp.sum(r << shifts, axis=1, dtype=jnp.uint32)

        def _pack_cols(nib):
            r = nib.reshape(nib.shape[0], -1, 8)
            shifts = (jnp.arange(8, dtype=jnp.uint32) * 4)[None, None, :]
            return jnp.sum(r << shifts, axis=2, dtype=jnp.uint32)

        def _dequant(qw, qz, sc, g_idx):
            shifts = jnp.arange(8, dtype=jnp.uint32) * 4
            wq = qw[:, None, :] >> shifts[None, :, None] & NIB
            wq = wq.reshape(-1, qw.shape[1]).astype(jnp.float32)
            zq = qz[:, :, None] >> shifts[None, None, :] & NIB
            zq = zq.reshape(qz.shape[0], -1).astype(jnp.float32) + 1.0
            return sc[g_idx] * (wq - zq[g_idx])
        w_gu = _dequant(qweight_gu, qzeros_gu, scales_gu, g_idx_gu)
        inter = jnp.einsum('bsh,hf->bsf', x, w_gu)
        gate, up = (inter[..., :INTER], inter[..., INTER:])
        h = jax.nn.silu(gate) * up
        w_d = _dequant(qweight_down, qzeros_down, scales_down, g_idx_down)
        return jnp.einsum('bsf,fh->bsh', h, w_d)
    x = L0_attn_x
    xn = _layernorm(x, axis=-1)
    s = _L0_attn_ref(xn, L0_attn_Wq, L0_attn_bq, L0_attn_Wk, L0_attn_bk, L0_attn_Wv, L0_attn_bv)
    g = _silu(_L0_ffn_ref(xn, L0_ffn_gate_w, L0_ffn_gate_b, L0_ffn_w1, L0_ffn_b1, L0_ffn_w2, L0_ffn_b2))
    x = x + s * g
    xn = _layernorm(x, axis=-1)
    s = _L1_attn_ref(xn, L1_attn_Wq, L1_attn_Wk, L1_attn_Wv, L1_attn_Wo)
    g = _silu(_L1_ffn_ref(xn, L1_ffn_qweight_gu, L1_ffn_qzeros_gu, L1_ffn_scales_gu, L1_ffn_g_idx_gu, L1_ffn_qweight_down, L1_ffn_qzeros_down, L1_ffn_scales_down, L1_ffn_g_idx_down))
    x = x + s * g
    return x

_drawn_inputs = setup_inputs


def setup_inputs(seed=0):
    import zlib

    import numpy as np

    out = dict(_drawn_inputs(seed))
    spreads = {'L0_attn_bq': (0.0, 0.8),
     'L0_attn_bk': (0.0, 0.8),
     'L0_attn_bv': (0.0, 0.8),
     'L0_ffn_gate_b': (0.0, 0.8),
     'L0_ffn_b1': (0.0, 0.8),
     'L0_ffn_b2': (0.0, 0.8)}
    factors = {'L0_attn_Wq': 8.0,
     'L0_attn_Wk': 8.0,
     'L0_attn_Wv': 5.151,
     'L0_ffn_gate_w': 7.236,
     'L0_ffn_w1': 5.708,
     'L0_ffn_w2': 5.451,
     'L1_attn_Wq': 3.095,
     'L1_attn_Wk': 2.724,
     'L1_ffn_scales_gu': 3.42,
     'L1_ffn_scales_down': 4.891}
    for name, (base, spread) in spreads.items():
        noise = np.random.default_rng([zlib.crc32(name.encode()), seed]).standard_normal(out[name].shape)
        drawn = base * np.exp(spread * noise) if base else spread * noise
        out[name] = jnp.asarray(drawn.astype(out[name].dtype))
    for name, factor in factors.items():
        out[name] = (out[name] * factor).astype(out[name].dtype)
    return out
```

```python
from contextlib import ExitStack

import concourse.bass as bass
from concourse import mybir

F32 = mybir.dt.float32
F32R = mybir.dt.float32r
U32 = mybir.dt.uint32
I32 = mybir.dt.int32
ALU = mybir.AluOpType
ACT = mybir.ActivationFunctionType
AX = mybir.AxisListType

P = 128
B, T, E = 2, 1024, 512
TOKENS = B * T
TILES = TOKENS // P
CH = 512
CHUNKS = TOKENS // CH
TPC = CH // P
KT = E // P
D, H, HKV = 16, 32, 8
G = H // HKV
EXPERTS = 3
EPS = 1e-5
QKV = 3 * D * HKV + EXPERTS + 1
NB = D * HKV
VISION = int(T * 0.3)


def flat(ap):
    return ap.rearrange("p a b -> p (a b)")


def layer0(nc, x, Wq, bq, Wk, bk, Wv, bv, gate_w, gate_b, w1, b1, w2, b2, ident_d, strength_d, x1_d):
    with ExitStack() as ctx:
        def sb(name, shape, dt=F32):
            return ctx.enter_context(nc.sbuf_tensor(name, shape, dt))

        def sem(name):
            return ctx.enter_context(nc.semaphore(name))

        w1h, w1l = sb("w1h", [P, EXPERTS, KT, E], F32R), sb("w1l", [P, EXPERTS, KT, E], F32R)
        w2h, w2l = sb("w2h", [P, EXPERTS, KT, E], F32R), sb("w2l", [P, EXPERTS, KT, E], F32R)
        w3h, w3l = sb("w3h", [P, KT, QKV], F32R), sb("w3l", [P, KT, QKV], F32R)
        b2p = sb("b2p", [2, EXPERTS, E], F32R)
        ones_r = sb("ones_r", [2, P], F32R)
        b1_sb = sb("b1_sb", [P, EXPERTS, KT])
        ident = sb("ident", [P, P])
        mean_var = sb("mean_var", [P, TILES, 2])
        rstd, nmr = sb("rstd", [P, TILES]), sb("nmr", [P, TILES])
        bias_row = sb("bias_row", [P, B, QKV])
        select = sb("select", [P, B, 2, EXPERTS])

        with ExitStack() as c0:
            def sb0(name, shape, dt=F32):
                return c0.enter_context(nc.sbuf_tensor(name, shape, dt))

            xall = sb0("xall", [P, B, TILES // B, E])
            wst = sb0("wst", [P, 2, KT, E])
            qst = wst[:, 1]
            w3f = sb0("w3f", [P, KT, QKV])
            bst = sb0("bst", [P, E + 2 * NB])
            b2st = sb0("b2st", [1, EXPERTS, E])
            b2l = sb0("b2l", [1, EXPERTS, E], F32R)
            gws = sb0("gws", [P, (E + 1) * EXPERTS])
            gbs = sb0("gbs", [P, EXPERTS])
            x0 = sb0("x0", [P, B, E])
            stats = sb0("stats", [P, TILES, 6])
            stats0 = sb0("stats0", [P, B, 6])
            mv0 = sb0("mv0", [P, B, 2])
            rstd0, nmr0 = sb0("rstd0", [P, B]), sb0("nmr0", [P, B])
            neg_half = sb0("neg_half", [P, TILES])
            veps = sb0("veps", [P, TILES + B])
            abs_sum = sb0("abs_sum", [P, TILES])
            strength = sb0("strength", [P, 2, TILES])
            weighed = sb0("weighed", [P, 2, TILES])
            ones = sb0("ones", [P, P])
            means = sb0("means", [P, 2, B])
            ratio = sb0("ratio", [P, B])
            logits0 = sb0("logits0", [P, B, EXPERTS])
            prod0 = sb0("prod0", [P, E])
            ge = sb0("ge", [P, B, 3])
            rank = sb0("rank", [P, B, EXPERTS])
            ps = c0.enter_context(nc.psum_tensor("ps0", [P, 2, TILES], F32))

            def sem0(name):
                return c0.enter_context(nc.semaphore(name))

            x_in = [sem0(f"x_in{b}") for b in range(B)]
            w_in = [sem0(f"w_in{u}") for u in range(2)]
            small_in, qkv_in, x0_in = sem0("small_in"), sem0("qkv_in"), sem0("x0_in")
            stats_done, rstd_done, abs_done = sem0("stats_done"), sem0("rstd_done"), sem0("abs_done")
            stats0_done, rstd0_done, xn0_done = sem0("stats0_done"), sem0("rstd0_done"), sem0("xn0_done")
            weighed_done, strength_ready = sem0("weighed_done"), sem0("strength_ready")
            hi_done, lo_done, consts, q_summed, b2_split, b2_in = sem0("hi_done"), sem0("lo_done"), sem0("consts"), sem0("q_summed"), sem0("b2_split"), sem0("b2_in")
            block = c0.enter_context(nc.Block())
            BT = TILES // B

            @block.sync
            def _(sp):
                for b in range(B):
                    sp.dma_start(xall[:, b], x[b].rearrange("(t p) e -> p t e", p=P)).then_inc(x_in[b], 16)
                for n in range(2 * EXPERTS):
                    w, e = (w1, w2)[n % 2], n // 2
                    if n == 1:
                        sp.wait_ge(q_summed, 1)
                    if n >= 2:
                        sp.wait_ge(lo_done, n - 1)
                    sp.dma_start(wst[:, n % 2], w[e].rearrange("(k p) f -> p k f", p=P)).then_inc(w_in[n % 2], 16)

            @block.gpsimd
            def _(pool):
                pool.memset(ones[:, :], 1.0).then_inc(consts, 1)
                pool.memset(neg_half[:, :], -0.5)
                pool.memset(ones_r[:, :].bitcast(F32), 1.0)
                pool.memset(w3f[:, :, QKV - 1:QKV], 0.0).then_inc(consts, 1)
                pool.memset(bias_row[:, :, QKV - 1:QKV], 0.0)
                pool.dma_start(x0[:, :, :], x[:, 0:1, :].rearrange("b o e -> o b e").broadcast_to([P, B, E])).then_inc(x0_in, 16)
                pool.dma_start(gws[:, :], gate_w.rearrange("(o a) e -> o (a e)", o=1).broadcast_to([P, (E + 1) * EXPERTS])).then_inc(small_in, 16)
                pool.dma_start(gbs[:, :], gate_b.rearrange("(o e) -> o e", o=1).broadcast_to([P, EXPERTS])).then_inc(small_in, 16)
                for n, v in enumerate((bq, bk, bv)):
                    at = (0, E, E + NB, E + 2 * NB)
                    pool.dma_start(bst[:, at[n]:at[n + 1]],
                                   v.rearrange("(o d) h -> o (d h)", o=1).broadcast_to([P, at[n + 1] - at[n]])).then_inc(small_in, 16)
                pool.dma_start(strength[:, :, :], strength_d).then_inc(small_in, 16)
                pool.dma_start(b2st[:, :, :], b2.rearrange("(o e) f -> o e f", o=1)).then_inc(small_in, 16)
                pool.dma_start(b1_sb[:, :, :], b1.rearrange("e (k p) -> p e k", p=P), allow_slow_non_contiguous=True).then_inc(small_in, 16)
                pool.wait_ge(b2_split, 1)
                pool.dma_start(b2p[1:2], b2l[:, :, :]).then_inc(b2_in, 16)
                pool.drain()
                pool.wait_ge(stats0_done, 1)
                pool.tensor_scalar(veps[:, TILES:], mv0[:, :, 1], EPS, None, ALU.add)
                pool.drain()
                pool.tensor_tensor(rstd0[:, :], veps[:, TILES:], neg_half[:, 0:B], ALU.pow)
                pool.drain()
                pool.tensor_tensor(nmr0[:, :], mv0[:, :, 0], rstd0[:, :], ALU.mult)
                pool.drain()
                pool.tensor_scalar(nmr0[:, :], nmr0[:, :], -1.0, None, ALU.mult).then_inc(rstd0_done, 1)
                for b in range(B):
                    tiles = slice(b * BT, b * BT + BT)
                    pool.wait_ge(stats_done, b + 1)
                    pool.tensor_scalar(veps[:, tiles], mean_var[:, tiles, 1], EPS, None, ALU.add)
                    pool.drain()
                    pool.tensor_tensor(rstd[:, tiles], veps[:, tiles], neg_half[:, tiles], ALU.pow)
                    pool.drain()
                    pool.tensor_tensor(nmr[:, tiles], mean_var[:, tiles, 0], rstd[:, tiles], ALU.mult)
                    pool.drain()
                    pool.tensor_scalar(nmr[:, tiles], nmr[:, tiles], -1.0, None, ALU.mult).then_inc(rstd_done, 1)
                pool.wait_ge(b2_in, 16)

            @block.scalar
            def _(act):
                act.dma_start(ident[:, :], ident_d).then_inc(qkv_in, 16)
                act.dma_start(qst, Wq.rearrange("(k p) d h -> p k (d h)", p=P)).then_inc(qkv_in, 16)
                act.dma_start(w3f[:, :, NB:2 * NB], Wk.rearrange("(k p) d h -> p k (d h)", p=P)).then_inc(qkv_in, 16)
                act.dma_start(w3f[:, :, 2 * NB:3 * NB], Wv.rearrange("(k p) d h -> p k (d h)", p=P)).then_inc(qkv_in, 16)
                act.dma_start(w3f[:, :, 3 * NB:3 * NB + EXPERTS],
                              gate_w[0:E].rearrange("(k p) e -> p k e", p=P)).then_inc(qkv_in, 16)
                act.wait_ge(x0_in, 16)
                act.wait_ge(rstd0_done, 1)
                for b in range(B):
                    act.activation(x0[:, b], x0[:, b], ACT.Identity, bias=nmr0[:, b:b + 1],
                                   scale=rstd0[:, b:b + 1]).then_inc(xn0_done, 1)
                for n in range(2 * EXPERTS):
                    act.wait_ge(w_in[n % 2], 16 * (n // 2 + 1))
                    act.activation((w1h, w2h)[n % 2][:, n // 2], wst[:, n % 2], ACT.Copy).then_inc(hi_done, 1)
                    if n in (1, 3):
                        b = n // 2
                        act.wait_ge(rstd_done, b + 1)
                        with act.Fori(0, BT) as t:
                            tile = flat(xall[:, b, bass.ds(t, 1), :])
                            act.activation(tile, tile, ACT.Abs,
                                           bias=nmr[:, bass.ds(t + b * BT, 1)], scale=rstd[:, bass.ds(t + b * BT, 1)],
                                           accum_out=abs_sum[:, bass.ds(t + b * BT, 1)]).then_inc(abs_done, 1)

            @block.vector
            def _(dve):
                dve.wait_ge(x0_in, 16)
                for b in range(B):
                    dve.bn_stats(stats0[:, b], x0[:, b])
                dve.drain()
                for b in range(B):
                    dve.bn_aggr(mv0[:, b], stats0[:, b])
                dve.drain().then_inc(stats0_done, 1)
                for b in range(B):
                    dve.wait_ge(x_in[b], 16)
                    with dve.Fori(0, BT) as t:
                        dve.bn_stats(stats[:, bass.ds(t + b * BT, 1), :], flat(xall[:, b, bass.ds(t, 1), :]))
                    dve.drain()
                    for t in range(b * BT, b * BT + BT):
                        dve.bn_aggr(mean_var[:, t], stats[:, t])
                    dve.drain().then_inc(stats_done, 1)
                dve.wait_ge(consts, 2)
                dve.wait_ge(qkv_in, 80)
                dve.wait_ge(small_in, 128)
                dve.tensor_reduce(w3f[:, :, 0:NB], qst.rearrange("p k (d g) -> p k d g", g=G), AX.X, ALU.add).then_inc(q_summed, 1)
                for b in range(B):
                    dve.tensor_reduce(bias_row[:, b, 0:NB], bst[:, 0:E].rearrange("p (d g) -> p d g", g=G), AX.X, ALU.add)
                    dve.tensor_copy(bias_row[:, b, NB:3 * NB], bst[:, E:])
                dve.tensor_copy(b2p[0:1], b2st[:, :, :])
                dve.drain()
                dve.tensor_copy(w3h[:, :, :], w3f[:, :, :])
                dve.tensor_tensor(b2l[:, :, :], b2st[:, :, :], b2p[0:1].bitcast(F32), ALU.subtract).then_inc(b2_split, 1)
                dve.drain()
                dve.tensor_tensor(w3l[:, :, :], w3f[:, :, :], w3h[:, :, :].bitcast(F32), ALU.subtract)
                for n in range(2 * EXPERTS):
                    dve.wait_ge(hi_done, n + 1)
                    e = n // 2
                    dve.tensor_tensor((w1l, w2l)[n % 2][:, e], wst[:, n % 2], (w1h, w2h)[n % 2][:, e].bitcast(F32),
                                      ALU.subtract).then_inc(lo_done, 1)
                dve.wait_ge(xn0_done, B)
                gview = gws[:, 0:E * EXPERTS].rearrange("p (a e) -> p e a", e=EXPERTS)
                for b in range(B):
                    for e in range(EXPERTS):
                        dve.tensor_tensor(prod0[:, :], x0[:, b], gview[:, e], ALU.mult)
                        dve.drain()
                        dve.tensor_reduce(logits0[:, b, e:e + 1], prod0[:, :], AX.X, ALU.add)
                        dve.drain()
                dve.wait_ge(abs_done, TILES)
                for k in range(2):
                    dve.tensor_tensor(weighed[:, k], strength[:, k], abs_sum[:, :], ALU.mult)
                dve.drain().then_inc(weighed_done, 1)
                dve.wait_ge(strength_ready, 1)
                dve.tensor_reduce(means[:, :, :], ps[:, :, :].rearrange("p k (b t) -> p k b t", b=B), AX.X, ALU.add)
                dve.drain()
                dve.tensor_scalar(means[:, 1], means[:, 1], 1e-8, None, ALU.add)
                dve.drain()
                dve.reciprocal(ratio[:, :], means[:, 1])
                dve.drain()
                dve.tensor_tensor(ratio[:, :], ratio[:, :], means[:, 0], ALU.mult)
                dve.drain()
                for b in range(B):
                    dve.scalar_tensor_tensor(out=bias_row[:, b, 3 * NB:3 * NB + EXPERTS], in0=gws[:, E * EXPERTS:],
                                             scalar=ratio[:, b:b + 1], in1=gbs[:, :], op0=ALU.mult, op1=ALU.add)
                dve.drain()
                dve.tensor_tensor(logits0[:, :, :], logits0[:, :, :], bias_row[:, :, 3 * NB:3 * NB + EXPERTS], ALU.add)
                dve.drain()
                for n, (i, j) in enumerate(((0, 1), (0, 2), (1, 2))):
                    dve.tensor_tensor(ge[:, :, n:n + 1], logits0[:, :, i:i + 1], logits0[:, :, j:j + 1], ALU.is_ge)
                dve.drain()
                dve.tensor_tensor(rank[:, :, 0:1], ge[:, :, 0:1], ge[:, :, 1:2], ALU.add)
                dve.tensor_tensor(rank[:, :, 1:2], ge[:, :, 0:1], ge[:, :, 2:3], ALU.subtract)
                dve.tensor_tensor(rank[:, :, 2:3], ge[:, :, 1:2], ge[:, :, 2:3], ALU.add)
                dve.drain()
                dve.tensor_scalar(rank[:, :, 0:1], rank[:, :, 0:1], -1.0, 2.0, ALU.mult, ALU.add)
                dve.tensor_scalar(rank[:, :, 1:2], rank[:, :, 1:2], 1.0, None, ALU.add)
                dve.drain()
                for i in range(2):
                    dve.tensor_scalar(select[:, :, i], rank[:, :, :], float(i), None, ALU.is_equal)
                dve.drain()

            @block.tensor
            def _(pe):
                pe.wait_ge(consts, 1)
                pe.wait_ge(weighed_done, 1)
                pe.matmul(ps[:, :, :], ones[:, :], weighed[:, :, :], start=True, stop=True).then_inc(strength_ready, 1)

        xb = sb("xb", [P, 2, TPC, E])
        xn = sb("xn", [P, TPC, E])
        xth, xtl = sb("xth", [P, KT, CH], F32R), sb("xtl", [P, KT, CH], F32R)
        af = sb("af", [P, 2, CH])
        ah, al = sb("ah", [P, 2, CH], F32R), sb("al", [P, 2, CH], F32R)
        qkv = sb("qkv", [P, TPC, QKV])
        moe = sb("moe", [P, TPC, E])
        pa, pb = sb("pa", [P, D, D, HKV]), sb("pb", [P, D, HKV, D])
        sc, at = sb("sc", [P, D, D]), sb("at", [P, D, D])
        smax, rsum = sb("smax", [P, D]), sb("rsum", [P, D])
        so = sb("so", [P, D, HKV])
        s_sb = sb("s_sb", [P, TPC, D, HKV])
        gl, gexp = sb("gl", [P, TPC, EXPERTS]), sb("gexp", [P, TPC, EXPERTS])
        gt = sb("gt", [P, 6, TPC])
        coef, coef2 = sb("coef", [P, TPC, EXPERTS]), sb("coef2", [P, TPC, EXPERTS])
        bank = ctx.enter_context(nc.psum_tensor("bank", [P, 8, 512], F32))

        xin = [sem(f"xin{u}") for u in range(2)]
        xout = [sem(f"xout{u}") for u in range(2)]
        xn_ready, tp_ready, xth_ready, xtl_ready = sem("xn_ready"), sem("tp_ready"), sem("xth_ready"), sem("xtl_ready")
        qkv_ps, qkv_ready = sem("qkv_ps"), sem("qkv_ready")
        p1_done, redA, sc_ready, exp_done, p2_done, redB = (sem(n) for n in ("p1_done", "redA", "sc_ready", "exp_done", "p2_done", "redB"))
        gl_ready, gexp_ready = sem("gl_ready"), sem("gexp_ready")
        f1_ps, act_ready, split_ready, f2_step, f2_evac = (sem(n) for n in ("f1_ps", "act_ready", "split_ready", "f2_step", "f2_evac"))
        th_ready, th_used, x1_ready = sem("th_ready"), sem("th_used"), sem("x1_ready")
        NF = EXPERTS * KT
        x1v = x1_d.rearrange("(c t p) e -> p c t e", p=P, t=TPC)
        xv = x.rearrange("b (c t p) e -> p (b c) t e", p=P, t=TPC)

        def chunks(eng, body):
            with eng.Fori(0, CHUNKS // 2) as j:
                for u in range(2):
                    body(j * 2 + u, u, j)

        block = ctx.enter_context(nc.Block())

        @block.sync
        def _(sp):
            sp.sem_inc(x1_ready, 1)
            for u in range(2):
                sp.dma_start(xb[:, u], xv[:, u]).then_inc(xin[u], 16)

            def body(c, u, j):
                sp.wait_ge(x1_ready, c * TPC + 1 + TPC)
                sp.dma_start(x1v[:, bass.ds(c, 1)].rearrange("p c t e -> p (c t) e"), xb[:, u]).then_inc(xout[u], 16)
                sp.wait_ge(xout[u], j * 16 + 16)
            with sp.Fori(0, CHUNKS // 2 - 1) as j:
                for u in range(2):
                    body(j * 2 + u, u, j)
                    sp.dma_start(xb[:, u], xv[:, bass.ds(j * 2 + u + 2, 1)].rearrange("p c t e -> p (c t) e")).then_inc(xin[u], 16)
            for u in range(2):
                c = CHUNKS - 2 + u
                sp.wait_ge(x1_ready, c * TPC + 1 + TPC)
                sp.dma_start(x1v[:, c], xb[:, u]).then_inc(xout[u], 16)
                sp.wait_ge(xout[u], 16 * (CHUNKS // 2))

        @block.gpsimd
        def _(pool):
            def body(c, u, j):
                for t in range(TPC):
                    pool.wait_ge(qkv_ready, c * TPC + t + 1)
                    pool.wait_ge(redA, c * TPC + t + 1)
                    q = qkv[:, t, 0:NB].rearrange("p (d o h) -> p d o h", o=1, h=HKV).broadcast_to([P, D, D, HKV])
                    k = qkv[:, t, NB:2 * NB].rearrange("p (o e h) -> p o e h", o=1, h=HKV).broadcast_to([P, D, D, HKV])
                    pool.tensor_tensor(pa[:, :, :, :], q, k, ALU.mult).then_inc(p1_done, 1)
                    pool.wait_ge(exp_done, c * TPC + t + 1)
                    pool.wait_ge(redB, c * TPC + t + 1)
                    a = at[:, :, :].rearrange("p d (o e) -> p d o e", o=1).broadcast_to([P, D, HKV, D])
                    v = qkv[:, t, 2 * NB:3 * NB].rearrange("p (o e h) -> p o h e", o=1, h=HKV).broadcast_to([P, D, HKV, D])
                    pool.tensor_tensor(pb[:, :, :, :], a, v, ALU.mult).then_inc(p2_done, 1)
            chunks(pool, body)

        @block.scalar
        def _(act):
            act.sem_inc(p2_done, 1)

            def body(c, u, j):
                act.wait_ge(xin[u], j * 16 + 16)
                for t in range(TPC):
                    act.wait_ge(tp_ready, c * TPC + 1)
                    act.activation(xn[:, t], xb[:, u, t], ACT.Identity, bias=nmr[:, bass.ds(c * TPC + t, 1)],
                                   scale=rstd[:, bass.ds(c * TPC + t, 1)]).then_inc(xn_ready, 1)
                act.wait_ge(f1_ps, c * NF + 1)
                act.wait_ge(qkv_ps, c * TPC + 1)
                for t in range(TPC):
                    act.wait_ge(tp_ready, c * TPC + t + 2)
                    act.activation(xth[:, :, t * P:t * P + P], bank[:, t % 2].rearrange("p (k q) -> p k q", k=KT),
                                   ACT.Copy).then_inc(xth_ready, 1)
                act.wait_ge(gl_ready, c + 1)
                act.activation(gexp[:, :, :], gl[:, :, :], ACT.Exp).then_inc(gexp_ready, 1)
                for e in range(EXPERTS):
                    f = (ACT.Tanh, ACT.Gelu, ACT.Silu)[e]
                    for n in range(KT):
                        m = e * KT + n
                        act.wait_ge(f1_ps, c * NF + m + 2)
                        act.wait_ge(f2_step, c * NF + m)
                        if m < 2:
                            act.wait_ge(th_used, c * TPC + 2)
                        act.activation(af[:, m % 2], bank[:, 2 + m % 2], f, bias=b1_sb[:, e, n:n + 1])
                        act.activation(ah[:, m % 2], bank[:, 2 + m % 2], f, bias=b1_sb[:, e, n:n + 1]).then_inc(act_ready, 1)
                        if m % 3 == 0:
                            t = m // 3
                            act.wait_ge(sc_ready, c * TPC + t + 1)
                            act.wait_ge(p2_done, c * TPC + t + 1)
                            act.activation(at[:, :, :], sc[:, :, :], ACT.Exp, scale=D ** -0.5).then_inc(exp_done, 1)
                for t in range(TPC):
                    act.wait_ge(f2_evac, c * EXPERTS * TPC + 2 * TPC + t + 2)
                    act.wait_ge(th_used, c * TPC + t + 1)
                    act.activation(af[:, t % 2], moe[:, t], ACT.Tanh, scale=0.5).then_inc(th_ready, 1)
            chunks(act, body)

        @block.vector
        def _(dve):
            dve.sem_inc(redA, 1)
            dve.sem_inc(redB, 1)
            dve.sem_inc(f2_evac, 1)
            dve.sem_inc(th_used, 2)
            dve.sem_inc(split_ready, 1)

            def scores(c, t):
                dve.wait_ge(p1_done, c * TPC + t + 1)
                dve.tensor_reduce(sc[:, :, :], pa[:, :, :, :], AX.X, ALU.add).then_inc(redA, 1)
                dve.drain()
                dve.tensor_reduce(smax[:, :], sc[:, :, :], AX.X, ALU.max)
                dve.drain()
                dve.tensor_tensor(sc[:, :, :], sc[:, :, :], smax[:, :].rearrange("p (d o) -> p d o", o=1).broadcast_to([P, D, D]),
                                  ALU.subtract).then_inc(sc_ready, 1)

            def sums(c, t):
                dve.wait_ge(exp_done, c * TPC + t + 1)
                dve.tensor_reduce(rsum[:, :], at[:, :, :], AX.X, ALU.add)
                dve.drain()
                dve.reciprocal(rsum[:, :], rsum[:, :])

            def mix(c, t):
                dve.wait_ge(p2_done, c * TPC + t + 2)
                dve.tensor_reduce(so[:, :, :], pb[:, :, :, :], AX.X, ALU.add).then_inc(redB, 1)
                dve.drain()
                dve.scalar_tensor_tensor(out=s_sb[:, t], in0=so[:, :, :], scalar=0.5,
                                         in1=rsum[:, :].rearrange("p (d o) -> p d o", o=1).broadcast_to([P, D, HKV]),
                                         op0=ALU.mult, op1=ALU.mult)

            def body(c, u, j):
                dve.wait_ge(qkv_ps, c * TPC + 1)
                dve.wait_ge(f1_ps, c * NF + 1)
                for t in range(TPC):
                    dve.wait_ge(xth_ready, c * TPC + t + 1)
                    dve.tensor_tensor(xtl[:, :, t * P:t * P + P], bank[:, t % 2].rearrange("p (k q) -> p k q", k=KT),
                                      xth[:, :, t * P:t * P + P].bitcast(F32), ALU.subtract).then_inc(xtl_ready, 1)
                for t in range(TPC):
                    dve.wait_ge(qkv_ps, c * TPC + t + 2)
                    dve.tensor_tensor(qkv[:, t], bank[:, t % 2, 0:QKV], flat(bias_row[:, bass.ds(j, 1), :]),
                                      ALU.add).then_inc(qkv_ready, 1)
                dve.drain()
                lg = qkv[:, :, 3 * NB:3 * NB + EXPERTS]
                dve.tensor_reduce(gt[:, 0], lg, AX.X, ALU.max)
                dve.drain()
                dve.tensor_tensor(gl[:, :, :], lg, gt[:, 0].rearrange("p (t o) -> p t o", o=1).broadcast_to([P, TPC, EXPERTS]),
                                  ALU.subtract).then_inc(gl_ready, 1)
                dve.wait_ge(gexp_ready, c + 1)
                dve.tensor_reduce(gt[:, 0], gexp[:, :, :], AX.X, ALU.add)
                dve.tensor_tensor(gt[:, 1], gexp[:, :, 0], gexp[:, :, 1], ALU.max)
                dve.tensor_tensor(gt[:, 2], gexp[:, :, 0], gexp[:, :, 1], ALU.min)
                dve.drain()
                dve.tensor_tensor(gt[:, 3], gt[:, 1], gexp[:, :, 2], ALU.min)
                dve.tensor_tensor(gt[:, 4], gt[:, 1], gexp[:, :, 2], ALU.max)
                dve.drain()
                dve.tensor_tensor(gt[:, 5], gt[:, 3], gt[:, 2], ALU.max)
                dve.drain()
                dve.scalar_tensor_tensor(out=gt[:, 0], in0=gt[:, 0], scalar=1e-8, in1=gt[:, 4], op0=ALU.mult, op1=ALU.add)
                dve.drain()
                dve.tensor_tensor(gt[:, 0], gt[:, 0], gt[:, 5], ALU.add)
                dve.drain()
                dve.reciprocal(gt[:, 1], gt[:, 0])
                dve.drain()
                dve.tensor_tensor(gt[:, 4], gt[:, 4], gt[:, 1], ALU.mult)
                dve.tensor_tensor(gt[:, 5], gt[:, 5], gt[:, 1], ALU.mult)
                dve.drain()
                for i, dst in enumerate((coef, coef2)):
                    val = gt[:, 4 + i].rearrange("p (t o) -> p t o", o=1).broadcast_to([P, TPC, EXPERTS])
                    chosen = flat(select[:, bass.ds(j, 1), i, :]).rearrange("p (o e) -> p o e", o=1).broadcast_to([P, TPC, EXPERTS])
                    dve.tensor_tensor(dst[:, :, :], val, chosen, ALU.mult)
                dve.drain()
                dve.tensor_tensor(coef[:, :, :], coef[:, :, :], coef2[:, :, :], ALU.add)
                scores(c, 0)
                for m in range(NF):
                    e = m // KT
                    dve.wait_ge(act_ready, c * NF + m + 1)
                    dve.tensor_tensor(al[:, m % 2], af[:, m % 2], ah[:, m % 2].bitcast(F32), ALU.subtract).then_inc(split_ready, 1)
                    t = m // 3
                    if m % 3 == 0:
                        sums(c, t)
                    if m % 3 == 1:
                        mix(c, t)
                    if m % 3 == 2 and t < TPC - 1:
                        scores(c, t + 1)
                    if (m % KT == 1 and e > 0) or m == NF - 1:
                        ee = e - 1 if m < NF - 1 else e
                        for t in range(TPC):
                            dve.wait_ge(f2_step, c * NF + (ee + 1) * KT + 2)
                            if ee == 0:
                                dve.tensor_scalar(moe[:, t], bank[:, 4 + t], coef[:, t, 0:1], None, ALU.mult).then_inc(f2_evac, 1)
                            else:
                                dve.scalar_tensor_tensor(out=moe[:, t], in0=bank[:, 4 + t], scalar=coef[:, t, ee:ee + 1],
                                                         in1=moe[:, t], op0=ALU.mult, op1=ALU.add).then_inc(f2_evac, 1)
                for t in range(TPC):
                    dve.wait_ge(th_ready, c * TPC + t + 1)
                    dve.scalar_tensor_tensor(out=moe[:, t], in0=af[:, t % 2], scalar=1.0, in1=moe[:, t],
                                             op0=ALU.add, op1=ALU.mult).then_inc(th_used, 1)
                    dve.drain()
                    m4 = moe[:, t].rearrange("p (a g) -> p a g", g=G)
                    s4 = s_sb[:, t].rearrange("p d (h o) -> p (d h) o", o=1).broadcast_to([P, NB, G])
                    dve.tensor_tensor(m4, m4, s4, ALU.mult)
                    dve.drain()
                    dve.tensor_tensor(xb[:, u, t], xb[:, u, t], moe[:, t], ALU.add).then_inc(x1_ready, 1)
            chunks(dve, body)

        @block.tensor
        def _(pe):
            pe.sem_inc(tp_ready, 1)
            pe.sem_inc(qkv_ps, 1)
            pe.sem_inc(f1_ps, 1)
            pe.sem_inc(f2_step, 2)

            def three(out, wh, wl, mh, ml, first, last):
                pe.matmul(out, wh, ml, start=first, stop=False)
                pe.matmul(out, wl, mh, start=False, stop=False)
                return pe.matmul(out, wh, mh, start=False, stop=last)

            def second_product(c, m):
                e, n = m // KT, m % KT
                pe.wait_ge(split_ready, c * NF + m + 2)
                if n == 0:
                    pe.wait_ge(f2_evac, (c * EXPERTS + e) * TPC + 1)
                for t in range(TPC):
                    out = bank[:, 4 + t]
                    if n == 0:
                        pe.matmul(out, ones_r[:, :], b2p[:, e], start=True, stop=False)
                    mm = three(out, ah[:, m % 2, t * P:t * P + P], al[:, m % 2, t * P:t * P + P], w2h[:, e, n], w2l[:, e, n],
                               False, n == KT - 1)
                mm.then_inc(f2_step, 1)

            def body(c, u, j):
                pe.wait_ge(split_ready, c * NF + 1)
                for t in range(TPC):
                    pe.wait_ge(xn_ready, c * TPC + t + 1)
                    if t >= 2:
                        pe.wait_ge(xtl_ready, c * TPC + t - 1)
                    for k in range(KT):
                        mm = pe.transpose(bank[:, t % 2, k * P:k * P + P], xn[:, t, k * P:k * P + P], ident[:, :])
                    mm.then_inc(tp_ready, 1)
                pe.wait_ge(xtl_ready, c * TPC + TPC)
                for t in range(TPC):
                    if t >= 2:
                        pe.wait_ge(qkv_ready, c * TPC + t - 1)
                    for k in range(KT):
                        mm = three(bank[:, t % 2, 0:QKV], xth[:, k, t * P:t * P + P], xtl[:, k, t * P:t * P + P],
                                   w3h[:, k], w3l[:, k], k == 0, k == KT - 1)
                    mm.then_inc(qkv_ps, 1)
                for m in range(NF + 1):
                    if m < NF:
                        e, n = m // KT, m % KT
                        if m >= 2:
                            pe.wait_ge(act_ready, c * NF + m - 1)
                        for k in range(KT):
                            mm = three(bank[:, 2 + m % 2], w1h[:, e, k, n * P:n * P + P], w1l[:, e, k, n * P:n * P + P],
                                       xth[:, k], xtl[:, k], k == 0, k == KT - 1)
                        mm.then_inc(f1_ps, 1)
                    if m >= 1:
                        second_product(c, m - 1)
                pe.wait_ge(qkv_ready, c * TPC + TPC)
            chunks(pe, body)


INTER = 1376
SG, SD = 4, 10
FT = (INTER + P - 1) // P
FW = [min(P, INTER - n * P) for n in range(FT)]
STEPS = [list(range(n, min(n + 2, FT))) for n in range(0, FT, 2)]
QKT = 2 * NB + E
NG = B * HKV
NBITS, PACK = 4, 8


def three(pe, out, wh, wl, mh, ml, first, last):
    pe.matmul(out, wh, ml, start=first, stop=False)
    pe.matmul(out, wl, mh, start=False, stop=False)
    return pe.matmul(out, wh, mh, start=False, stop=last)


def chunk_pairs(eng, body):
    with eng.Fori(0, CHUNKS // 2) as b:
        for u in range(2):
            body(b * 2 + u, u, b)


def layer1_projections(nc, Wq, Wk, Wv, ident_d, rotate_d, cos_d, sin_d, x1_d, q_scr, k_scr, xth, xtl, v_all):
    with ExitStack() as ctx:
        def sb(name, shape, dt=F32):
            return ctx.enter_context(nc.sbuf_tensor("c_" + name, shape, dt))

        def sem(name):
            return ctx.enter_context(nc.semaphore("c_" + name))

        OT = QKT // P
        ROT = OT - 1
        ident, rotate = sb("ident", [P, P]), sb("rotate", [P, P])
        cos, sin = sb("cos", [P, T]), sb("sin", [P, T])
        wn = sb("wn", [P, OT, E])
        wth, wtl = sb("wth", [P, KT, QKT], F32R), sb("wtl", [P, KT, QKT], F32R)
        xb, xn = sb("xb", [P, 2, TPC, E]), sb("xn", [P, TPC, E])
        stats, mv = sb("stats", [P, TPC, 6]), sb("mv", [P, TPC, 2])
        neg_half, veps = sb("neg_half", [P, TPC]), sb("veps", [P, TPC])
        rstd, nmr = sb("rstd", [P, TPC]), sb("nmr", [P, TPC])
        qf, qc, qs = sb("qf", [P, 2, CH]), sb("qc", [P, 2, CH]), sb("qs", [P, 2, CH])
        qh, ql = sb("qh", [P, 2, CH], F32R), sb("ql", [P, 2, CH], F32R)
        bank = ctx.enter_context(nc.psum_tensor("c_bank", [P, 8, 512], F32))
        w_in, ident_in, table_in = sem("w_in"), sem("ident_in"), sem("table_in")
        xin = [sem(f"xin{u}") for u in range(2)]
        q_out = [sem(f"q_out{u}") for u in range(2)]
        w_tp, w_hi, w_lo = sem("w_tp"), sem("w_hi"), sem("w_lo")
        stats_done, stats_seen, rstd_done, xn_ready = sem("stats_done"), sem("stats_seen"), sem("rstd_done"), sem("xn_ready")
        tp_ready, xth_ready, xtl_ready = sem("tp_ready"), sem("xth_ready"), sem("xtl_ready")
        proj_ps, qf_ready, rot_ps, qc_ready, rope_ready = (sem(n) for n in ("proj_ps", "qf_ready", "rot_ps", "qc_ready", "rope_ready"))
        qh_ready, ql_ready, q_free, v_tp, v_ready = (sem(n) for n in ("qh_ready", "ql_ready", "q_free", "v_tp", "v_ready"))
        x1v = x1_d.rearrange("(c t p) e -> p c t e", p=P, t=TPC)

        def before(c, m, n):
            return c * n + 2 + max(0, m - 1)

        block = ctx.enter_context(nc.Block())

        @block.sync
        def _(sp):
            sp.sem_inc(q_free, 2)
            for u in range(2):
                sp.dma_start(xb[:, u], x1v[:, u]).then_inc(xin[u], 16)

            def store(c, u, b):
                for m in range(ROT):
                    sp.wait_ge(ql_ready, c * ROT + m + 1)
                    if m < ROT - 1:
                        dst = q_scr[:, bass.ds(b * (HKV * G * D) + m * P, P), u * CH:u * CH + CH]
                    else:
                        dst = k_scr[:, bass.ds(b * P, P), u * CH:u * CH + CH]
                    sp.dma_start(dst[0], qh[:, m % 2].bitcast(F32)).then_inc(q_out[m % 2], 16)
                    sp.dma_start(dst[1], ql[:, m % 2].bitcast(F32)).then_inc(q_out[m % 2], 16)
                    for k in ([m - 1] if m else []) + ([m] if m == ROT - 1 else []):
                        each = (ROT + 1 - k % 2) // 2
                        sp.wait_ge(q_out[k % 2], (c * each + k // 2 + 1) * 32)
                        sp.sem_inc(q_free, 1)

            with sp.Fori(0, CHUNKS // 2 - 1) as b:
                for u in range(2):
                    store(b * 2 + u, u, b)
                    sp.wait_ge(xn_ready, (b * 2 + u) * TPC + TPC)
                    sp.wait_ge(stats_done, b * 2 + u + 1)
                    sp.dma_start(xb[:, u], x1v[:, bass.ds(b * 2 + u + 2, 1)].rearrange("p c t e -> p (c t) e")).then_inc(xin[u], 16)
            for u in range(2):
                store(CHUNKS - 2 + u, u, CHUNKS // 2 - 1)

        @block.gpsimd
        def _(pool):
            pool.sem_inc(qc_ready, 2)
            pool.memset(v_all[:, :, :, D:], 0.0)
            pool.memset(neg_half[:, :], -0.5)
            pool.drain()
            pool.memset(v_all[:, :, :, D:D + 1], 1.0)
            pool.drain()

            def body(c, u, b):
                pool.wait_ge(stats_done, c + 1)
                pool.sem_inc(stats_seen, 1)
                pool.tensor_scalar(veps[:, :], mv[:, :, 1], EPS, None, ALU.add)
                pool.drain()
                pool.wait_ge(tp_ready, c * TPC + 1)
                pool.tensor_tensor(rstd[:, :], veps[:, :], neg_half[:, :], ALU.pow)
                pool.drain()
                pool.tensor_tensor(nmr[:, :], mv[:, :, 0], rstd[:, :], ALU.mult)
                pool.drain()
                pool.tensor_scalar(nmr[:, :], nmr[:, :], -1.0, None, ALU.mult).then_inc(rstd_done, 1)
                pool.wait_ge(table_in, 32)
                for m in range(ROT):
                    pool.wait_ge(qf_ready, c * OT + m + 3)
                    pool.wait_ge(rope_ready, before(c, m, ROT))
                    pool.tensor_tensor(qc[:, m % 2], qf[:, m % 2], cos[:, u * CH:u * CH + CH], ALU.mult).then_inc(qc_ready, 1)
            chunk_pairs(pool, body)

        @block.scalar
        def _(act):
            act.dma_start(wn[:, 0:KT], Wq.rearrange("(o p) e -> p o e", p=P)).then_inc(w_in, 16)
            act.dma_start(wn[:, KT], Wk).then_inc(w_in, 16)
            act.dma_start(wn[:, KT + 1], Wv).then_inc(w_in, 16)
            act.dma_start(ident[:, :], ident_d).then_inc(ident_in, 16)
            act.dma_start(rotate[:, :], rotate_d).then_inc(ident_in, 16)
            act.dma_start(cos[:, :], cos_d).then_inc(table_in, 16)
            act.dma_start(sin[:, :], sin_d).then_inc(table_in, 16)
            act.sem_inc(qf_ready, 2)
            for o in range(OT):
                act.wait_ge(w_tp, o + 1)
                act.activation(wth[:, :, o * P:o * P + P], bank[:, o % 2].rearrange("p (k q) -> p k q", k=KT),
                               ACT.Copy).then_inc(w_hi, 1)

            def body(c, u, b):
                act.wait_ge(xin[u], b * 16 + 16)
                act.wait_ge(rstd_done, c + 1)
                act.wait_ge(tp_ready, c * TPC + 1)
                for t in range(TPC):
                    act.activation(xn[:, t], xb[:, u, t], ACT.Identity, bias=nmr[:, t:t + 1],
                                   scale=rstd[:, t:t + 1]).then_inc(xn_ready, 1)
                for t in range(TPC):
                    act.wait_ge(tp_ready, c * TPC + t + 2)
                    act.activation(xth[:, :, bass.ds((c * TPC + t) * P, P)], bank[:, t % 2].rearrange("p (k q) -> p k q", k=KT),
                                   ACT.Copy).then_inc(xth_ready, 1)
                for m in range(OT + 1):
                    if m < OT:
                        act.wait_ge(proj_ps, c * OT + m + 1)
                        if m == 1:
                            act.wait_ge(v_tp, c + 1)
                        else:
                            act.wait_ge(qc_ready, c * ROT + 2 + max(0, m - 1))
                            act.wait_ge(rot_ps, c * ROT + 2 + max(0, m - 1))
                        act.activation(qf[:, m % 2], bank[:, 2 + m % 2], ACT.Copy).then_inc(qf_ready, 1)
                    if 1 <= m <= ROT:
                        k = m - 1
                        act.wait_ge(rope_ready, c * ROT + k + 3)
                        act.wait_ge(q_free, before(c, k, ROT))
                        act.activation(qh[:, k % 2], qs[:, k % 2], ACT.Copy).then_inc(qh_ready, 1)
            chunk_pairs(act, body)

        @block.vector
        def _(dve):
            dve.sem_inc(rope_ready, 2)
            dve.sem_inc(v_ready, 1)
            for o in range(OT):
                dve.wait_ge(w_hi, o + 1)
                dve.tensor_tensor(wtl[:, :, o * P:o * P + P], bank[:, o % 2].rearrange("p (k q) -> p k q", k=KT),
                                  wth[:, :, o * P:o * P + P].bitcast(F32), ALU.subtract).then_inc(w_lo, 1)

            def body(c, u, b):
                dve.wait_ge(xin[u], b * 16 + 16)
                dve.wait_ge(tp_ready, c * TPC + 1)
                for t in range(TPC):
                    dve.bn_stats(stats[:, t], xb[:, u, t])
                dve.drain()
                for t in range(TPC):
                    dve.bn_aggr(mv[:, t], stats[:, t])
                dve.drain().then_inc(stats_done, 1)
                for t in range(TPC):
                    dve.wait_ge(xth_ready, c * TPC + t + 1)
                    at = bass.ds((c * TPC + t) * P, P)
                    dve.tensor_tensor(xtl[:, :, at], bank[:, t % 2].rearrange("p (k q) -> p k q", k=KT),
                                      xth[:, :, at].bitcast(F32), ALU.subtract).then_inc(xtl_ready, 1)
                dve.wait_ge(table_in, 32)
                for m in range(ROT):
                    dve.wait_ge(rot_ps, c * ROT + m + 3)
                    dve.tensor_tensor(qs[:, m % 2], bank[:, 4 + m % 2], sin[:, u * CH:u * CH + CH], ALU.mult)
                    dve.drain()
                    dve.wait_ge(qc_ready, c * ROT + m + 3)
                    dve.tensor_tensor(qs[:, m % 2], qs[:, m % 2], qc[:, m % 2], ALU.add).then_inc(rope_ready, 1)
                    dve.wait_ge(qh_ready, c * ROT + m + 1)
                    dve.tensor_tensor(ql[:, m % 2], qs[:, m % 2], qh[:, m % 2].bitcast(F32), ALU.subtract).then_inc(ql_ready, 1)
                dve.wait_ge(v_tp, c + 2)
                for t in range(TPC):
                    last = dve.tensor_copy(v_all[:, bass.ds(b * HKV, HKV), u * TPC + t, 0:D],
                                           bank[:, 6, t * P:t * P + P].rearrange("p (g d) -> p g d", d=D))
                last.then_inc(v_ready, 1)
            chunk_pairs(dve, body)

        @block.tensor
        def _(pe):
            pe.sem_inc(tp_ready, 1)
            pe.sem_inc(rot_ps, 2)
            pe.sem_inc(v_tp, 1)
            pe.wait_ge(w_in, 48)
            pe.wait_ge(ident_in, 32)
            for o in range(OT):
                if o >= 2:
                    pe.wait_ge(w_lo, o - 1)
                for k in range(KT):
                    mm = pe.transpose(bank[:, o % 2, k * P:k * P + P], wn[:, o, k * P:k * P + P], ident[:, :])
                mm.then_inc(w_tp, 1)
            pe.wait_ge(w_lo, OT)

            def body(c, u, b):
                for t in range(TPC):
                    pe.wait_ge(xn_ready, c * TPC + t + 1)
                    if t >= 2:
                        pe.wait_ge(xtl_ready, c * TPC + t - 1)
                    for k in range(KT):
                        mm = pe.transpose(bank[:, t % 2, k * P:k * P + P], xn[:, t, k * P:k * P + P], ident[:, :])
                    mm.then_inc(tp_ready, 1)
                pe.wait_ge(xtl_ready, c * TPC + TPC)
                now = bass.ds(c * CH, CH)
                for m in range(OT + 1):
                    if m < OT:
                        pe.wait_ge(qf_ready, before(c, m, OT))
                        for k in range(KT):
                            mm = three(pe, bank[:, 2 + m % 2], wth[:, k, m * P:m * P + P], wtl[:, k, m * P:m * P + P],
                                       xth[:, k, now], xtl[:, k, now], k == 0, k == KT - 1)
                        mm.then_inc(proj_ps, 1)
                    if m >= 1:
                        k = m - 1
                        pe.wait_ge(qf_ready, c * OT + k + 3)
                        if k < ROT:
                            pe.wait_ge(rope_ready, before(c, k, ROT))
                            pe.matmul(bank[:, 4 + k % 2], rotate[:, :], qf[:, k % 2], start=True, stop=True).then_inc(rot_ps, 1)
                        else:
                            pe.wait_ge(v_ready, c + 1)
                            for t in range(TPC):
                                mm = pe.transpose(bank[:, 6, t * P:t * P + P], qf[:, k % 2, t * P:t * P + P], ident[:, :])
                            mm.then_inc(v_tp, 1)
            chunk_pairs(pe, body)


def layer1_ffn(nc, qw_gu, qz_gu, sc_gu, gi_gu, qw_d, qz_d, sc_d, gi_d, shift_d, lane_shift_d, row_d, s_gu_scr, z_gu_scr,
               xth, xtl, acc):
    with ExitStack() as ctx:
        def sb(name, shape, dt=F32):
            return ctx.enter_context(nc.sbuf_tensor("d_" + name, shape, dt))

        def sem(name):
            return ctx.enter_context(nc.semaphore("d_" + name))

        W = 2 * P
        hot_gu, hot_d = sb("hot_gu", [2 * SG, E], F32R), sb("hot_d", [2 * SD, INTER], F32R)
        sd, zd = sb("sd", [2 * SD, E], F32R), sb("zd", [SD, E], F32R)
        lane_shift = sb("lane_shift", [P, 1], U32)
        with ExitStack() as c0:
            def sb0(name, shape, dt=F32):
                return c0.enter_context(nc.sbuf_tensor("e_" + name, shape, dt))

            def sem0(name):
                return c0.enter_context(nc.semaphore("e_" + name))

            F2 = 2 * INTER
            s_in, s_out, small = sem0("s_in"), sem0("s_out"), sem0("small")
            split, back = sem0("split"), sem0("back")
            sg = sb0("sg", [SG, F2])
            sgh, sgl = sb0("sgh", [SG, F2], F32R), sb0("sgl", [SG, F2], F32R)
            zg, zu = sb0("zg", [SG, F2 // PACK], U32), sb0("zu", [SG, F2 // PACK, PACK], U32)
            zdp, zdu = sb0("zdp", [SD, E // PACK], U32), sb0("zdu", [SD, E // PACK, PACK], U32)
            sdn, sdl = sb0("sdn", [SD, E]), sb0("sdl", [SD, E], F32R)
            shift = sb0("shift", [P, PACK], U32)
            row = sb0("row", [2 * SD, 2])
            idx = sb0("idx", [2 * SD, E + INTER], I32)
            idf = sb0("idf", [2 * SD, E + INTER])
            neg = sb0("neg", [2 * SD, E + INTER])
            block = c0.enter_context(nc.Block())

            @block.sync
            def _(sp):
                sp.dma_start(sg[:, :], sc_gu).then_inc(s_in, 16)
                sp.dma_start(zg[:, :], qz_gu).then_inc(s_in, 16)
                sp.dma_start(sdn[:, :], sc_d).then_inc(s_in, 16)
                sp.dma_start(zdp[:, :], qz_d).then_inc(s_in, 16)
                sp.dma_start(shift[:, :], shift_d).then_inc(s_in, 16)
                sp.dma_start(row[:, :], row_d).then_inc(s_in, 16)
                sp.dma_start(lane_shift[:, :], lane_shift_d).then_inc(s_in, 16)
                sp.dma_start(idx[:, 0:E], gi_gu.rearrange("(o k) -> o k", o=1).broadcast_to([2 * SD, E])).then_inc(s_in, 16)
                sp.dma_start(idx[:, E:], gi_d.rearrange("(o k) -> o k", o=1).broadcast_to([2 * SD, INTER])).then_inc(s_in, 16)
                sp.wait_ge(split, 1)
                sp.dma_start(s_gu_scr[0:SG], sgh[:, :].bitcast(F32)).then_inc(s_out, 16)
                sp.dma_start(s_gu_scr[SG:], sgl[:, :].bitcast(F32)).then_inc(s_out, 16)
                sp.dma_start(z_gu_scr, sg[:, :]).then_inc(s_out, 16)
                sp.dma_start(sd[SD:].bitcast(F32), sdl[:, :].bitcast(F32)).then_inc(s_out, 16)
                sp.wait_ge(s_out, 64)

            @block.vector
            def _(dve):
                dve.wait_ge(s_in, 144)
                dve.tensor_copy(sgh[:, :], sg[:, :])
                dve.tensor_copy(sd[0:SD], sdn[:, :])
                dve.drain()
                dve.tensor_tensor(sgl[:, :], sg[:, :], sgh[:, :].bitcast(F32), ALU.subtract)
                dve.tensor_tensor(sdl[:, :], sdn[:, :], sd[0:SD].bitcast(F32), ALU.subtract)
                for packed, out, n in ((zg, zu, SG), (zdp, zdu, SD)):
                    c = packed.shape[1]
                    dve.tensor_tensor(out[:, :, :], packed[:, :].rearrange("p (c o) -> p c o", o=1).broadcast_to([n, c, PACK]),
                                      shift[0:n, :].rearrange("p (o i) -> p o i", o=1).broadcast_to([n, c, PACK]),
                                      ALU.logical_shift_right)
                dve.drain()
                for out in (zu, zdu):
                    dve.tensor_scalar(out[:, :, :], out[:, :, :], 15, None, ALU.bitwise_and)
                dve.drain()
                dve.tensor_scalar(sg[:, :], zu[:, :, :].rearrange("p c i -> p (c i)"), 1.0, None, ALU.add)
                dve.tensor_scalar(zd[:, :], zdu[:, :, :].rearrange("p c i -> p (c i)"), 1.0, None, ALU.add)
                dve.tensor_copy(idf[:, :], idx[:, :])
                dve.drain()
                for at, n in ((slice(0, E), SG), (slice(E, E + INTER), SD)):
                    dve.tensor_scalar(neg[:, at], idf[:, at], 0.0, float(n), ALU.is_lt, ALU.mult)
                dve.drain()
                dve.tensor_tensor(idf[:, :], idf[:, :], neg[:, :], ALU.add)
                dve.drain()
                for at, n in ((slice(0, E), SG), (slice(E, E + INTER), SD)):
                    dve.tensor_scalar(idf[:, at], idf[:, at], 0.0, float(n - 1), ALU.max, ALU.min)
                dve.drain()
                dve.tensor_scalar(hot_gu[:, :], idf[0:2 * SG, 0:E], row[0:2 * SG, 0:1], None, ALU.is_equal)
                dve.tensor_scalar(hot_d[:, :], idf[:, E:], row[:, 1:2], None, ALU.is_equal)
                dve.drain().then_inc(split, 1)

        sz, zz = sb("sz", [2 * SG, 2, 2, W], F32R), sb("zz", [SG, 2, 2, W], F32R)
        hot = sb("hot", [2 * SD, 2, P], F32R)
        qw = sb("qw", [P, 2, 2 * W], U32)
        wq = sb("wq", [P, 2 * W], U32)
        wf = sb("wf", [P, 2 * W])
        wgh, wgl = sb("wgh", [P, 2, KT, 2, W], F32R), sb("wgl", [P, 2, KT, 2, W], F32R)
        wdh, wdl = sb("wdh", [P, 2, 2, E], F32R), sb("wdl", [P, 2, 2, E], F32R)
        hs = sb("hs", [P, 2, CH])
        hh, hl = sb("hh", [P, 2, CH], F32R), sb("hl", [P, 2, CH], F32R)
        bank = ctx.enter_context(nc.psum_tensor("d_bank", [P, 8, 512], F32))
        sz_in, qw_in2 = sem("sz_in"), sem("qw_in2")
        qw_in = [sem(f"qw_in{u}") for u in range(2)]
        hot_ready, row_ps, unpacked, w_ready = sem("hot_ready"), sem("row_ps"), sem("unpacked"), sem("w_ready")
        f1_ps, silu_ready, h_ready, hh_ready, hl_ready = (sem(n) for n in ("f1_ps", "silu_ready", "h_ready", "hh_ready", "hl_ready"))
        f2_ps, acc_ready, gate_ready = sem("f2_ps"), sem("acc_ready"), sem("gate_ready")
        tanh_ready = sem("tanh_ready")

        def piece_number(s, b, n):
            return b * 3 + (6 * s + n)

        def pieces(s, b, u):
            return [(u, "gu")] + ([(2, "down")] if u == 1 else [])

        def tiles_before(s):
            return CHUNKS * sum(len(STEPS[k]) for k in range(s))

        qgv = qw_gu.rearrange("r (h f) -> r h f", h=2)
        block = ctx.enter_context(nc.Block())

        def each_chunk(eng, body):
            with eng.Fori(0, 2) as b:
                for u in range(2):
                    body(-1, None, u, b)
            for s in range(len(STEPS)):
                with eng.Fori(0, 2) as b:
                    for u in range(2):
                        body(s, b * 2 + u, u, b)

        @block.sync
        def _(sp):
            def body(s, c, u, b):
                if s + 1 == len(STEPS):
                    return
                tiles = STEPS[s + 1]
                f0, w = tiles[0] * P, sum(FW[n] for n in tiles)
                for n, kind in pieces(s + 1, b, u):
                    number = piece_number(s + 1, b, n)
                    sp.wait_ge(unpacked, number + (1 if n == 0 else 0))
                    dst = qw[:, (n if kind == "gu" else 0)]
                    if kind == "gu":
                        src = qgv[bass.ds((b * 2 + u) * (P // PACK), P // PACK), :, f0:f0 + w]
                        for h in range(2):
                            sp.dma_start(dst[:, h * W:h * W + w],
                                         src[:, h].rearrange("r (o f) -> r o f", o=1).broadcast_to([P // PACK, PACK, w])).then_inc(qw_in[n], 16)
                    else:
                        rows = FW[tiles[0]] // PACK
                        at = b * (P // PACK) + f0 // PACK if len(tiles) > 1 else f0 // PACK
                        src = qw_d[bass.ds(at, rows), :] if len(tiles) > 1 else qw_d[at:at + rows, :]
                        sp.dma_start(dst[0:rows * PACK, :],
                                     src.rearrange("r (o f) -> r o f", o=1).broadcast_to([rows, PACK, E])).then_inc(qw_in2, 16)

            def scales(s):
                if s > 0:
                    sp.wait_ge(w_ready, 6 * s + 1)
                tiles = STEPS[s]
                f0, w = tiles[0] * P, sum(FW[n] for n in tiles)
                for scr, dst in ((s_gu_scr, sz), (z_gu_scr, zz)):
                    sp.dma_start(dst[:, s % 2, :, 0:w].bitcast(F32), scr.rearrange("r (h f) -> r h f", h=2)[:, :, f0:f0 + w]).then_inc(sz_in, 16)

            sp.sem_inc(unpacked, 1)
            scales(0)
            with sp.Fori(0, 2) as b:
                for u in range(2):
                    body(-1, None, u, b)
            for s in range(len(STEPS)):
                if s + 1 < len(STEPS):
                    scales(s + 1)
                with sp.Fori(0, 2) as b:
                    for u in range(2):
                        body(s, b * 2 + u, u, b)

        @block.vector
        def _(dve):
            dve.sem_inc(h_ready, 1)
            dve.sem_inc(hl_ready, 1)
            dve.sem_inc(w_ready, 1)
            dve.sem_inc(acc_ready, 1)

            def piece(s, b, u, n, kind):
                tiles = STEPS[s]
                w = sum(FW[k] for k in tiles)
                number = piece_number(s, b, n)
                rows = P if kind == "gu" else FW[tiles[0]]
                if kind == "gu":
                    dve.tensor_copy(hot[0:2 * SG, n % 2], hot_gu[:, bass.ds((b * 2 + u) * P, P)]).then_inc(hot_ready, 1)
                    dve.wait_ge(qw_in[n], (b + (2 * s + 1)) * 32)
                    v3 = lambda a: a.rearrange("p (h f) -> p h f", h=2)[0:rows, :, 0:w]
                    src, into = qw[:, n], (wgh[:, s % 2, bass.ds(b * 2 + u, 1)], wgl[:, s % 2, bass.ds(b * 2 + u, 1)])
                    into = [a.rearrange("p k h f -> p (k h) f")[:, :, 0:w] for a in into]
                else:
                    at = bass.ds(b * P + tiles[0] * P, P) if len(tiles) > 1 else slice(tiles[0] * P, tiles[0] * P + rows)
                    dve.tensor_copy(hot[:, n % 2, 0:rows], hot_d[:, at]).then_inc(hot_ready, 1)
                    dve.wait_ge(qw_in2, (b + (2 * s + 1)) * 16)
                    v3 = lambda a: a[0:rows]
                    k = bass.ds(b, 1) if len(tiles) > 1 else slice(0, 1)
                    src, into = qw[:, 0], [flat(a[:, s % 2, k])[0:rows] for a in (wdh, wdl)]
                first = 2 * (n // 2)
                dve.tensor_scalar(v3(wq[:, :]), v3(src), lane_shift[0:rows, 0:1], 15, ALU.logical_shift_right,
                                  ALU.bitwise_and).then_inc(unpacked, 1)
                dve.drain()
                dve.wait_ge(row_ps, number + 1)
                dve.tensor_tensor(v3(wf[:, :]), v3(wq[:, :]), v3(bank[:, first + 1]), ALU.subtract)
                dve.drain()
                dve.tensor_tensor(v3(wf[:, :]), v3(wf[:, :]), v3(bank[:, first]), ALU.mult)
                dve.drain()
                dve.tensor_copy(into[0], v3(wf[:, :]))
                dve.drain()
                dve.tensor_tensor(into[1], v3(wf[:, :]), into[0].bitcast(F32), ALU.subtract).then_inc(w_ready, 1)

            def body(s, c, u, b):
                if s == -1:
                    dve.wait_ge(sz_in, 32)
                else:
                    tiles = STEPS[s]
                    for n in range(len(tiles)):
                        rows = FW[tiles[n]]
                        number = c * len(tiles) + tiles_before(s) + n
                        dve.wait_ge(silu_ready, number + 1)
                        dve.tensor_tensor(hs[0:rows, n], hs[0:rows, n], bank[0:rows, 2 * n + 1], ALU.mult).then_inc(h_ready, 1)
                        dve.wait_ge(hh_ready, number + 1)
                        dve.tensor_tensor(hl[0:rows, n], hs[0:rows, n], hh[0:rows, n].bitcast(F32), ALU.subtract).then_inc(hl_ready, 1)
                if s + 1 < len(STEPS):
                    for n, kind in pieces(s + 1, b, u):
                        piece(s + 1, b, u, n, kind)
                if s >= 0:
                    for t in range(TPC):
                        dve.wait_ge(f2_ps, c * TPC + (s * TILES + t + 2))
                        a = flat(acc[:, bass.ds(c * TPC + t, 1), :])
                        if s == 0:
                            dve.tensor_copy(a, bank[:, 4 + t]).then_inc(acc_ready, 1)
                        else:
                            dve.tensor_tensor(a, a, bank[:, 4 + t], ALU.add).then_inc(acc_ready, 1)
            each_chunk(dve, body)
            with dve.Fori(0, TILES // 2) as k:
                for n in range(2):
                    dve.wait_ge(tanh_ready, k * 2 + n + 1)
                    a = flat(acc[:, bass.ds(k * 2 + n, 1), :])
                    dve.scalar_tensor_tensor(out=a, in0=hs[:, n], scalar=1.0, in1=a, op0=ALU.add, op1=ALU.mult).then_inc(gate_ready, 1)

        @block.scalar
        def _(act):
            def body(s, c, u, b):
                if s == -1:
                    return
                tiles = STEPS[s]
                for n in range(len(tiles)):
                    rows = FW[tiles[n]]
                    number = c * len(tiles) + tiles_before(s) + n
                    act.wait_ge(f1_ps, number + 1)
                    act.wait_ge(hl_ready, c * len(tiles) + tiles_before(s) + 1)
                    act.activation(hs[0:rows, n], bank[0:rows, 2 * n], ACT.Silu).then_inc(silu_ready, 1)
                    act.wait_ge(h_ready, number + 2)
                    act.wait_ge(f2_ps, c * TPC + (s * TILES + 1))
                    act.activation(hh[0:rows, n], hs[0:rows, n], ACT.Copy).then_inc(hh_ready, 1)
            each_chunk(act, body)
            act.wait_ge(hl_ready, CHUNKS * FT + 1)
            with act.Fori(0, TILES // 2) as k:
                for n in range(2):
                    act.wait_ge(acc_ready, k * 2 + (len(STEPS) - 1) * TILES + n + 2)
                    act.wait_ge(gate_ready, k * 2 + n + 1)
                    act.activation(hs[:, n], flat(acc[:, bass.ds(k * 2 + n, 1), :]), ACT.Tanh, scale=0.5).then_inc(tanh_ready, 1)

        @block.tensor
        def _(pe):
            pe.sem_inc(f2_ps, 1)
            pe.sem_inc(gate_ready, 2)

            def piece(s, b, u, n, kind):
                tiles = STEPS[s]
                w = sum(FW[k] for k in tiles)
                number = piece_number(s, b, n)
                first = 2 * (n // 2)
                pe.wait_ge(hot_ready, number + 1)
                pe.wait_ge(w_ready, number + 1)
                if kind == "gu":
                    out = [bank[:, first + k].rearrange("p (h f) -> p h f", h=2)[:, :, 0:w] for k in range(2)]
                    pe.matmul(out[0], hot[0:2 * SG, n % 2], sz[:, s % 2, :, 0:w], start=True, stop=True)
                    pe.matmul(out[1], hot[0:SG, n % 2], zz[:, s % 2, :, 0:w], start=True, stop=True).then_inc(row_ps, 1)
                else:
                    rows = FW[tiles[0]]
                    pe.matmul(bank[0:rows, first], hot[:, n % 2, 0:rows], sd[:, :], start=True, stop=True)
                    pe.matmul(bank[0:rows, first + 1], hot[0:SD, n % 2, 0:rows], zd[:, :], start=True, stop=True).then_inc(row_ps, 1)

            def body(s, c, u, b):
                if s == -1:
                    pe.wait_ge(sz_in, 32)
                    for n, kind in pieces(0, b, u):
                        piece(0, b, u, n, kind)
                    return
                tiles = STEPS[s]
                now = bass.ds(c * CH, CH)
                making = pieces(s + 1, b, u) if s + 1 < len(STEPS) else []
                if making:
                    pe.wait_ge(sz_in, 32 * (s + 2))
                for n in range(len(tiles)):
                    rows, f0 = FW[tiles[n]], n * P
                    pe.wait_ge(h_ready, c * len(tiles) + tiles_before(s) + 1)
                    pe.wait_ge(w_ready, piece_number(s + 1, b, u) + 1 if making else 6 * len(STEPS) + 1)
                    for h in range(2):
                        for k in range(KT):
                            mm = three(pe, bank[0:rows, 2 * n + h], wgh[:, s % 2, k, h, f0:f0 + rows], wgl[:, s % 2, k, h, f0:f0 + rows],
                                       xth[:, k, now], xtl[:, k, now], k == 0, k == KT - 1)
                    mm.then_inc(f1_ps, 1)
                for n, kind in making[0:1]:
                    pe.wait_ge(h_ready, c * len(tiles) + tiles_before(s) + 2)
                    piece(s + 1, b, u, n, kind)
                pe.wait_ge(acc_ready, c * TPC + s * TILES + 1)
                for n in range(len(tiles)):
                    rows = FW[tiles[n]]
                    pe.wait_ge(hl_ready, c * len(tiles) + tiles_before(s) + n + 2)
                    for t in range(TPC):
                        mm = three(pe, bank[:, 4 + t], hh[0:rows, n, t * P:t * P + P], hl[0:rows, n, t * P:t * P + P],
                                   wdh[0:rows, s % 2, n], wdl[0:rows, s % 2, n], n == 0, n == len(tiles) - 1)
                        if n == len(tiles) - 1:
                            mm.then_inc(f2_ps, 1)
                for n, kind in making[1:]:
                    pe.wait_ge(h_ready, c * len(tiles) + tiles_before(s) + len(tiles) + 1)
                    piece(s + 1, b, u, n, kind)
            each_chunk(pe, body)


HG = G
QB = T // P
HALF = T // CH
PART = 3 * D
M_ROW = 2 * PART
UNITS = [(h, k) for h in range(HALF) for k in range((h + 1) * CH // P)]
ITEMS = [(h, q) for h in range(HG) for q in range(QB)]
ITEMS_FROM, ITEMS_BY, MTURN_AT = 2, 4, 10
LOADED = 2 * 3 * 2 * 16
LEAST = -3.0e38


def layer1_attention(nc, ident_d, mask_d, minus_d, q_scr, k_scr, v_all, ctx_sb):
    with ExitStack() as ctx:
        def sb(name, shape, dt=F32):
            return ctx.enter_context(nc.sbuf_tensor("f_" + name, shape, dt))

        def sem(name):
            return ctx.enter_context(nc.semaphore("f_" + name))

        ident, mask = sb("ident", [P, P]), sb("mask", [P, T])
        minus = sb("minus", [P, 2, T])
        qst = sb("qst", [P, 2, 2, T], F32R)
        kst = sb("kst", [P, 2, 2, T], F32R)
        vst = sb("vst", [P, 2, QB, 2 * D])
        prob = sb("prob", [P, 2, HG, CH])
        mx = sb("mx", [P, 2, HG * QB])
        mt = sb("mt", [HG * QB, 2, P], F32R)
        ctxt = sb("ctxt", [P, HALF, CH])
        rden = sb("rden", [P, QB, HG])
        bank = ctx.enter_context(nc.psum_tensor("f_bank", [P, 8, 512], F32))
        const_in, consts = sem("const_in"), sem("consts")
        item_seen, diag_seen = sem("item_seen"), sem("diag_seen")
        qk_in = [sem(f"qk_in{u}") for u in range(2)]
        m_in = [sem(f"m_in{u}") for u in range(2)]
        item_ps, item_done, mturn_ps, mt_ready = sem("item_ps"), sem("item_done"), sem("mturn_ps"), sem("mt_ready")
        st_ps, exp_done, masked, av_done, vst_ready = (sem(n) for n in ("st_ps", "exp_done", "masked", "av_done", "vst_ready"))
        ctxt_ready, cturn_ps, out_ready = sem("ctxt_ready"), sem("cturn_ps"), sem("out_ready")
        NU, NS, NI = len(UNITS), len(UNITS) * HG, len(ITEMS)
        DIAG = sum(k * P >= h * CH for h, k in UNITS)
        pairs = [bank[:, 0:2].rearrange("p a b -> p (a b)"), bank[:, 2:4].rearrange("p a b -> p (a b)")]

        def groups(eng, body):
            with eng.Fori(0, NG // 2 - 1) as j:
                for u in range(2):
                    body(j * 2 + u, u, j, True)
            body(NG - 2, 0, NG // 2 - 1, True)
            body(NG - 1, 1, NG // 2 - 1, False)

        def span(h, k):
            return max(0, k * P - h * CH)

        def beside(i):
            return range(max(0, i - ITEMS_FROM) * ITEMS_BY, min(NI, max(0, i + 1 - ITEMS_FROM) * ITEMS_BY))

        block = ctx.enter_context(nc.Block())

        @block.sync
        def _(sp):
            def load(n, u):
                for par in range(2):
                    for part, (qp, kp) in enumerate(((0, 0), (1, 0), (0, 1))):
                        r = par * PART + part * D
                        src = q_scr[qp, bass.ds(n * (HG * D), HG * D), :].rearrange("(i p d) t -> p d i t", p=2, d=D)[par]
                        sp.dma_start(qst[r:r + D, u].bitcast(F32), src).then_inc(qk_in[u], 16)
                        sp.dma_start(kst[r:r + D, u, par].bitcast(F32), k_scr[kp, bass.ds(n * D, D), :]).then_inc(qk_in[u], 16)

            def maxima(n, u):
                sp.wait_ge(mt_ready, n + 1)
                for hh in range(HG):
                    sp.dma_start(qst[M_ROW + hh % 2:M_ROW + hh % 2 + 1, u, hh // 2].rearrange("o (b q) -> o b q", q=P).bitcast(F32),
                                 mt[hh * QB:hh * QB + QB, u].bitcast(F32)).then_inc(m_in[u], 16)

            sp.wait_ge(consts, 1)
            for u in range(2):
                load(u, u)
            maxima(0, 0)
            with sp.Fori(0, NG // 2 - 1) as j:
                for u in range(2):
                    n = j * 2 + u
                    maxima(n + 1, 1 - u)
                    sp.wait_ge(st_ps, n * NS + NS)
                    load(n + 2, u)
            maxima(NG - 1, 1)

        @block.gpsimd
        def _(pool):
            def values(n, u):
                pool.tensor_copy(vst[:, u].rearrange("p b d -> p (b d)"),
                                 v_all[:, bass.ds(n, 1)].rearrange("p n b d -> p (n b d)")).then_inc(vst_ready, 1)

            def body(n, u, j, more):
                for i, (h, k) in enumerate(UNITS):
                    if k * P >= h * CH:
                        pool.wait_ge(exp_done, n * NS + ((i + 1) * HG + 1))
                        pool.sem_inc(diag_seen, 1)
                        p = prob[:, i % 2, :, span(h, k):span(h, k) + P]
                        pool.affine_select(out=p, in_=p, compare_op=ALU.is_ge, fill=0.0, base=0,
                                           pattern=[[0, HG], [1, P]], channel_multiplier=-1).then_inc(masked, 1)
                    if i == 2 and more:
                        pool.wait_ge(av_done, n * NU + 1)
                        values(n + 1, 1 - u)
            values(0, 0)
            groups(pool, body)

        @block.scalar
        def _(act):
            act.dma_start(ident[:, :], ident_d).then_inc(const_in, 16)
            act.dma_start(mask[:, :], mask_d).then_inc(const_in, 16)
            act.dma_start(minus[M_ROW:M_ROW + 2], minus_d).then_inc(const_in, 16)
            act.sem_inc(exp_done, 1)
            act.sem_inc(ctxt_ready, 1)

            def turn(n, h):
                act.wait_ge(av_done, n * NU + (CH // P if h == 0 else NU) + 1)
                act.wait_ge(cturn_ps, n + 1)
                act.activation(ctxt[:, h], bank[:, 6 + h], ACT.Copy).then_inc(ctxt_ready, 1)

            def body(n, u, j, more):
                for i, (h, k) in enumerate(UNITS):
                    lo = span(h, k)
                    act.wait_ge(av_done, n * NU + max(0, i - 1) + 1)
                    for hh in range(HG):
                        c = i * HG + hh
                        act.wait_ge(st_ps, n * NS + c + 1)
                        act.activation(prob[:, i % 2, hh, lo:], bank[:, 4 + c % 2, lo:], ACT.Exp, scale=D ** -0.5).then_inc(exp_done, 1)
                    if i == CH // P + 1:
                        turn(n, 0)
                turn(n, 1)
            groups(act, body)

        @block.vector
        def _(dve):
            dve.memset(qst[:, :, :, :].bitcast(U32), 0)
            dve.memset(kst[:, :, :, :].bitcast(U32), 0)
            dve.wait_ge(const_in, 48)
            dve.drain()
            for u in range(2):
                last = dve.tensor_copy(kst[M_ROW:M_ROW + 2, u], minus[M_ROW:M_ROW + 2])
            last.then_inc(consts, 1)
            dve.sem_inc(out_ready, 1)

            def items(n, u, numbers):
                for s in numbers:
                    hh, qb = ITEMS[s]
                    w = (qb + 1) * P
                    dve.wait_ge(item_ps, n * NI + s + 1)
                    dve.sem_inc(item_seen, 1)
                    sc = pairs[s % 2][:, 0:w]
                    dve.tensor_tensor_reduce(sc, sc, mask[:, T - w:T], 1.0, LEAST, ALU.add, ALU.max,
                                             mx[:, u, hh * QB + qb:hh * QB + qb + 1]).then_inc(item_done, 1)

            def maxima(n, u):
                dve.wait_ge(mturn_ps, n + 1)
                dve.tensor_copy(mt[:, u], bank[0:HG * QB, 0, 0:P]).then_inc(mt_ready, 1)

            def body(n, u, j, more):
                for i in range(NU):
                    if more:
                        items(n + 1, 1 - u, beside(i))
                        if i == MTURN_AT:
                            maxima(n + 1, 1 - u)
                dve.wait_ge(cturn_ps, n + 2)
                turned = pairs[1].rearrange("p (b h d) -> p b h d", h=HG, d=2 * D)
                dve.reciprocal(rden[:, :, :], turned[:, :, :, D])
                dve.drain()
                dve.tensor_tensor(ctx_sb[:, bass.ds(n, 1)].rearrange("p n b (h d) -> p (n b) h d", d=D), turned[:, :, :, 0:D],
                                  rden[:, :, :].rearrange("p b (h o) -> p b h o", o=1).broadcast_to([P, QB, HG, D]),
                                  ALU.mult).then_inc(out_ready, 1)
            items(0, 0, range(NI))
            maxima(0, 0)
            groups(dve, body)

        @block.tensor
        def _(pe):
            pe.sem_inc(av_done, 1)
            pe.sem_inc(cturn_ps, 1)

            def items(n, u, numbers, first):
                for s in numbers:
                    hh, qb = ITEMS[s]
                    w = (qb + 1) * P
                    if s >= 2:
                        pe.wait_ge(item_done, n * NI + s - 1)
                    elif not first:
                        pe.wait_ge(mt_ready, n) if s == 0 else pe.wait_ge(out_ready, n)
                    for at in range(0, w, CH):
                        mm = pe.matmul(pairs[s % 2][:, at:min(w, at + CH)], qst[0:M_ROW, u, hh // 2, qb * P:qb * P + P],
                                       kst[0:M_ROW, u, hh % 2, at:min(w, at + CH)], start=True, stop=True)
                    mm.then_inc(item_ps, 1)

            def maxima(n, u):
                pe.wait_ge(item_done, n * NI + NI)
                pe.transpose(bank[0:HG * QB, 0, 0:P], mx[:, u], ident[:, :]).then_inc(mturn_ps, 1)

            def weighed(n, u, i):
                h, k = UNITS[i]
                pe.wait_ge(exp_done, n * NS + ((i + 1) * HG + 1))
                if k * P >= h * CH:
                    pe.wait_ge(masked, n * DIAG + sum(kk * P >= hf * CH for hf, kk in UNITS[:i + 1]))
                if k == 0:
                    pe.wait_ge(ctxt_ready, n * HALF + 1)
                lo = span(h, k)
                for hh in range(HG):
                    mm = pe.matmul(bank[2 * D * hh:2 * D * (hh + 1), 6 + h, lo:], vst[:, u, k], prob[:, i % 2, hh, lo:],
                                   start=(k == 0), stop=(k == (h + 1) * CH // P - 1))
                mm.then_inc(av_done, 1)

            def body(n, u, j, more):
                pe.wait_ge(m_in[u], j * (16 * HG) + 16 * HG)
                pe.wait_ge(vst_ready, n + 1)
                for i, (h, k) in enumerate(UNITS):
                    lo = span(h, k)
                    for hh in range(HG):
                        c = i * HG + hh
                        pe.wait_ge(exp_done, n * NS + max(1, c))
                        pe.matmul(bank[:, 4 + c % 2, lo:], kst[0:M_ROW + 2, u, hh % 2, k * P:k * P + P],
                                  qst[0:M_ROW + 2, u, hh // 2, h * CH + lo:(h + 1) * CH], start=True, stop=True).then_inc(st_ps, 1)
                    if i > 0:
                        weighed(n, u, i - 1)
                    if more:
                        if i == ITEMS_FROM:
                            pe.wait_ge(qk_in[1 - u], (j + u) * LOADED + LOADED)
                        items(n + 1, 1 - u, beside(i), False)
                        if i == MTURN_AT:
                            maxima(n + 1, 1 - u)
                weighed(n, u, NU - 1)
                pe.wait_ge(ctxt_ready, n * HALF + HALF + 1)
                pe.wait_ge(out_ready, n + 1)
                for b in range(QB):
                    mm = pe.transpose(pairs[1][:, b * P:b * P + P], ctxt[:, b // (CH // P), (b % (CH // P)) * P:(b % (CH // P)) * P + P],
                                      ident[:, :])
                mm.then_inc(cturn_ps, 1)
            pe.wait_ge(const_in, 48)
            pe.wait_ge(qk_in[0], LOADED)
            items(0, 0, range(NI), True)
            maxima(0, 0)
            groups(pe, body)


def layer1_output(nc, Wo, ident_d, x1_d, ctx_sb, acc, out):
    with ExitStack() as ctx:
        def sb(name, shape, dt=F32):
            return ctx.enter_context(nc.sbuf_tensor("g_" + name, shape, dt))

        def sem(name):
            return ctx.enter_context(nc.semaphore("g_" + name))

        ident = sb("ident", [P, P])
        wn = sb("wn", [P, KT, E])
        woh, wol = sb("woh", [P, KT, E], F32R), sb("wol", [P, KT, E], F32R)
        x1 = sb("x1", [P, TILES, E])
        ct = sb("ct", [P, 2, E])
        cth, ctl = sb("cth", [P, 2, KT, P], F32R), sb("ctl", [P, 2, KT, P], F32R)
        bank = ctx.enter_context(nc.psum_tensor("g_bank", [P, 8, 512], F32))
        w_in, x_in = sem("w_in"), sem("x_in")
        w_tp, w_hi, w_lo = sem("w_tp"), sem("w_hi"), sem("w_lo")
        ct_ready, ct_tp, cth_ready, ctl_ready, proj_ps, out_ready = (
            sem(n) for n in ("ct_ready", "ct_tp", "cth_ready", "ctl_ready", "proj_ps", "out_ready"))
        read_ps = sem("read_ps")
        y_out = [sem(f"y_out{u}") for u in range(2)]
        k4 = lambda a: a.rearrange("p (k q) -> p k q", k=KT)
        outv = out.rearrange("b (t p) e -> p (b t) e", p=P)

        def tiles(eng, body):
            with eng.Fori(0, TILES // 2) as j:
                for u in range(2):
                    body(j * 2 + u, u, j)

        block = ctx.enter_context(nc.Block())

        @block.sync
        def _(sp):
            sp.dma_start(wn[:, :, :], Wo.rearrange("(o p) e -> p o e", p=P)).then_inc(w_in, 16)
            sp.dma_start(ident[:, :], ident_d).then_inc(w_in, 16)
            sp.dma_start(x1[:, :, :], x1_d.rearrange("(t p) e -> p t e", p=P)).then_inc(x_in, 16)

            def body(t, u, j):
                sp.wait_ge(out_ready, t + 1)
                sp.dma_start(outv[:, bass.ds(t, 1)].rearrange("p t e -> p (t e)"),
                             x1[:, bass.ds(t, 1)].rearrange("p t e -> p (t e)")).then_inc(y_out[u], 16)
            tiles(sp, body)
            for u in range(2):
                sp.wait_ge(y_out[u], 16 * (TILES // 2))

        @block.gpsimd
        def _(pool):
            pool.sem_inc(ct_tp, 2)
            with pool.Fori(0, B) as b:
                for qb in range(QB):
                    pool.wait_ge(ct_tp, b * QB + qb + 1)
                    pool.tensor_copy(ct[:, qb % 2].rearrange("p (g d) -> p g d", g=HKV),
                                     ctx_sb[:, bass.ds(b * HKV, HKV), qb]).then_inc(ct_ready, 1)

        @block.scalar
        def _(act):
            for o in range(KT):
                act.wait_ge(w_tp, o + 1)
                act.activation(woh[:, :, o * P:o * P + P], k4(bank[:, o % 2]), ACT.Copy).then_inc(w_hi, 1)

            def body(t, u, j):
                act.wait_ge(ct_tp, t + 3)
                act.wait_ge(proj_ps, t + 1)
                act.activation(cth[:, u], k4(bank[:, u]), ACT.Copy).then_inc(cth_ready, 1)
            tiles(act, body)

        @block.vector
        def _(dve):
            for o in range(KT):
                dve.wait_ge(w_hi, o + 1)
                dve.tensor_tensor(wol[:, :, o * P:o * P + P], k4(bank[:, o % 2]), woh[:, :, o * P:o * P + P].bitcast(F32),
                                  ALU.subtract).then_inc(w_lo, 1)
            dve.sem_inc(ctl_ready, 2)
            dve.wait_ge(x_in, 16)

            def body(t, u, j):
                dve.wait_ge(cth_ready, t + 1)
                dve.tensor_tensor(ctl[:, u], k4(bank[:, u]), cth[:, u].bitcast(F32), ALU.subtract).then_inc(ctl_ready, 1)
                dve.wait_ge(proj_ps, t + 3)
                a = flat(acc[:, bass.ds(t, 1)])
                x = flat(x1[:, bass.ds(t, 1)])
                dve.scalar_tensor_tensor(out=a, in0=bank[:, 2 + u], scalar=0.5, in1=a, op0=ALU.mult, op1=ALU.mult).then_inc(read_ps, 1)
                dve.drain()
                dve.tensor_tensor(x, x, a, ALU.add).then_inc(out_ready, 1)
            dve.sem_inc(read_ps, 2)
            tiles(dve, body)

        @block.tensor
        def _(pe):
            pe.sem_inc(proj_ps, 2)
            pe.wait_ge(w_in, 32)
            for o in range(KT):
                if o >= 2:
                    pe.wait_ge(w_lo, o - 1)
                for k in range(KT):
                    mm = pe.transpose(bank[:, o % 2, k * P:k * P + P], wn[:, o, k * P:k * P + P], ident[:, :])
                mm.then_inc(w_tp, 1)
            pe.wait_ge(w_lo, KT)

            def body(t, u, j):
                pe.wait_ge(ct_ready, t + 1)
                pe.wait_ge(ctl_ready, t + 1)
                for k in range(KT):
                    mm = pe.transpose(bank[:, u, k * P:k * P + P], ct[:, u, k * P:k * P + P], ident[:, :])
                mm.then_inc(ct_tp, 1)
                pe.wait_ge(ctl_ready, t + 3)
                pe.wait_ge(read_ps, t + 1)
                for k in range(KT):
                    mm = three(pe, bank[:, 2 + u], cth[:, u, k], ctl[:, u, k], woh[:, k], wol[:, k], k == 0, k == KT - 1)
                mm.then_inc(proj_ps, 1)
            tiles(pe, body)


def program(nc, i, out, x1=None):
    x1_d = nc.dram_tensor("x1_d", [TOKENS, E], F32).ap() if x1 is None else x1
    if x1 is None:
        layer0(nc, i["L0_attn_x"], i["L0_attn_Wq"], i["L0_attn_bq"], i["L0_attn_Wk"], i["L0_attn_bk"], i["L0_attn_Wv"],
               i["L0_attn_bv"], i["L0_ffn_gate_w"], i["L0_ffn_gate_b"], i["L0_ffn_w1"], i["L0_ffn_b1"], i["L0_ffn_w2"],
               i["L0_ffn_b2"], i["ident_d"], i["strength_d"], x1_d)
    q_scr = nc.dram_tensor("q_scr", [2, B * E, T], F32).ap()
    k_scr = nc.dram_tensor("k_scr", [2, B * NB, T], F32).ap()
    s_gu_scr = nc.dram_tensor("s_gu_scr", [2 * SG, 2 * INTER], F32).ap()
    z_gu_scr = nc.dram_tensor("z_gu_scr", [SG, 2 * INTER], F32).ap()
    with nc.sbuf_tensor("acc", [P, TILES, E], F32) as acc, nc.sbuf_tensor("v_all", [P, NG, T // P, 2 * D], F32) as v_all:
        with nc.sbuf_tensor("xth1", [P, KT, TOKENS], F32R) as xth, nc.sbuf_tensor("xtl1", [P, KT, TOKENS], F32R) as xtl:
            layer1_projections(nc, i["L1_attn_Wq"], i["L1_attn_Wk"], i["L1_attn_Wv"], i["ident_d"], i["rotate_d"], i["cos_d"],
                               i["sin_d"], x1_d, q_scr, k_scr, xth, xtl, v_all)
            layer1_ffn(nc, i["L1_ffn_qweight_gu"], i["L1_ffn_qzeros_gu"], i["L1_ffn_scales_gu"], i["L1_ffn_g_idx_gu"],
                       i["L1_ffn_qweight_down"], i["L1_ffn_qzeros_down"], i["L1_ffn_scales_down"], i["L1_ffn_g_idx_down"],
                       i["shift_d"], i["lane_shift_d"], i["row_d"], s_gu_scr, z_gu_scr, xth, xtl, acc)
        with nc.sbuf_tensor("ctx_sb", [P, NG, T // P, HG * D], F32) as ctx_sb:
            layer1_attention(nc, i["ident_d"], i["mask_d"], i["minus_d"], q_scr, k_scr, v_all, ctx_sb)
            layer1_output(nc, i["L1_attn_Wo"], i["ident_d"], x1_d, ctx_sb, acc, out)


def shape_constants():
    import numpy as np

    f = np.float32
    heads_per_tile = P // D
    c = {"ident_d": np.eye(P, dtype=f)}
    position = (np.arange(P)[:, None] + P * (np.arange(TILES) % (T // P))[None, :])
    text = position >= VISION
    c["strength_d"] = np.stack([text / f((T - VISION) * E), ~text / f(VISION * E)], 1).astype(f)
    inv = (f(1.0) / (f(500000.0) ** (np.arange(0, D, 2, dtype=f) / f(D)))).astype(f)
    wavelen = (f(2 * np.pi) / inv).astype(f)
    low = np.where(wavelen > f(1024.0), inv / f(32.0), inv).astype(f)
    smooth = ((f(1024) / wavelen - f(1.0)) / f(3.0)).astype(f)
    smoothed = ((f(1) - smooth) * low / f(32) + smooth * low).astype(f)
    medium = ~(wavelen < f(1024.0)) & ~(wavelen > f(256.0))
    freqs = (np.arange(T, dtype=f)[:, None] * np.where(medium, smoothed, low).astype(f)[None]).astype(f)
    emb = np.concatenate([freqs, freqs], -1)
    c["cos_d"] = np.tile(np.cos(emb).astype(f).T, (heads_per_tile, 1))
    c["sin_d"] = np.tile(np.sin(emb).astype(f).T, (heads_per_tile, 1))
    rotate = np.zeros((P, P), f)
    for m in range(P):
        first = m % D < D // 2
        rotate[m + D // 2 if first else m - D // 2, m] = -1 if first else 1
    c["rotate_d"] = rotate
    c["shift_d"] = np.tile((np.arange(PACK) * NBITS).astype(np.uint32), (P, 1))
    c["lane_shift_d"] = (np.arange(P) % PACK * NBITS).astype(np.uint32)[:, None]
    c["row_d"] = np.stack([np.arange(2 * SD) % SG, np.arange(2 * SD) % SD], 1).astype(f)
    mask = np.zeros((P, T), f)
    mask[:, T - P:] = np.triu(np.full((P, P), -1e30, f), 1)
    c["mask_d"] = mask
    minus = np.zeros((2, 2, T), f)
    minus[0, 0], minus[1, 1] = -1, -1
    c["minus_d"] = minus
    return c


def kernel(**inputs):
    import numpy as np
    import concourse.bacc as bacc
    from concourse.bass_utils import run_bass_kernel_spmd

    nc = bacc.Bacc("TRN2", target_bir_lowering=False, num_devices=1)
    arrays = {name: np.ascontiguousarray(a) for name, a in {**inputs, **shape_constants()}.items()}
    handles = {name: nc.dram_tensor(name, a.shape, mybir.dt.from_np(a.dtype), kind="ExternalInput").ap() for name, a in arrays.items()}
    out = nc.dram_tensor("out", (B, T, E), F32, kind="ExternalOutput").ap()
    program(nc, handles, out)
    r = run_bass_kernel_spmd(nc, [arrays], core_ids=[0])
    return r.results[0]["out"]
```

```python
from contextlib import ExitStack

import concourse.bass as bass
from concourse import mybir

F32 = mybir.dt.float32
F32R = mybir.dt.float32r
U32 = mybir.dt.uint32
I32 = mybir.dt.int32
ALU = mybir.AluOpType
ACT = mybir.ActivationFunctionType
AX = mybir.AxisListType

P = 128
B, T, E = 2, 1024, 512
TOKENS = B * T
TILES = TOKENS // P
CH = 512
CHUNKS = TOKENS // CH
TPC = CH // P
KT = E // P
D, H, HKV = 16, 32, 8
G = H // HKV
EXPERTS = 3
EPS = 1e-5
QKV = 3 * D * HKV + EXPERTS + 1
NB = D * HKV
VISION = int(T * 0.3)


def flat(ap):
    return ap.rearrange("p a b -> p (a b)")


def layer0(nc, x, Wq, bq, Wk, bk, Wv, bv, gate_w, gate_b, w1, b1, w2, b2, ident_d, strength_d, x1_d):
    with ExitStack() as ctx:
        def sb(name, shape, dt=F32):
            return ctx.enter_context(nc.sbuf_tensor(name, shape, dt))

        def sem(name):
            return ctx.enter_context(nc.semaphore(name))

        w1h, w1l = sb("w1h", [P, EXPERTS, KT, E], F32R), sb("w1l", [P, EXPERTS, KT, E], F32R)
        w2h, w2l = sb("w2h", [P, EXPERTS, KT, E], F32R), sb("w2l", [P, EXPERTS, KT, E], F32R)
        w3h, w3l = sb("w3h", [P, KT, QKV], F32R), sb("w3l", [P, KT, QKV], F32R)
        b2p = sb("b2p", [2, EXPERTS, E], F32R)
        ones_r = sb("ones_r", [2, P], F32R)
        b1_sb = sb("b1_sb", [P, EXPERTS, KT])
        ident = sb("ident", [P, P])
        mean_var = sb("mean_var", [P, TILES, 2])
        rstd, nmr = sb("rstd", [P, TILES]), sb("nmr", [P, TILES])
        bias_row = sb("bias_row", [P, B, QKV])
        select = sb("select", [P, B, 2, EXPERTS])

        with ExitStack() as c0:
            def sb0(name, shape, dt=F32):
                return c0.enter_context(nc.sbuf_tensor(name, shape, dt))

            xall = sb0("xall", [P, B, TILES // B, E])
            wst = sb0("wst", [P, 2, KT, E])
            qst = wst[:, 1]
            w3f = sb0("w3f", [P, KT, QKV])
            bst = sb0("bst", [P, E + 2 * NB])
            b2st = sb0("b2st", [1, EXPERTS, E])
            b2l = sb0("b2l", [1, EXPERTS, E], F32R)
            gws = sb0("gws", [P, (E + 1) * EXPERTS])
            gbs = sb0("gbs", [P, EXPERTS])
            x0 = sb0("x0", [P, B, E])
            stats = sb0("stats", [P, TILES, 6])
            stats0 = sb0("stats0", [P, B, 6])
            mv0 = sb0("mv0", [P, B, 2])
            rstd0, nmr0 = sb0("rstd0", [P, B]), sb0("nmr0", [P, B])
            neg_half = sb0("neg_half", [P, TILES])
            veps = sb0("veps", [P, TILES + B])
            abs_sum = sb0("abs_sum", [P, TILES])
            strength = sb0("strength", [P, 2, TILES])
            weighed = sb0("weighed", [P, 2, TILES])
            ones = sb0("ones", [P, P])
            means = sb0("means", [P, 2, B])
            ratio = sb0("ratio", [P, B])
            logits0 = sb0("logits0", [P, B, EXPERTS])
            prod0 = sb0("prod0", [P, E])
            ge = sb0("ge", [P, B, 3])
            rank = sb0("rank", [P, B, EXPERTS])
            ps = c0.enter_context(nc.psum_tensor("ps0", [P, 2, TILES], F32))

            def sem0(name):
                return c0.enter_context(nc.semaphore(name))

            x_in = [sem0(f"x_in{b}") for b in range(B)]
            w_in = [sem0(f"w_in{u}") for u in range(2)]
            small_in, qkv_in, x0_in = sem0("small_in"), sem0("qkv_in"), sem0("x0_in")
            stats_done, rstd_done, abs_done = sem0("stats_done"), sem0("rstd_done"), sem0("abs_done")
            stats0_done, rstd0_done, xn0_done = sem0("stats0_done"), sem0("rstd0_done"), sem0("xn0_done")
            weighed_done, strength_ready = sem0("weighed_done"), sem0("strength_ready")
            hi_done, lo_done, consts, q_summed, b2_split, b2_in = sem0("hi_done"), sem0("lo_done"), sem0("consts"), sem0("q_summed"), sem0("b2_split"), sem0("b2_in")
            block = c0.enter_context(nc.Block())
            BT = TILES // B

            @block.sync
            def _(sp):
                for b in range(B):
                    sp.dma_start(xall[:, b], x[b].rearrange("(t p) e -> p t e", p=P)).then_inc(x_in[b], 16)
                for n in range(2 * EXPERTS):
                    w, e = (w1, w2)[n % 2], n // 2
                    if n == 1:
                        sp.wait_ge(q_summed, 1)
                    if n >= 2:
                        sp.wait_ge(lo_done, n - 1)
                    sp.dma_start(wst[:, n % 2], w[e].rearrange("(k p) f -> p k f", p=P)).then_inc(w_in[n % 2], 16)

            @block.gpsimd
            def _(pool):
                pool.memset(ones[:, :], 1.0).then_inc(consts, 1)
                pool.memset(neg_half[:, :], -0.5)
                pool.memset(ones_r[:, :].bitcast(F32), 1.0)
                pool.memset(w3f[:, :, QKV - 1:QKV], 0.0).then_inc(consts, 1)
                pool.memset(bias_row[:, :, QKV - 1:QKV], 0.0)
                pool.dma_start(x0[:, :, :], x[:, 0:1, :].rearrange("b o e -> o b e").broadcast_to([P, B, E])).then_inc(x0_in, 16)
                pool.dma_start(gws[:, :], gate_w.rearrange("(o a) e -> o (a e)", o=1).broadcast_to([P, (E + 1) * EXPERTS])).then_inc(small_in, 16)
                pool.dma_start(gbs[:, :], gate_b.rearrange("(o e) -> o e", o=1).broadcast_to([P, EXPERTS])).then_inc(small_in, 16)
                for n, v in enumerate((bq, bk, bv)):
                    at = (0, E, E + NB, E + 2 * NB)
                    pool.dma_start(bst[:, at[n]:at[n + 1]],
                                   v.rearrange("(o d) h -> o (d h)", o=1).broadcast_to([P, at[n + 1] - at[n]])).then_inc(small_in, 16)
                pool.dma_start(strength[:, :, :], strength_d).then_inc(small_in, 16)
                pool.dma_start(b2st[:, :, :], b2.rearrange("(o e) f -> o e f", o=1)).then_inc(small_in, 16)
                pool.dma_start(b1_sb[:, :, :], b1.rearrange("e (k p) -> p e k", p=P), allow_slow_non_contiguous=True).then_inc(small_in, 16)
                pool.wait_ge(b2_split, 1)
                pool.dma_start(b2p[1:2], b2l[:, :, :]).then_inc(b2_in, 16)
                pool.drain()
                pool.wait_ge(stats0_done, 1)
                pool.tensor_scalar(veps[:, TILES:], mv0[:, :, 1], EPS, None, ALU.add)
                pool.drain()
                pool.tensor_tensor(rstd0[:, :], veps[:, TILES:], neg_half[:, 0:B], ALU.pow)
                pool.drain()
                pool.tensor_tensor(nmr0[:, :], mv0[:, :, 0], rstd0[:, :], ALU.mult)
                pool.drain()
                pool.tensor_scalar(nmr0[:, :], nmr0[:, :], -1.0, None, ALU.mult).then_inc(rstd0_done, 1)
                for b in range(B):
                    tiles = slice(b * BT, b * BT + BT)
                    pool.wait_ge(stats_done, b + 1)
                    pool.tensor_scalar(veps[:, tiles], mean_var[:, tiles, 1], EPS, None, ALU.add)
                    pool.drain()
                    pool.tensor_tensor(rstd[:, tiles], veps[:, tiles], neg_half[:, tiles], ALU.pow)
                    pool.drain()
                    pool.tensor_tensor(nmr[:, tiles], mean_var[:, tiles, 0], rstd[:, tiles], ALU.mult)
                    pool.drain()
                    pool.tensor_scalar(nmr[:, tiles], nmr[:, tiles], -1.0, None, ALU.mult).then_inc(rstd_done, 1)
                pool.wait_ge(b2_in, 16)

            @block.scalar
            def _(act):
                act.dma_start(ident[:, :], ident_d).then_inc(qkv_in, 16)
                act.dma_start(qst, Wq.rearrange("(k p) d h -> p k (d h)", p=P)).then_inc(qkv_in, 16)
                act.dma_start(w3f[:, :, NB:2 * NB], Wk.rearrange("(k p) d h -> p k (d h)", p=P)).then_inc(qkv_in, 16)
                act.dma_start(w3f[:, :, 2 * NB:3 * NB], Wv.rearrange("(k p) d h -> p k (d h)", p=P)).then_inc(qkv_in, 16)
                act.dma_start(w3f[:, :, 3 * NB:3 * NB + EXPERTS],
                              gate_w[0:E].rearrange("(k p) e -> p k e", p=P)).then_inc(qkv_in, 16)
                act.wait_ge(x0_in, 16)
                act.wait_ge(rstd0_done, 1)
                for b in range(B):
                    act.activation(x0[:, b], x0[:, b], ACT.Identity, bias=nmr0[:, b:b + 1],
                                   scale=rstd0[:, b:b + 1]).then_inc(xn0_done, 1)
                for n in range(2 * EXPERTS):
                    act.wait_ge(w_in[n % 2], 16 * (n // 2 + 1))
                    act.activation((w1h, w2h)[n % 2][:, n // 2], wst[:, n % 2], ACT.Copy).then_inc(hi_done, 1)
                    if n in (1, 3):
                        b = n // 2
                        act.wait_ge(rstd_done, b + 1)
                        with act.Fori(0, BT) as t:
                            tile = flat(xall[:, b, bass.ds(t, 1), :])
                            act.activation(tile, tile, ACT.Abs,
                                           bias=nmr[:, bass.ds(t + b * BT, 1)], scale=rstd[:, bass.ds(t + b * BT, 1)],
                                           accum_out=abs_sum[:, bass.ds(t + b * BT, 1)]).then_inc(abs_done, 1)

            @block.vector
            def _(dve):
                dve.wait_ge(x0_in, 16)
                for b in range(B):
                    dve.bn_stats(stats0[:, b], x0[:, b])
                dve.drain()
                for b in range(B):
                    dve.bn_aggr(mv0[:, b], stats0[:, b])
                dve.drain().then_inc(stats0_done, 1)
                for b in range(B):
                    dve.wait_ge(x_in[b], 16)
                    with dve.Fori(0, BT) as t:
                        dve.bn_stats(stats[:, bass.ds(t + b * BT, 1), :], flat(xall[:, b, bass.ds(t, 1), :]))
                    dve.drain()
                    for t in range(b * BT, b * BT + BT):
                        dve.bn_aggr(mean_var[:, t], stats[:, t])
                    dve.drain().then_inc(stats_done, 1)
                dve.wait_ge(consts, 2)
                dve.wait_ge(qkv_in, 80)
                dve.wait_ge(small_in, 128)
                dve.tensor_reduce(w3f[:, :, 0:NB], qst.rearrange("p k (d g) -> p k d g", g=G), AX.X, ALU.add).then_inc(q_summed, 1)
                for b in range(B):
                    dve.tensor_reduce(bias_row[:, b, 0:NB], bst[:, 0:E].rearrange("p (d g) -> p d g", g=G), AX.X, ALU.add)
                    dve.tensor_copy(bias_row[:, b, NB:3 * NB], bst[:, E:])
                dve.tensor_copy(b2p[0:1], b2st[:, :, :])
                dve.drain()
                dve.tensor_copy(w3h[:, :, :], w3f[:, :, :])
                dve.tensor_tensor(b2l[:, :, :], b2st[:, :, :], b2p[0:1].bitcast(F32), ALU.subtract).then_inc(b2_split, 1)
                dve.drain()
                dve.tensor_tensor(w3l[:, :, :], w3f[:, :, :], w3h[:, :, :].bitcast(F32), ALU.subtract)
                for n in range(2 * EXPERTS):
                    dve.wait_ge(hi_done, n + 1)
                    e = n // 2
                    dve.tensor_tensor((w1l, w2l)[n % 2][:, e], wst[:, n % 2], (w1h, w2h)[n % 2][:, e].bitcast(F32),
                                      ALU.subtract).then_inc(lo_done, 1)
                dve.wait_ge(xn0_done, B)
                gview = gws[:, 0:E * EXPERTS].rearrange("p (a e) -> p e a", e=EXPERTS)
                for b in range(B):
                    for e in range(EXPERTS):
                        dve.tensor_tensor(prod0[:, :], x0[:, b], gview[:, e], ALU.mult)
                        dve.drain()
                        dve.tensor_reduce(logits0[:, b, e:e + 1], prod0[:, :], AX.X, ALU.add)
                        dve.drain()
                dve.wait_ge(abs_done, TILES)
                for k in range(2):
                    dve.tensor_tensor(weighed[:, k], strength[:, k], abs_sum[:, :], ALU.mult)
                dve.drain().then_inc(weighed_done, 1)
                dve.wait_ge(strength_ready, 1)
                dve.tensor_reduce(means[:, :, :], ps[:, :, :].rearrange("p k (b t) -> p k b t", b=B), AX.X, ALU.add)
                dve.drain()
                dve.tensor_scalar(means[:, 1], means[:, 1], 1e-8, None, ALU.add)
                dve.drain()
                dve.reciprocal(ratio[:, :], means[:, 1])
                dve.drain()
                dve.tensor_tensor(ratio[:, :], ratio[:, :], means[:, 0], ALU.mult)
                dve.drain()
                for b in range(B):
                    dve.scalar_tensor_tensor(out=bias_row[:, b, 3 * NB:3 * NB + EXPERTS], in0=gws[:, E * EXPERTS:],
                                             scalar=ratio[:, b:b + 1], in1=gbs[:, :], op0=ALU.mult, op1=ALU.add)
                dve.drain()
                dve.tensor_tensor(logits0[:, :, :], logits0[:, :, :], bias_row[:, :, 3 * NB:3 * NB + EXPERTS], ALU.add)
                dve.drain()
                for n, (i, j) in enumerate(((0, 1), (0, 2), (1, 2))):
                    dve.tensor_tensor(ge[:, :, n:n + 1], logits0[:, :, i:i + 1], logits0[:, :, j:j + 1], ALU.is_ge)
                dve.drain()
                dve.tensor_tensor(rank[:, :, 0:1], ge[:, :, 0:1], ge[:, :, 1:2], ALU.add)
                dve.tensor_tensor(rank[:, :, 1:2], ge[:, :, 0:1], ge[:, :, 2:3], ALU.subtract)
                dve.tensor_tensor(rank[:, :, 2:3], ge[:, :, 1:2], ge[:, :, 2:3], ALU.add)
                dve.drain()
                dve.tensor_scalar(rank[:, :, 0:1], rank[:, :, 0:1], -1.0, 2.0, ALU.mult, ALU.add)
                dve.tensor_scalar(rank[:, :, 1:2], rank[:, :, 1:2], 1.0, None, ALU.add)
                dve.drain()
                for i in range(2):
                    dve.tensor_scalar(select[:, :, i], rank[:, :, :], float(i), None, ALU.is_equal)
                dve.drain()

            @block.tensor
            def _(pe):
                pe.wait_ge(consts, 1)
                pe.wait_ge(weighed_done, 1)
                pe.matmul(ps[:, :, :], ones[:, :], weighed[:, :, :], start=True, stop=True).then_inc(strength_ready, 1)

        xb = sb("xb", [P, 2, TPC, E])
        xn = sb("xn", [P, TPC, E])
        xth, xtl = sb("xth", [P, KT, CH], F32R), sb("xtl", [P, KT, CH], F32R)
        af = sb("af", [P, 2, CH])
        ah, al = sb("ah", [P, 2, CH], F32R), sb("al", [P, 2, CH], F32R)
        qkv = sb("qkv", [P, TPC, QKV])
        moe = sb("moe", [P, TPC, E])
        pa, pb = sb("pa", [P, D, D, HKV]), sb("pb", [P, D, HKV, D])
        sc, at = sb("sc", [P, D, D]), sb("at", [P, D, D])
        smax, rsum = sb("smax", [P, D]), sb("rsum", [P, D])
        so = sb("so", [P, D, HKV])
        s_sb = sb("s_sb", [P, TPC, D, HKV])
        gl, gexp = sb("gl", [P, TPC, EXPERTS]), sb("gexp", [P, TPC, EXPERTS])
        gt = sb("gt", [P, 6, TPC])
        coef, coef2 = sb("coef", [P, TPC, EXPERTS]), sb("coef2", [P, TPC, EXPERTS])
        bank = ctx.enter_context(nc.psum_tensor("bank", [P, 8, 512], F32))

        xin = [sem(f"xin{u}") for u in range(2)]
        xout = [sem(f"xout{u}") for u in range(2)]
        xn_ready, tp_ready, xth_ready, xtl_ready = sem("xn_ready"), sem("tp_ready"), sem("xth_ready"), sem("xtl_ready")
        qkv_ps, qkv_ready = sem("qkv_ps"), sem("qkv_ready")
        p1_done, redA, sc_ready, exp_done, p2_done, redB = (sem(n) for n in ("p1_done", "redA", "sc_ready", "exp_done", "p2_done", "redB"))
        gl_ready, gexp_ready = sem("gl_ready"), sem("gexp_ready")
        f1_ps, act_ready, split_ready, f2_step, f2_evac = (sem(n) for n in ("f1_ps", "act_ready", "split_ready", "f2_step", "f2_evac"))
        th_ready, th_used, x1_ready = sem("th_ready"), sem("th_used"), sem("x1_ready")
        NF = EXPERTS * KT
        x1v = x1_d.rearrange("(c t p) e -> p c t e", p=P, t=TPC)
        xv = x.rearrange("b (c t p) e -> p (b c) t e", p=P, t=TPC)

        def chunks(eng, body):
            with eng.Fori(0, CHUNKS // 2) as j:
                for u in range(2):
                    body(j * 2 + u, u, j)

        block = ctx.enter_context(nc.Block())

        @block.sync
        def _(sp):
            sp.sem_inc(x1_ready, 1)
            for u in range(2):
                sp.dma_start(xb[:, u], xv[:, u]).then_inc(xin[u], 16)

            def body(c, u, j):
                sp.wait_ge(x1_ready, c * TPC + 1 + TPC)
                sp.dma_start(x1v[:, bass.ds(c, 1)].rearrange("p c t e -> p (c t) e"), xb[:, u]).then_inc(xout[u], 16)
                sp.wait_ge(xout[u], j * 16 + 16)
            with sp.Fori(0, CHUNKS // 2 - 1) as j:
                for u in range(2):
                    body(j * 2 + u, u, j)
                    sp.dma_start(xb[:, u], xv[:, bass.ds(j * 2 + u + 2, 1)].rearrange("p c t e -> p (c t) e")).then_inc(xin[u], 16)
            for u in range(2):
                c = CHUNKS - 2 + u
                sp.wait_ge(x1_ready, c * TPC + 1 + TPC)
                sp.dma_start(x1v[:, c], xb[:, u]).then_inc(xout[u], 16)
                sp.wait_ge(xout[u], 16 * (CHUNKS // 2))

        @block.gpsimd
        def _(pool):
            def body(c, u, j):
                for t in range(TPC):
                    pool.wait_ge(qkv_ready, c * TPC + t + 1)
                    pool.wait_ge(redA, c * TPC + t + 1)
                    q = qkv[:, t, 0:NB].rearrange("p (d o h) -> p d o h", o=1, h=HKV).broadcast_to([P, D, D, HKV])
                    k = qkv[:, t, NB:2 * NB].rearrange("p (o e h) -> p o e h", o=1, h=HKV).broadcast_to([P, D, D, HKV])
                    pool.tensor_tensor(pa[:, :, :, :], q, k, ALU.mult).then_inc(p1_done, 1)
                    pool.wait_ge(exp_done, c * TPC + t + 1)
                    pool.wait_ge(redB, c * TPC + t + 1)
                    a = at[:, :, :].rearrange("p d (o e) -> p d o e", o=1).broadcast_to([P, D, HKV, D])
                    v = qkv[:, t, 2 * NB:3 * NB].rearrange("p (o e h) -> p o h e", o=1, h=HKV).broadcast_to([P, D, HKV, D])
                    pool.tensor_tensor(pb[:, :, :, :], a, v, ALU.mult).then_inc(p2_done, 1)
            chunks(pool, body)

        @block.scalar
        def _(act):
            act.sem_inc(p2_done, 1)

            def body(c, u, j):
                act.wait_ge(xin[u], j * 16 + 16)
                for t in range(TPC):
                    act.wait_ge(tp_ready, c * TPC + 1)
                    act.activation(xn[:, t], xb[:, u, t], ACT.Identity, bias=nmr[:, bass.ds(c * TPC + t, 1)],
                                   scale=rstd[:, bass.ds(c * TPC + t, 1)]).then_inc(xn_ready, 1)
                act.wait_ge(f1_ps, c * NF + 1)
                act.wait_ge(qkv_ps, c * TPC + 1)
                for t in range(TPC):
                    act.wait_ge(tp_ready, c * TPC + t + 2)
                    act.activation(xth[:, :, t * P:t * P + P], bank[:, t % 2].rearrange("p (k q) -> p k q", k=KT),
                                   ACT.Copy).then_inc(xth_ready, 1)
                act.wait_ge(gl_ready, c + 1)
                act.activation(gexp[:, :, :], gl[:, :, :], ACT.Exp).then_inc(gexp_ready, 1)
                for e in range(EXPERTS):
                    f = (ACT.Tanh, ACT.Gelu, ACT.Silu)[e]
                    for n in range(KT):
                        m = e * KT + n
                        act.wait_ge(f1_ps, c * NF + m + 2)
                        act.wait_ge(f2_step, c * NF + m)
                        if m < 2:
                            act.wait_ge(th_used, c * TPC + 2)
                        act.activation(af[:, m % 2], bank[:, 2 + m % 2], f, bias=b1_sb[:, e, n:n + 1])
                        act.activation(ah[:, m % 2], bank[:, 2 + m % 2], f, bias=b1_sb[:, e, n:n + 1]).then_inc(act_ready, 1)
                        if m % 3 == 0:
                            t = m // 3
                            act.wait_ge(sc_ready, c * TPC + t + 1)
                            act.wait_ge(p2_done, c * TPC + t + 1)
                            act.activation(at[:, :, :], sc[:, :, :], ACT.Exp, scale=D ** -0.5).then_inc(exp_done, 1)
                for t in range(TPC):
                    act.wait_ge(f2_evac, c * EXPERTS * TPC + 2 * TPC + t + 2)
                    act.wait_ge(th_used, c * TPC + t + 1)
                    act.activation(af[:, t % 2], moe[:, t], ACT.Tanh, scale=0.5).then_inc(th_ready, 1)
            chunks(act, body)

        @block.vector
        def _(dve):
            dve.sem_inc(redA, 1)
            dve.sem_inc(redB, 1)
            dve.sem_inc(f2_evac, 1)
            dve.sem_inc(th_used, 2)
            dve.sem_inc(split_ready, 1)

            def scores(c, t):
                dve.wait_ge(p1_done, c * TPC + t + 1)
                dve.tensor_reduce(sc[:, :, :], pa[:, :, :, :], AX.X, ALU.add).then_inc(redA, 1)
                dve.drain()
                dve.tensor_reduce(smax[:, :], sc[:, :, :], AX.X, ALU.max)
                dve.drain()
                dve.tensor_tensor(sc[:, :, :], sc[:, :, :], smax[:, :].rearrange("p (d o) -> p d o", o=1).broadcast_to([P, D, D]),
                                  ALU.subtract).then_inc(sc_ready, 1)

            def sums(c, t):
                dve.wait_ge(exp_done, c * TPC + t + 1)
                dve.tensor_reduce(rsum[:, :], at[:, :, :], AX.X, ALU.add)
                dve.drain()
                dve.reciprocal(rsum[:, :], rsum[:, :])

            def mix(c, t):
                dve.wait_ge(p2_done, c * TPC + t + 2)
                dve.tensor_reduce(so[:, :, :], pb[:, :, :, :], AX.X, ALU.add).then_inc(redB, 1)
                dve.drain()
                dve.scalar_tensor_tensor(out=s_sb[:, t], in0=so[:, :, :], scalar=0.5,
                                         in1=rsum[:, :].rearrange("p (d o) -> p d o", o=1).broadcast_to([P, D, HKV]),
                                         op0=ALU.mult, op1=ALU.mult)

            def body(c, u, j):
                dve.wait_ge(qkv_ps, c * TPC + 1)
                dve.wait_ge(f1_ps, c * NF + 1)
                for t in range(TPC):
                    dve.wait_ge(xth_ready, c * TPC + t + 1)
                    dve.tensor_tensor(xtl[:, :, t * P:t * P + P], bank[:, t % 2].rearrange("p (k q) -> p k q", k=KT),
                                      xth[:, :, t * P:t * P + P].bitcast(F32), ALU.subtract).then_inc(xtl_ready, 1)
                for t in range(TPC):
                    dve.wait_ge(qkv_ps, c * TPC + t + 2)
                    dve.tensor_tensor(qkv[:, t], bank[:, t % 2, 0:QKV], flat(bias_row[:, bass.ds(j, 1), :]),
                                      ALU.add).then_inc(qkv_ready, 1)
                dve.drain()
                lg = qkv[:, :, 3 * NB:3 * NB + EXPERTS]
                dve.tensor_reduce(gt[:, 0], lg, AX.X, ALU.max)
                dve.drain()
                dve.tensor_tensor(gl[:, :, :], lg, gt[:, 0].rearrange("p (t o) -> p t o", o=1).broadcast_to([P, TPC, EXPERTS]),
                                  ALU.subtract).then_inc(gl_ready, 1)
                dve.wait_ge(gexp_ready, c + 1)
                dve.tensor_reduce(gt[:, 0], gexp[:, :, :], AX.X, ALU.add)
                dve.tensor_tensor(gt[:, 1], gexp[:, :, 0], gexp[:, :, 1], ALU.max)
                dve.tensor_tensor(gt[:, 2], gexp[:, :, 0], gexp[:, :, 1], ALU.min)
                dve.drain()
                dve.tensor_tensor(gt[:, 3], gt[:, 1], gexp[:, :, 2], ALU.min)
                dve.tensor_tensor(gt[:, 4], gt[:, 1], gexp[:, :, 2], ALU.max)
                dve.drain()
                dve.tensor_tensor(gt[:, 5], gt[:, 3], gt[:, 2], ALU.max)
                dve.drain()
                dve.scalar_tensor_tensor(out=gt[:, 0], in0=gt[:, 0], scalar=1e-8, in1=gt[:, 4], op0=ALU.mult, op1=ALU.add)
                dve.drain()
                dve.tensor_tensor(gt[:, 0], gt[:, 0], gt[:, 5], ALU.add)
                dve.drain()
                dve.reciprocal(gt[:, 1], gt[:, 0])
                dve.drain()
                dve.tensor_tensor(gt[:, 4], gt[:, 4], gt[:, 1], ALU.mult)
                dve.tensor_tensor(gt[:, 5], gt[:, 5], gt[:, 1], ALU.mult)
                dve.drain()
                for i, dst in enumerate((coef, coef2)):
                    val = gt[:, 4 + i].rearrange("p (t o) -> p t o", o=1).broadcast_to([P, TPC, EXPERTS])
                    chosen = flat(select[:, bass.ds(j, 1), i, :]).rearrange("p (o e) -> p o e", o=1).broadcast_to([P, TPC, EXPERTS])
                    dve.tensor_tensor(dst[:, :, :], val, chosen, ALU.mult)
                dve.drain()
                dve.tensor_tensor(coef[:, :, :], coef[:, :, :], coef2[:, :, :], ALU.add)
                scores(c, 0)
                for m in range(NF):
                    e = m // KT
                    dve.wait_ge(act_ready, c * NF + m + 1)
                    dve.tensor_tensor(al[:, m % 2], af[:, m % 2], ah[:, m % 2].bitcast(F32), ALU.subtract).then_inc(split_ready, 1)
                    t = m // 3
                    if m % 3 == 0:
                        sums(c, t)
                    if m % 3 == 1:
                        mix(c, t)
                    if m % 3 == 2 and t < TPC - 1:
                        scores(c, t + 1)
                    if (m % KT == 1 and e > 0) or m == NF - 1:
                        ee = e - 1 if m < NF - 1 else e
                        for t in range(TPC):
                            dve.wait_ge(f2_step, c * NF + (ee + 1) * KT + 2)
                            if ee == 0:
                                dve.tensor_scalar(moe[:, t], bank[:, 4 + t], coef[:, t, 0:1], None, ALU.mult).then_inc(f2_evac, 1)
                            else:
                                dve.scalar_tensor_tensor(out=moe[:, t], in0=bank[:, 4 + t], scalar=coef[:, t, ee:ee + 1],
                                                         in1=moe[:, t], op0=ALU.mult, op1=ALU.add).then_inc(f2_evac, 1)
                for t in range(TPC):
                    dve.wait_ge(th_ready, c * TPC + t + 1)
                    dve.scalar_tensor_tensor(out=moe[:, t], in0=af[:, t % 2], scalar=1.0, in1=moe[:, t],
                                             op0=ALU.add, op1=ALU.mult).then_inc(th_used, 1)
                    dve.drain()
                    m4 = moe[:, t].rearrange("p (a g) -> p a g", g=G)
                    s4 = s_sb[:, t].rearrange("p d (h o) -> p (d h) o", o=1).broadcast_to([P, NB, G])
                    dve.tensor_tensor(m4, m4, s4, ALU.mult)
                    dve.drain()
                    dve.tensor_tensor(xb[:, u, t], xb[:, u, t], moe[:, t], ALU.add).then_inc(x1_ready, 1)
            chunks(dve, body)

        @block.tensor
        def _(pe):
            pe.sem_inc(tp_ready, 1)
            pe.sem_inc(qkv_ps, 1)
            pe.sem_inc(f1_ps, 1)
            pe.sem_inc(f2_step, 2)

            def three(out, wh, wl, mh, ml, first, last):
                pe.matmul(out, wh, ml, start=first, stop=False)
                pe.matmul(out, wl, mh, start=False, stop=False)
                return pe.matmul(out, wh, mh, start=False, stop=last)

            def second_product(c, m):
                e, n = m // KT, m % KT
                pe.wait_ge(split_ready, c * NF + m + 2)
                if n == 0:
                    pe.wait_ge(f2_evac, (c * EXPERTS + e) * TPC + 1)
                for t in range(TPC):
                    out = bank[:, 4 + t]
                    if n == 0:
                        pe.matmul(out, ones_r[:, :], b2p[:, e], start=True, stop=False)
                    mm = three(out, ah[:, m % 2, t * P:t * P + P], al[:, m % 2, t * P:t * P + P], w2h[:, e, n], w2l[:, e, n],
                               False, n == KT - 1)
                mm.then_inc(f2_step, 1)

            def body(c, u, j):
                pe.wait_ge(split_ready, c * NF + 1)
                for t in range(TPC):
                    pe.wait_ge(xn_ready, c * TPC + t + 1)
                    if t >= 2:
                        pe.wait_ge(xtl_ready, c * TPC + t - 1)
                    for k in range(KT):
                        mm = pe.transpose(bank[:, t % 2, k * P:k * P + P], xn[:, t, k * P:k * P + P], ident[:, :])
                    mm.then_inc(tp_ready, 1)
                pe.wait_ge(xtl_ready, c * TPC + TPC)
                for t in range(TPC):
                    if t >= 2:
                        pe.wait_ge(qkv_ready, c * TPC + t - 1)
                    for k in range(KT):
                        mm = three(bank[:, t % 2, 0:QKV], xth[:, k, t * P:t * P + P], xtl[:, k, t * P:t * P + P],
                                   w3h[:, k], w3l[:, k], k == 0, k == KT - 1)
                    mm.then_inc(qkv_ps, 1)
                for m in range(NF + 1):
                    if m < NF:
                        e, n = m // KT, m % KT
                        if m >= 2:
                            pe.wait_ge(act_ready, c * NF + m - 1)
                        for k in range(KT):
                            mm = three(bank[:, 2 + m % 2], w1h[:, e, k, n * P:n * P + P], w1l[:, e, k, n * P:n * P + P],
                                       xth[:, k], xtl[:, k], k == 0, k == KT - 1)
                        mm.then_inc(f1_ps, 1)
                    if m >= 1:
                        second_product(c, m - 1)
                pe.wait_ge(qkv_ready, c * TPC + TPC)
            chunks(pe, body)


INTER = 1376
SG, SD = 4, 10
FT = (INTER + P - 1) // P
FW = [min(P, INTER - n * P) for n in range(FT)]
STEPS = [list(range(n, min(n + 2, FT))) for n in range(0, FT, 2)]
QKT = 2 * NB + E
NG = B * HKV
NBITS, PACK = 4, 8


def three(pe, out, wh, wl, mh, ml, first, last):
    pe.matmul(out, wh, ml, start=first, stop=False)
    pe.matmul(out, wl, mh, start=False, stop=False)
    return pe.matmul(out, wh, mh, start=False, stop=last)


def chunk_pairs(eng, body):
    with eng.Fori(0, CHUNKS // 2) as b:
        for u in range(2):
            body(b * 2 + u, u, b)


def layer1_projections(nc, Wq, Wk, Wv, ident_d, rotate_d, cos_d, sin_d, x1_d, q_scr, k_scr, xth, xtl, v_all):
    with ExitStack() as ctx:
        def sb(name, shape, dt=F32):
            return ctx.enter_context(nc.sbuf_tensor("c_" + name, shape, dt))

        def sem(name):
            return ctx.enter_context(nc.semaphore("c_" + name))

        OT = QKT // P
        ROT = OT - 1
        ident, rotate = sb("ident", [P, P]), sb("rotate", [P, P])
        cos, sin = sb("cos", [P, T]), sb("sin", [P, T])
        wn = sb("wn", [P, OT, E])
        wth, wtl = sb("wth", [P, KT, QKT], F32R), sb("wtl", [P, KT, QKT], F32R)
        xb, xn = sb("xb", [P, 2, TPC, E]), sb("xn", [P, TPC, E])
        stats, mv = sb("stats", [P, TPC, 6]), sb("mv", [P, TPC, 2])
        neg_half, veps = sb("neg_half", [P, TPC]), sb("veps", [P, TPC])
        rstd, nmr = sb("rstd", [P, TPC]), sb("nmr", [P, TPC])
        qf, qc, qs = sb("qf", [P, 2, CH]), sb("qc", [P, 2, CH]), sb("qs", [P, 2, CH])
        qh, ql = sb("qh", [P, 2, CH], F32R), sb("ql", [P, 2, CH], F32R)
        bank = ctx.enter_context(nc.psum_tensor("c_bank", [P, 8, 512], F32))
        w_in, ident_in, table_in = sem("w_in"), sem("ident_in"), sem("table_in")
        xin = [sem(f"xin{u}") for u in range(2)]
        q_out = [sem(f"q_out{u}") for u in range(2)]
        w_tp, w_hi, w_lo = sem("w_tp"), sem("w_hi"), sem("w_lo")
        stats_done, stats_seen, rstd_done, xn_ready = sem("stats_done"), sem("stats_seen"), sem("rstd_done"), sem("xn_ready")
        tp_ready, xth_ready, xtl_ready = sem("tp_ready"), sem("xth_ready"), sem("xtl_ready")
        proj_ps, qf_ready, rot_ps, qc_ready, rope_ready = (sem(n) for n in ("proj_ps", "qf_ready", "rot_ps", "qc_ready", "rope_ready"))
        qh_ready, ql_ready, q_free, v_tp, v_ready = (sem(n) for n in ("qh_ready", "ql_ready", "q_free", "v_tp", "v_ready"))
        x1v = x1_d.rearrange("(c t p) e -> p c t e", p=P, t=TPC)

        def before(c, m, n):
            return c * n + 2 + max(0, m - 1)

        block = ctx.enter_context(nc.Block())

        @block.sync
        def _(sp):
            sp.sem_inc(q_free, 2)
            for u in range(2):
                sp.dma_start(xb[:, u], x1v[:, u]).then_inc(xin[u], 16)

            def store(c, u, b):
                for m in range(ROT):
                    sp.wait_ge(ql_ready, c * ROT + m + 1)
                    heads = P // D
                    if m < ROT - 1:
                        dst, parts = q_scr[bass.ds(b * (HKV * G) + m * heads, heads)], (qh, ql, qh)
                    else:
                        dst, parts = k_scr[bass.ds(b * HKV, HKV)], (qh, qh, ql)
                    for n, part in enumerate(parts):
                        sp.dma_start(dst[:, n, :, u * CH:u * CH + CH], part[:, m % 2].bitcast(F32)).then_inc(q_out[m % 2], 16)
                    for k in ([m - 1] if m else []) + ([m] if m == ROT - 1 else []):
                        each = (ROT + 1 - k % 2) // 2
                        sp.wait_ge(q_out[k % 2], (c * each + k // 2 + 1) * 48)
                        sp.sem_inc(q_free, 1)

            with sp.Fori(0, CHUNKS // 2 - 1) as b:
                for u in range(2):
                    store(b * 2 + u, u, b)
                    sp.wait_ge(xn_ready, (b * 2 + u) * TPC + TPC)
                    sp.wait_ge(stats_done, b * 2 + u + 1)
                    sp.dma_start(xb[:, u], x1v[:, bass.ds(b * 2 + u + 2, 1)].rearrange("p c t e -> p (c t) e")).then_inc(xin[u], 16)
            for u in range(2):
                store(CHUNKS - 2 + u, u, CHUNKS // 2 - 1)

        @block.gpsimd
        def _(pool):
            pool.sem_inc(qc_ready, 2)
            pool.memset(v_all[:, :, :, D:], 0.0)
            pool.memset(neg_half[:, :], -0.5)
            pool.drain()
            pool.memset(v_all[:, :, :, D:D + 1], 1.0)
            pool.drain()

            def body(c, u, b):
                pool.wait_ge(stats_done, c + 1)
                pool.sem_inc(stats_seen, 1)
                pool.tensor_scalar(veps[:, :], mv[:, :, 1], EPS, None, ALU.add)
                pool.drain()
                pool.wait_ge(tp_ready, c * TPC + 1)
                pool.tensor_tensor(rstd[:, :], veps[:, :], neg_half[:, :], ALU.pow)
                pool.drain()
                pool.tensor_tensor(nmr[:, :], mv[:, :, 0], rstd[:, :], ALU.mult)
                pool.drain()
                pool.tensor_scalar(nmr[:, :], nmr[:, :], -1.0, None, ALU.mult).then_inc(rstd_done, 1)
                pool.wait_ge(table_in, 32)
                for m in range(ROT):
                    pool.wait_ge(qf_ready, c * OT + m + 3)
                    pool.wait_ge(rope_ready, before(c, m, ROT))
                    pool.tensor_tensor(qc[:, m % 2], qf[:, m % 2], cos[:, u * CH:u * CH + CH], ALU.mult).then_inc(qc_ready, 1)
            chunk_pairs(pool, body)

        @block.scalar
        def _(act):
            act.dma_start(wn[:, 0:KT], Wq.rearrange("(o p) e -> p o e", p=P)).then_inc(w_in, 16)
            act.dma_start(wn[:, KT], Wk).then_inc(w_in, 16)
            act.dma_start(wn[:, KT + 1], Wv).then_inc(w_in, 16)
            act.dma_start(ident[:, :], ident_d).then_inc(ident_in, 16)
            act.dma_start(rotate[:, :], rotate_d).then_inc(ident_in, 16)
            act.dma_start(cos[:, :], cos_d).then_inc(table_in, 16)
            act.dma_start(sin[:, :], sin_d).then_inc(table_in, 16)
            act.sem_inc(qf_ready, 2)
            for o in range(OT):
                act.wait_ge(w_tp, o + 1)
                act.activation(wth[:, :, o * P:o * P + P], bank[:, o % 2].rearrange("p (k q) -> p k q", k=KT),
                               ACT.Copy).then_inc(w_hi, 1)

            def body(c, u, b):
                act.wait_ge(xin[u], b * 16 + 16)
                act.wait_ge(rstd_done, c + 1)
                act.wait_ge(tp_ready, c * TPC + 1)
                for t in range(TPC):
                    act.activation(xn[:, t], xb[:, u, t], ACT.Identity, bias=nmr[:, t:t + 1],
                                   scale=rstd[:, t:t + 1]).then_inc(xn_ready, 1)
                for t in range(TPC):
                    act.wait_ge(tp_ready, c * TPC + t + 2)
                    act.activation(xth[:, :, bass.ds((c * TPC + t) * P, P)], bank[:, t % 2].rearrange("p (k q) -> p k q", k=KT),
                                   ACT.Copy).then_inc(xth_ready, 1)
                for m in range(OT + 1):
                    if m < OT:
                        act.wait_ge(proj_ps, c * OT + m + 1)
                        if m == 1:
                            act.wait_ge(v_tp, c + 1)
                        else:
                            act.wait_ge(qc_ready, c * ROT + 2 + max(0, m - 1))
                            act.wait_ge(rot_ps, c * ROT + 2 + max(0, m - 1))
                        act.activation(qf[:, m % 2], bank[:, 2 + m % 2], ACT.Copy).then_inc(qf_ready, 1)
                    if 1 <= m <= ROT:
                        k = m - 1
                        act.wait_ge(rope_ready, c * ROT + k + 3)
                        act.wait_ge(q_free, before(c, k, ROT))
                        act.activation(qh[:, k % 2], qs[:, k % 2], ACT.Copy).then_inc(qh_ready, 1)
            chunk_pairs(act, body)

        @block.vector
        def _(dve):
            dve.sem_inc(rope_ready, 2)
            dve.sem_inc(v_ready, 1)
            for o in range(OT):
                dve.wait_ge(w_hi, o + 1)
                dve.tensor_tensor(wtl[:, :, o * P:o * P + P], bank[:, o % 2].rearrange("p (k q) -> p k q", k=KT),
                                  wth[:, :, o * P:o * P + P].bitcast(F32), ALU.subtract).then_inc(w_lo, 1)

            def body(c, u, b):
                dve.wait_ge(xin[u], b * 16 + 16)
                dve.wait_ge(tp_ready, c * TPC + 1)
                for t in range(TPC):
                    dve.bn_stats(stats[:, t], xb[:, u, t])
                dve.drain()
                for t in range(TPC):
                    dve.bn_aggr(mv[:, t], stats[:, t])
                dve.drain().then_inc(stats_done, 1)
                for t in range(TPC):
                    dve.wait_ge(xth_ready, c * TPC + t + 1)
                    at = bass.ds((c * TPC + t) * P, P)
                    dve.tensor_tensor(xtl[:, :, at], bank[:, t % 2].rearrange("p (k q) -> p k q", k=KT),
                                      xth[:, :, at].bitcast(F32), ALU.subtract).then_inc(xtl_ready, 1)
                dve.wait_ge(table_in, 32)
                for m in range(ROT):
                    dve.wait_ge(rot_ps, c * ROT + m + 3)
                    dve.tensor_tensor(qs[:, m % 2], bank[:, 4 + m % 2], sin[:, u * CH:u * CH + CH], ALU.mult)
                    dve.drain()
                    dve.wait_ge(qc_ready, c * ROT + m + 3)
                    dve.tensor_tensor(qs[:, m % 2], qs[:, m % 2], qc[:, m % 2], ALU.add).then_inc(rope_ready, 1)
                    dve.wait_ge(qh_ready, c * ROT + m + 1)
                    dve.tensor_tensor(ql[:, m % 2], qs[:, m % 2], qh[:, m % 2].bitcast(F32), ALU.subtract).then_inc(ql_ready, 1)
                dve.wait_ge(v_tp, c + 2)
                for t in range(TPC):
                    last = dve.tensor_copy(v_all[:, bass.ds(b * HKV, HKV), u * TPC + t, 0:D],
                                           bank[:, 6, t * P:t * P + P].rearrange("p (g d) -> p g d", d=D))
                last.then_inc(v_ready, 1)
            chunk_pairs(dve, body)

        @block.tensor
        def _(pe):
            pe.sem_inc(tp_ready, 1)
            pe.sem_inc(rot_ps, 2)
            pe.sem_inc(v_tp, 1)
            pe.wait_ge(w_in, 48)
            pe.wait_ge(ident_in, 32)
            for o in range(OT):
                if o >= 2:
                    pe.wait_ge(w_lo, o - 1)
                for k in range(KT):
                    mm = pe.transpose(bank[:, o % 2, k * P:k * P + P], wn[:, o, k * P:k * P + P], ident[:, :])
                mm.then_inc(w_tp, 1)
            pe.wait_ge(w_lo, OT)

            def body(c, u, b):
                for t in range(TPC):
                    pe.wait_ge(xn_ready, c * TPC + t + 1)
                    if t >= 2:
                        pe.wait_ge(xtl_ready, c * TPC + t - 1)
                    for k in range(KT):
                        mm = pe.transpose(bank[:, t % 2, k * P:k * P + P], xn[:, t, k * P:k * P + P], ident[:, :])
                    mm.then_inc(tp_ready, 1)
                pe.wait_ge(xtl_ready, c * TPC + TPC)
                now = bass.ds(c * CH, CH)
                for m in range(OT + 1):
                    if m < OT:
                        pe.wait_ge(qf_ready, before(c, m, OT))
                        for k in range(KT):
                            mm = three(pe, bank[:, 2 + m % 2], wth[:, k, m * P:m * P + P], wtl[:, k, m * P:m * P + P],
                                       xth[:, k, now], xtl[:, k, now], k == 0, k == KT - 1)
                        mm.then_inc(proj_ps, 1)
                    if m >= 1:
                        k = m - 1
                        pe.wait_ge(qf_ready, c * OT + k + 3)
                        if k < ROT:
                            pe.wait_ge(rope_ready, before(c, k, ROT))
                            pe.matmul(bank[:, 4 + k % 2], rotate[:, :], qf[:, k % 2], start=True, stop=True).then_inc(rot_ps, 1)
                        else:
                            pe.wait_ge(v_ready, c + 1)
                            for t in range(TPC):
                                mm = pe.transpose(bank[:, 6, t * P:t * P + P], qf[:, k % 2, t * P:t * P + P], ident[:, :])
                            mm.then_inc(v_tp, 1)
            chunk_pairs(pe, body)


def layer1_ffn(nc, qw_gu, qz_gu, sc_gu, gi_gu, qw_d, qz_d, sc_d, gi_d, shift_d, lane_shift_d, row_d, s_gu_scr, z_gu_scr,
               xth, xtl, acc):
    with ExitStack() as ctx:
        def sb(name, shape, dt=F32):
            return ctx.enter_context(nc.sbuf_tensor("d_" + name, shape, dt))

        def sem(name):
            return ctx.enter_context(nc.semaphore("d_" + name))

        W = 2 * P
        hot_gu, hot_d = sb("hot_gu", [2 * SG, E], F32R), sb("hot_d", [2 * SD, INTER], F32R)
        sd, zd = sb("sd", [2 * SD, E], F32R), sb("zd", [SD, E], F32R)
        lane_shift = sb("lane_shift", [P, 1], U32)
        with ExitStack() as c0:
            def sb0(name, shape, dt=F32):
                return c0.enter_context(nc.sbuf_tensor("e_" + name, shape, dt))

            def sem0(name):
                return c0.enter_context(nc.semaphore("e_" + name))

            F2 = 2 * INTER
            s_in, s_out, small = sem0("s_in"), sem0("s_out"), sem0("small")
            split, back = sem0("split"), sem0("back")
            sg = sb0("sg", [SG, F2])
            sgh, sgl = sb0("sgh", [SG, F2], F32R), sb0("sgl", [SG, F2], F32R)
            zg, zu = sb0("zg", [SG, F2 // PACK], U32), sb0("zu", [SG, F2 // PACK, PACK], U32)
            zdp, zdu = sb0("zdp", [SD, E // PACK], U32), sb0("zdu", [SD, E // PACK, PACK], U32)
            sdn, sdl = sb0("sdn", [SD, E]), sb0("sdl", [SD, E], F32R)
            shift = sb0("shift", [P, PACK], U32)
            row = sb0("row", [2 * SD, 2])
            idx = sb0("idx", [2 * SD, E + INTER], I32)
            idf = sb0("idf", [2 * SD, E + INTER])
            neg = sb0("neg", [2 * SD, E + INTER])
            block = c0.enter_context(nc.Block())

            @block.sync
            def _(sp):
                sp.dma_start(sg[:, :], sc_gu).then_inc(s_in, 16)
                sp.dma_start(zg[:, :], qz_gu).then_inc(s_in, 16)
                sp.dma_start(sdn[:, :], sc_d).then_inc(s_in, 16)
                sp.dma_start(zdp[:, :], qz_d).then_inc(s_in, 16)
                sp.dma_start(shift[:, :], shift_d).then_inc(s_in, 16)
                sp.dma_start(row[:, :], row_d).then_inc(s_in, 16)
                sp.dma_start(lane_shift[:, :], lane_shift_d).then_inc(s_in, 16)
                sp.dma_start(idx[:, 0:E], gi_gu.rearrange("(o k) -> o k", o=1).broadcast_to([2 * SD, E])).then_inc(s_in, 16)
                sp.dma_start(idx[:, E:], gi_d.rearrange("(o k) -> o k", o=1).broadcast_to([2 * SD, INTER])).then_inc(s_in, 16)
                sp.wait_ge(split, 1)
                sp.dma_start(s_gu_scr[0:SG], sgh[:, :].bitcast(F32)).then_inc(s_out, 16)
                sp.dma_start(s_gu_scr[SG:], sgl[:, :].bitcast(F32)).then_inc(s_out, 16)
                sp.dma_start(z_gu_scr, sg[:, :]).then_inc(s_out, 16)
                sp.dma_start(sd[SD:].bitcast(F32), sdl[:, :].bitcast(F32)).then_inc(s_out, 16)
                sp.wait_ge(s_out, 64)

            @block.vector
            def _(dve):
                dve.wait_ge(s_in, 144)
                dve.tensor_copy(sgh[:, :], sg[:, :])
                dve.tensor_copy(sd[0:SD], sdn[:, :])
                dve.drain()
                dve.tensor_tensor(sgl[:, :], sg[:, :], sgh[:, :].bitcast(F32), ALU.subtract)
                dve.tensor_tensor(sdl[:, :], sdn[:, :], sd[0:SD].bitcast(F32), ALU.subtract)
                for packed, out, n in ((zg, zu, SG), (zdp, zdu, SD)):
                    c = packed.shape[1]
                    dve.tensor_tensor(out[:, :, :], packed[:, :].rearrange("p (c o) -> p c o", o=1).broadcast_to([n, c, PACK]),
                                      shift[0:n, :].rearrange("p (o i) -> p o i", o=1).broadcast_to([n, c, PACK]),
                                      ALU.logical_shift_right)
                dve.drain()
                for out in (zu, zdu):
                    dve.tensor_scalar(out[:, :, :], out[:, :, :], 15, None, ALU.bitwise_and)
                dve.drain()
                dve.tensor_scalar(sg[:, :], zu[:, :, :].rearrange("p c i -> p (c i)"), 1.0, None, ALU.add)
                dve.tensor_scalar(zd[:, :], zdu[:, :, :].rearrange("p c i -> p (c i)"), 1.0, None, ALU.add)
                dve.tensor_copy(idf[:, :], idx[:, :])
                dve.drain()
                for at, n in ((slice(0, E), SG), (slice(E, E + INTER), SD)):
                    dve.tensor_scalar(neg[:, at], idf[:, at], 0.0, float(n), ALU.is_lt, ALU.mult)
                dve.drain()
                dve.tensor_tensor(idf[:, :], idf[:, :], neg[:, :], ALU.add)
                dve.drain()
                for at, n in ((slice(0, E), SG), (slice(E, E + INTER), SD)):
                    dve.tensor_scalar(idf[:, at], idf[:, at], 0.0, float(n - 1), ALU.max, ALU.min)
                dve.drain()
                dve.tensor_scalar(hot_gu[:, :], idf[0:2 * SG, 0:E], row[0:2 * SG, 0:1], None, ALU.is_equal)
                dve.tensor_scalar(hot_d[:, :], idf[:, E:], row[:, 1:2], None, ALU.is_equal)
                dve.drain().then_inc(split, 1)

        sz, zz = sb("sz", [2 * SG, 2, 2, W], F32R), sb("zz", [SG, 2, 2, W], F32R)
        hot = sb("hot", [2 * SD, 3, P], F32R)
        qw = sb("qw", [P, 2, 2 * W], U32)
        wq = sb("wq", [P, 2 * W], U32)
        wf = sb("wf", [P, 2 * W])
        wgh, wgl = sb("wgh", [P, 2, KT, 2, W], F32R), sb("wgl", [P, 2, KT, 2, W], F32R)
        wdh, wdl = sb("wdh", [P, 2, 2, E], F32R), sb("wdl", [P, 2, 2, E], F32R)
        hs = sb("hs", [P, 2, CH])
        hh, hl = sb("hh", [P, 2, CH], F32R), sb("hl", [P, 2, CH], F32R)
        bank = ctx.enter_context(nc.psum_tensor("d_bank", [P, 8, 512], F32))
        sz_in, qw_in2 = sem("sz_in"), sem("qw_in2")
        qw_in = [sem(f"qw_in{u}") for u in range(2)]
        hot_ready, row_ps, unpacked, w_ready = sem("hot_ready"), sem("row_ps"), sem("unpacked"), sem("w_ready")
        f1_ps, silu_ready, h_ready, hh_ready, hl_ready = (sem(n) for n in ("f1_ps", "silu_ready", "h_ready", "hh_ready", "hl_ready"))
        f2_tile, f2_ps, acc_ready, gate_ready = sem("f2_tile"), sem("f2_ps"), sem("acc_ready"), sem("gate_ready")
        tanh_ready = sem("tanh_ready")

        def piece_number(s, b, n):
            return b * 3 + (6 * s + n)

        PIECES = [(0, "gu"), (1, "gu"), (2, "down")]

        def tile(s, b, u, n):
            return (b * 2 + u) * len(STEPS[s]) + (CHUNKS * sum(len(STEPS[k]) for k in range(s)) + n)

        def slot(s, u, n):
            return n if len(STEPS[s]) == 2 else u

        qgv = qw_gu.rearrange("r (h f) -> r h f", h=2)
        block = ctx.enter_context(nc.Block())

        def each_pair(eng, body):
            for s in range(-1, len(STEPS)):
                with eng.Fori(0, CHUNKS // 2) as b:
                    body(s, b)

        @block.sync
        def _(sp):
            def body(s, b):
                if s + 1 == len(STEPS):
                    return
                tiles = STEPS[s + 1]
                f0, w = tiles[0] * P, sum(FW[n] for n in tiles)
                for n, kind in PIECES:
                    number = piece_number(s + 1, b, n)
                    sp.wait_ge(unpacked, number + (1 if n == 0 else 0))
                    dst = qw[:, (n if kind == "gu" else 0)]
                    if kind == "gu":
                        src = qgv[bass.ds((b * 2 + n) * (P // PACK), P // PACK), :, f0:f0 + w]
                        for h in range(2):
                            sp.dma_start(dst[:, h * W:h * W + w],
                                         src[:, h].rearrange("r (o f) -> r o f", o=1).broadcast_to([P // PACK, PACK, w])).then_inc(qw_in[n], 16)
                    else:
                        rows = FW[tiles[0]] // PACK
                        at = b * (P // PACK) + f0 // PACK if len(tiles) > 1 else f0 // PACK
                        src = qw_d[bass.ds(at, rows), :] if len(tiles) > 1 else qw_d[at:at + rows, :]
                        sp.dma_start(dst[0:rows * PACK, :],
                                     src.rearrange("r (o f) -> r o f", o=1).broadcast_to([rows, PACK, E])).then_inc(qw_in2, 16)

            def scales(s):
                if s > 0:
                    sp.wait_ge(w_ready, 6 * s + 1)
                tiles = STEPS[s]
                f0, w = tiles[0] * P, sum(FW[n] for n in tiles)
                for scr, dst in ((s_gu_scr, sz), (z_gu_scr, zz)):
                    sp.dma_start(dst[:, s % 2, :, 0:w].bitcast(F32), scr.rearrange("r (h f) -> r h f", h=2)[:, :, f0:f0 + w]).then_inc(sz_in, 16)

            sp.sem_inc(unpacked, 1)
            scales(0)
            with sp.Fori(0, CHUNKS // 2) as b:
                body(-1, b)
            for s in range(len(STEPS) - 1):
                scales(s + 1)
                with sp.Fori(0, CHUNKS // 2) as b:
                    body(s, b)

        @block.vector
        def _(dve):
            dve.sem_inc(h_ready, 2)
            dve.sem_inc(hl_ready, 2)
            dve.sem_inc(w_ready, 1)
            dve.sem_inc(acc_ready, 1)

            def pick(s, b):
                tiles = STEPS[s]
                rows = FW[tiles[0]]
                for n in range(2):
                    dve.tensor_copy(hot[0:2 * SG, n], hot_gu[:, bass.ds((b * 2 + n) * P, P)]).then_inc(hot_ready, 1)
                at = bass.ds(b * P + tiles[0] * P, P) if len(tiles) > 1 else slice(tiles[0] * P, tiles[0] * P + rows)
                dve.tensor_copy(hot[:, 2, 0:rows], hot_d[:, at]).then_inc(hot_ready, 1)

            def piece(s, b, n, kind):
                tiles = STEPS[s]
                w = sum(FW[k] for k in tiles)
                number = piece_number(s, b, n)
                rows = P if kind == "gu" else FW[tiles[0]]
                if kind == "gu":
                    dve.wait_ge(qw_in[n], (b + (2 * s + 1)) * 32)
                    v3 = lambda a: a.rearrange("p (h f) -> p h f", h=2)[0:rows, :, 0:w]
                    src, into = qw[:, n], (wgh[:, s % 2, bass.ds(b * 2 + n, 1)], wgl[:, s % 2, bass.ds(b * 2 + n, 1)])
                    into = [a.rearrange("p k h f -> p (k h) f")[:, :, 0:w] for a in into]
                else:
                    dve.wait_ge(qw_in2, (b + (2 * s + 1)) * 16)
                    v3 = lambda a: a[0:rows]
                    k = bass.ds(b, 1) if len(tiles) > 1 else slice(0, 1)
                    src, into = qw[:, 0], [flat(a[:, s % 2, k])[0:rows] for a in (wdh, wdl)]
                first = 2 * (n % 2)
                dve.tensor_scalar(v3(wq[:, :]), v3(src), lane_shift[0:rows, 0:1], 15, ALU.logical_shift_right,
                                  ALU.bitwise_and).then_inc(unpacked, 1)
                dve.drain()
                dve.wait_ge(row_ps, number + 1)
                dve.tensor_tensor(v3(wf[:, :]), v3(wq[:, :]), v3(bank[:, first + 1]), ALU.subtract)
                dve.drain()
                dve.tensor_tensor(v3(wf[:, :]), v3(wf[:, :]), v3(bank[:, first]), ALU.mult)
                dve.drain()
                dve.tensor_copy(into[0], v3(wf[:, :]))
                dve.drain()
                dve.tensor_tensor(into[1], v3(wf[:, :]), into[0].bitcast(F32), ALU.subtract).then_inc(w_ready, 1)

            def product(s, b, u, n):
                k, v, rows = tile(s, b, u, n), slot(s, u, n), FW[STEPS[s][n]]
                dve.wait_ge(silu_ready, k + 1)
                dve.tensor_tensor(hs[0:rows, v], hs[0:rows, v], bank[0:rows, 2 * v + 1], ALU.mult).then_inc(h_ready, 1)
                dve.wait_ge(hh_ready, k + 1)
                dve.tensor_tensor(hl[0:rows, v], hs[0:rows, v], hh[0:rows, v].bitcast(F32), ALU.subtract).then_inc(hl_ready, 1)

            def gather(s, b, u):
                for t in range(TPC):
                    dve.wait_ge(f2_ps, (b * 2 + u) * TPC + (s * TILES + t + 2))
                    a = flat(acc[:, bass.ds((b * 2 + u) * TPC + t, 1), :])
                    if s == 0:
                        dve.tensor_copy(a, bank[:, 4 + t]).then_inc(acc_ready, 1)
                    else:
                        dve.tensor_tensor(a, a, bank[:, 4 + t], ALU.add).then_inc(acc_ready, 1)

            def body(s, b):
                if s == -1:
                    dve.wait_ge(sz_in, 32)
                    pick(0, b)
                    for n, kind in PIECES:
                        piece(0, b, n, kind)
                    return
                two, making = len(STEPS[s]) == 2, s + 1 < len(STEPS)
                if making:
                    pick(s + 1, b)
                product(s, b, 0, 0)
                if making:
                    piece(s + 1, b, *PIECES[0])
                if two:
                    product(s, b, 0, 1)
                if making:
                    piece(s + 1, b, *PIECES[1])
                product(s, b, 1, 0)
                gather(s, b, 0)
                if making:
                    piece(s + 1, b, *PIECES[2])
                if two:
                    product(s, b, 1, 1)
                gather(s, b, 1)
            each_pair(dve, body)
            with dve.Fori(0, TILES // 2) as k:
                for n in range(2):
                    dve.wait_ge(tanh_ready, k * 2 + n + 1)
                    a = flat(acc[:, bass.ds(k * 2 + n, 1), :])
                    dve.scalar_tensor_tensor(out=a, in0=hs[:, n], scalar=1.0, in1=a, op0=ALU.add, op1=ALU.mult).then_inc(gate_ready, 1)

        @block.scalar
        def _(act):
            def body(s, b):
                if s == -1:
                    return
                for u in range(2):
                    for n in range(len(STEPS[s])):
                        k, v, rows = tile(s, b, u, n), slot(s, u, n), FW[STEPS[s][n]]
                        act.wait_ge(f1_ps, k + 1)
                        act.wait_ge(hl_ready, k + 1)
                        act.activation(hs[0:rows, v], bank[0:rows, 2 * v], ACT.Silu).then_inc(silu_ready, 1)
                        act.wait_ge(h_ready, k + 3)
                        if n + 1 < len(STEPS[s]):
                            act.wait_ge(f2_tile, b * 2 + (s * CHUNKS + u + 1))
                        else:
                            act.wait_ge(f2_ps, (b * 2 + u) * TPC + (s * TILES + 1))
                        act.activation(hh[0:rows, v], hs[0:rows, v], ACT.Copy).then_inc(hh_ready, 1)
            each_pair(act, body)
            act.wait_ge(hl_ready, CHUNKS * FT + 2)
            with act.Fori(0, TILES // 2) as k:
                for n in range(2):
                    act.wait_ge(acc_ready, k * 2 + (len(STEPS) - 1) * TILES + n + 2)
                    act.wait_ge(gate_ready, k * 2 + n + 1)
                    act.activation(hs[:, n], flat(acc[:, bass.ds(k * 2 + n, 1), :]), ACT.Tanh, scale=0.5).then_inc(tanh_ready, 1)

        @block.tensor
        def _(pe):
            pe.sem_inc(f2_ps, 1)
            pe.sem_inc(f2_tile, 1)
            pe.sem_inc(gate_ready, 2)

            def piece(s, b, n, kind):
                tiles = STEPS[s]
                w = sum(FW[k] for k in tiles)
                number = piece_number(s, b, n)
                first = 2 * (n % 2)
                pe.wait_ge(hot_ready, number + 1)
                pe.wait_ge(w_ready, number + (1 if n == 0 else 0))
                if kind == "gu":
                    out = [bank[:, first + k].rearrange("p (h f) -> p h f", h=2)[:, :, 0:w] for k in range(2)]
                    pe.matmul(out[0], hot[0:2 * SG, n], sz[:, s % 2, :, 0:w], start=True, stop=True)
                    pe.matmul(out[1], hot[0:SG, n], zz[:, s % 2, :, 0:w], start=True, stop=True).then_inc(row_ps, 1)
                else:
                    rows = FW[tiles[0]]
                    pe.matmul(bank[0:rows, first], hot[:, n, 0:rows], sd[:, :], start=True, stop=True)
                    pe.matmul(bank[0:rows, first + 1], hot[0:SD, n, 0:rows], zd[:, :], start=True, stop=True).then_inc(row_ps, 1)

            def gate_up(s, b, u, n, between=lambda: None):
                k, v, rows = tile(s, b, u, n), slot(s, u, n), FW[STEPS[s][n]]
                now = bass.ds((b * 2 + u) * CH, CH)
                pe.wait_ge(h_ready, k + 1)
                pe.wait_ge(w_ready, piece_number(s + 1, b, 0) + (n + 2 if u == 1 else 1) if s + 1 < len(STEPS)
                           else 6 * len(STEPS) + 1)
                for h in range(2):
                    if h == 1:
                        between()
                    for c in range(KT):
                        mm = three(pe, bank[0:rows, 2 * v + h], wgh[:, s % 2, c, h, n * P:n * P + rows],
                                   wgl[:, s % 2, c, h, n * P:n * P + rows], xth[:, c, now], xtl[:, c, now], c == 0, c == KT - 1)
                mm.then_inc(f1_ps, 1)

            def down(s, b, u, n):
                k, v, rows = tile(s, b, u, n), slot(s, u, n), FW[STEPS[s][n]]
                if n == 0:
                    pe.wait_ge(acc_ready, (b * 2 + u) * TPC + s * TILES + 1)
                pe.wait_ge(hl_ready, k + 3)
                last = n == len(STEPS[s]) - 1
                for t in range(TPC):
                    mm = three(pe, bank[:, 4 + t], hh[0:rows, v, t * P:t * P + P], hl[0:rows, v, t * P:t * P + P],
                               wdh[0:rows, s % 2, n], wdl[0:rows, s % 2, n], n == 0, last)
                    if last:
                        mm.then_inc(f2_ps, 1)
                if not last:
                    mm.then_inc(f2_tile, 1)

            def body(s, b):
                if s == -1:
                    pe.wait_ge(sz_in, 32)
                    for n, kind in PIECES:
                        piece(0, b, n, kind)
                    return
                two, making = len(STEPS[s]) == 2, s + 1 < len(STEPS)
                if making:
                    pe.wait_ge(sz_in, 32 * (s + 2))
                gate_up(s, b, 0, 0)

                def first_piece():
                    if making:
                        pe.wait_ge(h_ready, tile(s, b, 0, 0) + 3)
                        piece(s + 1, b, *PIECES[0])
                if two:
                    gate_up(s, b, 0, 1, first_piece)
                if two:
                    down(s, b, 0, 0)
                if making:
                    pe.wait_ge(h_ready, tile(s, b, 0, 1) + 3)
                    piece(s + 1, b, *PIECES[1])
                gate_up(s, b, 1, 0)
                down(s, b, 0, len(STEPS[s]) - 1)
                if making:
                    pe.wait_ge(h_ready, tile(s, b, 1, 0) + 3)
                    piece(s + 1, b, *PIECES[2])
                if two:
                    gate_up(s, b, 1, 1)
                    down(s, b, 1, 0)
                down(s, b, 1, len(STEPS[s]) - 1)
            each_pair(pe, body)


HG = G
QB = T // P
HALF = T // CH
QPH = CH // P
PART = 3 * D
M_ROW = 2 * PART
STACKS = 3
UNITS = [(0, k) for k in range(QPH)] + [(1, k) for k in (0, 4, 5, 6, 7, 1, 2, 3)]
NU, NC = len(UNITS), 2 * len(UNITS)
HEAD = 3
ITEMS = [(h, q, at, min(CH, (q + 1) * P - at)) for h in range(HG) for q in range(QB) for at in range(0, (q + 1) * P, CH)]
ITEMS_FROM, ITEMS_TO = HEAD, 19
TURN_MAXIMA = 19
TURN_FIRST_HALF = 11
LOADED = 4 * 16
LEAST = -3.0e38


def beside(c):
    cost = [w + 96 for *_, w in ITEMS]
    upto = lambda x: sum(sum(cost[:s + 1]) <= sum(cost) * x / (ITEMS_TO - ITEMS_FROM) + 1e-6 for s in range(len(ITEMS)))
    return range(upto(c - ITEMS_FROM), upto(c + 1 - ITEMS_FROM)) if ITEMS_FROM <= c < ITEMS_TO else range(0)


def layer1_attention(nc, ident_d, mask_d, minus_d, q_scr, k_scr, v_all, ctx_sb):
    with ExitStack() as ctx:
        def sb(name, shape, dt=F32):
            return ctx.enter_context(nc.sbuf_tensor("f_" + name, shape, dt))

        def sem(name):
            return ctx.enter_context(nc.semaphore("f_" + name))

        ident, mask, zero = sb("ident", [P, P]), sb("mask", [P, CH]), sb("zero", [P, 1])
        minus = sb("minus", [P, 2, 1])
        qst = sb("qst", [P, STACKS, 2, T], F32R)
        kst = sb("kst", [P, STACKS, 2, T], F32R)
        vst = sb("vst", [P, STACKS, QB, 2 * D])
        prob = sb("prob", [P, 2, HG, CH])
        mx = sb("mx", [P, STACKS, 2, 2, QB])
        mx_first = sb("mx_first", [P, 2, 2, QB])
        mt = sb("mt", [HG * QB, STACKS, P], F32R)
        ctxt = sb("ctxt", [P, HALF, CH])
        rden = sb("rden", [P, QPH, HG])
        bank = ctx.enter_context(nc.psum_tensor("f_bank", [P, 8, 512], F32))
        item_bank = [bank[:, 0], bank[:, 1]]
        score_bank = [bank[:, 2:4], bank[:, 4:6]]
        sum_bank = [bank[:, 6], bank[:, 7]]
        const_in, cleared = sem("const_in"), sem("cleared")
        minus_in = sem("minus_in")
        item_seen, diag_seen = sem("item_seen"), sem("diag_seen")
        qk_in = [sem(f"qk_in{u}") for u in range(STACKS)]
        m_in = [sem(f"m_in{u}") for u in range(STACKS)]
        item_ps, item_done, mx_ready, mturn_ps, mt_ready = (sem(n) for n in ("item_ps", "item_done", "mx_ready", "mturn_ps", "mt_ready"))
        st_ps, exp_done, masked, av_done, vst_ready = (sem(n) for n in ("st_ps", "exp_done", "masked", "av_done", "vst_ready"))
        ctxt_ready, cturn_ps, out_ready = sem("ctxt_ready"), sem("cturn_ps"), sem("out_ready")
        NI = len(ITEMS)
        ROUNDS = (NG - 1) // STACKS

        def span(h, k):
            return max(0, k * P - h * CH)

        def diagonal(h, k):
            return k * P >= h * CH

        DIAG = 2 * sum(diagonal(*unit) for unit in UNITS)

        def group(j, k):
            return j * STACKS + k, k % STACKS, j + k // STACKS

        def groups(eng, step, tail):
            for c in range(HEAD):
                step(c, group(0, 0), group(0, 1), None)
            with eng.Fori(0, ROUNDS) as j:
                for k in range(STACKS):
                    for c in range(HEAD, NC):
                        step(c, group(j, k), group(j, k + 1), None)
                    for c in range(HEAD):
                        step(c, group(j, k + 1), None, group(j, k))
            for c in range(HEAD, NC):
                step(c, group(ROUNDS, 0), None, None)
            tail(group(ROUNDS, 0))

        block = ctx.enter_context(nc.Block())

        @block.sync
        def _(sp):
            def load(g):
                n, u, _ = g
                for par in range(2):
                    r = slice(par * PART, par * PART + PART)
                    sp.dma_start(kst[r, u, par].bitcast(F32), k_scr[bass.ds(n, 1)].rearrange("n c d t -> (n c d) t")).then_inc(qk_in[u], 16)
                    src = q_scr[bass.ds(n * HG, HG)].rearrange("(i p) c d t -> p (c d) i t", p=2)[par]
                    sp.dma_start(qst[r, u].bitcast(F32), src).then_inc(qk_in[u], 16)

            def maxima(g):
                n, u, _ = g
                sp.wait_ge(mt_ready, n + 1)
                for par in range(2):
                    sp.dma_start(qst[M_ROW + par:M_ROW + par + 1, u].rearrange("o i (b q) -> o (i b) q", q=P).bitcast(F32),
                                 mt[par * 2 * QB:(par + 1) * 2 * QB, u].bitcast(F32)).then_inc(m_in[u], 16)

            def step(g, after, third):
                maxima(after)
                if third is not None:
                    sp.wait_ge(st_ps, g[0] * NC + NC)
                    load(third)

            sp.dma_start(minus[M_ROW:M_ROW + 2], minus_d).then_inc(minus_in, 16)
            for u in range(STACKS):
                sp.wait_ge(cleared, u + 1)
                load(group(0, u))
            maxima(group(0, 0))
            with sp.Fori(0, ROUNDS - 1) as j:
                for k in range(STACKS):
                    step(group(j, k), group(j, k + 1), group(j, k + STACKS))
            for k in range(STACKS):
                step(group(ROUNDS - 1, k), group(ROUNDS - 1, k + 1), group(ROUNDS - 1, k + STACKS) if k == 0 else None)

        @block.gpsimd
        def _(pool):
            def values(g):
                n, u, _ = g
                pool.tensor_copy(vst[:, u].rearrange("p b d -> p (b d)"),
                                 v_all[:, bass.ds(n, 1)].rearrange("p n b d -> p (n b d)")).then_inc(vst_ready, 1)

            def step(c, g, after, before):
                n = g[0]
                h, k = UNITS[c // 2]
                if diagonal(h, k):
                    pool.wait_ge(exp_done, n * NC + (c + 3))
                    pool.sem_inc(diag_seen, 1)
                    p = prob[:, c // 2 % 2, c % 2 * 2:c % 2 * 2 + 2, span(h, k):span(h, k) + P]
                    pool.affine_select(out=p, in_=p, compare_op=ALU.is_ge, fill=0.0, base=0,
                                       pattern=[[0, 2], [1, P]], channel_multiplier=-1).then_inc(masked, 1)
                if c == HEAD and after is not None:
                    pool.wait_ge(av_done, n * NU + 2)
                    values(after)
            values(group(0, 0))
            groups(pool, step, lambda g: None)

        @block.scalar
        def _(act):
            act.dma_start(ident[:, :], ident_d).then_inc(const_in, 16)
            act.dma_start(mask[:, :], mask_d).then_inc(const_in, 16)
            act.sem_inc(exp_done, 2)

            def turn(g, h):
                n = g[0]
                act.wait_ge(av_done, n * NU + (QPH if h == 0 else NU) + 2)
                act.wait_ge(cturn_ps, n * HALF + h + 1)
                act.activation(ctxt[:, h], sum_bank[h], ACT.Copy).then_inc(ctxt_ready, 1)

            def step(c, g, after, before):
                n = g[0]
                lo = span(*UNITS[c // 2])
                if c == 2 and before is not None:
                    turn(before, 1)
                if c == 2 * QPH + 2:
                    turn(g, 0)
                if c % 2 == 0:
                    act.wait_ge(av_done, n * NU + c // 2 + 1)
                act.wait_ge(st_ps, n * NC + c + 1)
                act.activation(prob[:, c // 2 % 2, c % 2 * 2:c % 2 * 2 + 2, lo:], score_bank[c % 2][:, :, lo:], ACT.Exp,
                               scale=D ** -0.5).then_inc(exp_done, 1)
            groups(act, step, lambda g: turn(g, 1))

        @block.vector
        def _(dve):
            dve.memset(zero[:, :], 0.0)
            dve.wait_ge(minus_in, 16)
            dve.drain()
            for u in range(STACKS):
                dve.tensor_copy(kst[:, u].rearrange("p a t -> p (a t)"), zero[:, :].broadcast_to([P, 2 * T]))
                dve.drain()
                dve.tensor_copy(kst[M_ROW:M_ROW + 2, u], minus[M_ROW:M_ROW + 2].broadcast_to([2, 2, T])).then_inc(cleared, 1)
            dve.sem_inc(item_done, 2)
            dve.sem_inc(out_ready, 2)
            dve.wait_ge(const_in, 32)

            def items(g, numbers):
                n, u, _ = g
                for s in numbers:
                    h, q, at, w = ITEMS[s]
                    sc = item_bank[s % 2][:, 0:w]
                    dve.wait_ge(item_ps, n * NI + s + 1)
                    if at + w == (q + 1) * P:
                        dve.sem_inc(item_seen, 1)
                        dve.tensor_tensor_reduce(sc, sc, mask[:, CH - w:CH], 1.0, LEAST, ALU.add, ALU.max,
                                                 mx[:, u, h % 2, h // 2, q:q + 1]).then_inc(item_done, 1)
                    else:
                        dve.tensor_reduce(mx_first[:, h % 2, h // 2, q:q + 1], sc, AX.X, ALU.max).then_inc(item_done, 1)

            def maxima(g):
                n, u, _ = g
                dve.drain()
                more = mx[:, u, :, :, QPH:]
                dve.tensor_tensor(more, more, mx_first[:, :, :, QPH:], ALU.max).then_inc(mx_ready, 1)
                dve.wait_ge(mturn_ps, n + 1)
                dve.tensor_copy(mt[:, u], item_bank[0][0:HG * QB, 0:P]).then_inc(mt_ready, 1)

            def normalize(g, h):
                n = g[0]
                dve.drain()
                dve.wait_ge(cturn_ps, n * HALF + h + 3)
                turned = sum_bank[h].rearrange("p (b h d) -> p b h d", h=HG, d=2 * D)
                dve.reciprocal(rden[:, :, :], turned[:, :, :, D])
                dve.drain()
                dve.tensor_tensor(ctx_sb[:, bass.ds(n, 1), h * QPH:(h + 1) * QPH].rearrange("p n b (h d) -> p (n b) h d", d=D),
                                  turned[:, :, :, 0:D], rden[:, :, :].rearrange("p b (h o) -> p b h o", o=1).broadcast_to([P, QPH, HG, D]),
                                  ALU.mult).then_inc(out_ready, 1)

            def step(c, g, after, before):
                if after is not None:
                    items(after, beside(c))
                    if c == TURN_MAXIMA:
                        maxima(after)
                if c == HEAD - 1 and before is not None:
                    normalize(before, 1)
                if c == TURN_FIRST_HALF:
                    normalize(g, 0)
            items(group(0, 0), range(NI))
            maxima(group(0, 0))
            groups(dve, step, lambda g: normalize(g, 1))

        @block.tensor
        def _(pe):
            pe.sem_inc(av_done, 2)
            pe.sem_inc(cturn_ps, 2)

            def items(g, numbers, first=False):
                n, u, turns = g
                for s in numbers:
                    h, q, at, w = ITEMS[s]
                    if s == 0:
                        pe.wait_ge(qk_in[u], turns * LOADED + LOADED)
                        if not first:
                            pe.wait_ge(mt_ready, n)
                    pe.wait_ge(item_done, n * NI + s + 1)
                    pe.matmul(item_bank[s % 2][:, 0:w], qst[0:M_ROW, u, h // 2, q * P:q * P + P],
                              kst[0:M_ROW, u, h % 2, at:at + w], start=True, stop=True).then_inc(item_ps, 1)

            def maxima(g):
                n, u, _ = g
                pe.wait_ge(mx_ready, n + 1)
                pe.transpose(item_bank[0][0:HG * QB, 0:P], mx[:, u].rearrange("p a b c -> p (a b c)"), ident[:, :]).then_inc(mturn_ps, 1)

            def scores(g, c):
                n, u, turns = g
                h, k = UNITS[c // 2]
                lo = span(h, k)
                if c == 0:
                    pe.wait_ge(m_in[u], turns * (16 * 2) + 16 * 2)
                pe.wait_ge(exp_done, n * NC + c + 1)
                for hh in range(2):
                    mm = pe.matmul(score_bank[c % 2][:, hh, lo:], kst[0:M_ROW + 2, u, hh, k * P:k * P + P],
                                   qst[0:M_ROW + 2, u, c % 2, h * CH + lo:(h + 1) * CH], start=True, stop=True)
                mm.then_inc(st_ps, 1)

            def weighed(g, i):
                n, u, _ = g
                h, k = UNITS[i]
                last = [kk for hh, kk in UNITS if hh == h][-1]
                pe.wait_ge(exp_done, n * NC + (2 * i + 4))
                if diagonal(h, k):
                    pe.wait_ge(masked, n * DIAG + 2 * sum(diagonal(*unit) for unit in UNITS[:i + 1]))
                if i == 0:
                    pe.wait_ge(vst_ready, n + 1)
                if k == 0:
                    pe.wait_ge(out_ready, n * HALF + h + 1)
                lo = span(h, k)
                for hh in range(HG):
                    mm = pe.matmul(sum_bank[h][2 * D * hh:2 * D * (hh + 1), lo:], vst[:, u, k], prob[:, i % 2, hh, lo:],
                                   start=(k == 0), stop=(k == last))
                mm.then_inc(av_done, 1)

            def turn(g, h):
                n = g[0]
                pe.wait_ge(ctxt_ready, n * HALF + h + 1)
                for b in range(QPH):
                    mm = pe.transpose(sum_bank[h][:, b * P:b * P + P], ctxt[:, h, b * P:b * P + P], ident[:, :])
                mm.then_inc(cturn_ps, 1)

            def step(c, g, after, before):
                scores(g, c)
                numbers = beside(c) if after is not None else range(0)
                if numbers:
                    items(after, numbers[:1])
                if c % 2 == 1:
                    if c > 1:
                        weighed(g, c // 2 - 1)
                    elif before is not None:
                        weighed(before, NU - 1)
                if numbers:
                    items(after, numbers[1:])
                if c == TURN_MAXIMA and after is not None:
                    maxima(after)
                if c == HEAD - 1 and before is not None:
                    turn(before, 1)
                if c == TURN_FIRST_HALF:
                    turn(g, 0)

            def tail(g):
                weighed(g, NU - 1)
                turn(g, 1)
            pe.wait_ge(const_in, 32)
            pe.wait_ge(cleared, STACKS)
            items(group(0, 0), range(NI), True)
            maxima(group(0, 0))
            groups(pe, step, tail)


def layer1_output(nc, Wo, ident_d, x1_d, ctx_sb, acc, out):
    with ExitStack() as ctx:
        def sb(name, shape, dt=F32):
            return ctx.enter_context(nc.sbuf_tensor("g_" + name, shape, dt))

        def sem(name):
            return ctx.enter_context(nc.semaphore("g_" + name))

        ident = sb("ident", [P, P])
        wn = sb("wn", [P, KT, E])
        woh, wol = sb("woh", [P, KT, E], F32R), sb("wol", [P, KT, E], F32R)
        x1 = sb("x1", [P, TILES, E])
        ct = sb("ct", [P, 2, E])
        cth, ctl = sb("cth", [P, 2, KT, P], F32R), sb("ctl", [P, 2, KT, P], F32R)
        bank = ctx.enter_context(nc.psum_tensor("g_bank", [P, 8, 512], F32))
        w_in, x_in = sem("w_in"), sem("x_in")
        w_tp, w_hi, w_lo = sem("w_tp"), sem("w_hi"), sem("w_lo")
        ct_ready, ct_tp, cth_ready, ctl_ready, proj_ps, out_ready = (
            sem(n) for n in ("ct_ready", "ct_tp", "cth_ready", "ctl_ready", "proj_ps", "out_ready"))
        read_ps = sem("read_ps")
        y_out = [sem(f"y_out{u}") for u in range(2)]
        k4 = lambda a: a.rearrange("p (k q) -> p k q", k=KT)
        outv = out.rearrange("b (t p) e -> p (b t) e", p=P)

        def tiles(eng, body):
            with eng.Fori(0, TILES // 2) as j:
                for u in range(2):
                    body(j * 2 + u, u, j)

        block = ctx.enter_context(nc.Block())

        @block.sync
        def _(sp):
            sp.dma_start(wn[:, :, :], Wo.rearrange("(o p) e -> p o e", p=P)).then_inc(w_in, 16)
            sp.dma_start(ident[:, :], ident_d).then_inc(w_in, 16)
            sp.dma_start(x1[:, :, :], x1_d.rearrange("(t p) e -> p t e", p=P)).then_inc(x_in, 16)

            def body(t, u, j):
                sp.wait_ge(out_ready, t + 1)
                sp.dma_start(outv[:, bass.ds(t, 1)].rearrange("p t e -> p (t e)"),
                             x1[:, bass.ds(t, 1)].rearrange("p t e -> p (t e)")).then_inc(y_out[u], 16)
            tiles(sp, body)
            for u in range(2):
                sp.wait_ge(y_out[u], 16 * (TILES // 2))

        @block.gpsimd
        def _(pool):
            pool.sem_inc(ct_tp, 2)
            with pool.Fori(0, B) as b:
                for qb in range(QB):
                    pool.wait_ge(ct_tp, b * QB + qb + 1)
                    pool.tensor_copy(ct[:, qb % 2].rearrange("p (g d) -> p g d", g=HKV),
                                     ctx_sb[:, bass.ds(b * HKV, HKV), qb]).then_inc(ct_ready, 1)

        @block.scalar
        def _(act):
            for o in range(KT):
                act.wait_ge(w_tp, o + 1)
                act.activation(woh[:, :, o * P:o * P + P], k4(bank[:, o % 2]), ACT.Copy).then_inc(w_hi, 1)

            def body(t, u, j):
                act.wait_ge(ct_tp, t + 3)
                act.wait_ge(proj_ps, t + 1)
                act.activation(cth[:, u], k4(bank[:, u]), ACT.Copy).then_inc(cth_ready, 1)
            tiles(act, body)

        @block.vector
        def _(dve):
            for o in range(KT):
                dve.wait_ge(w_hi, o + 1)
                dve.tensor_tensor(wol[:, :, o * P:o * P + P], k4(bank[:, o % 2]), woh[:, :, o * P:o * P + P].bitcast(F32),
                                  ALU.subtract).then_inc(w_lo, 1)
            dve.sem_inc(ctl_ready, 2)
            dve.wait_ge(x_in, 16)

            def body(t, u, j):
                dve.wait_ge(cth_ready, t + 1)
                dve.tensor_tensor(ctl[:, u], k4(bank[:, u]), cth[:, u].bitcast(F32), ALU.subtract).then_inc(ctl_ready, 1)
                dve.wait_ge(proj_ps, t + 3)
                a = flat(acc[:, bass.ds(t, 1)])
                x = flat(x1[:, bass.ds(t, 1)])
                dve.scalar_tensor_tensor(out=a, in0=bank[:, 2 + u], scalar=0.5, in1=a, op0=ALU.mult, op1=ALU.mult).then_inc(read_ps, 1)
                dve.drain()
                dve.tensor_tensor(x, x, a, ALU.add).then_inc(out_ready, 1)
            dve.sem_inc(read_ps, 2)
            tiles(dve, body)

        @block.tensor
        def _(pe):
            pe.sem_inc(proj_ps, 2)
            pe.wait_ge(w_in, 32)
            for o in range(KT):
                if o >= 2:
                    pe.wait_ge(w_lo, o - 1)
                for k in range(KT):
                    mm = pe.transpose(bank[:, o % 2, k * P:k * P + P], wn[:, o, k * P:k * P + P], ident[:, :])
                mm.then_inc(w_tp, 1)
            pe.wait_ge(w_lo, KT)

            def body(t, u, j):
                pe.wait_ge(ct_ready, t + 1)
                pe.wait_ge(ctl_ready, t + 1)
                for k in range(KT):
                    mm = pe.transpose(bank[:, u, k * P:k * P + P], ct[:, u, k * P:k * P + P], ident[:, :])
                mm.then_inc(ct_tp, 1)
                pe.wait_ge(ctl_ready, t + 3)
                pe.wait_ge(read_ps, t + 1)
                for k in range(KT):
                    mm = three(pe, bank[:, 2 + u], cth[:, u, k], ctl[:, u, k], woh[:, k], wol[:, k], k == 0, k == KT - 1)
                mm.then_inc(proj_ps, 1)
            tiles(pe, body)


def program(nc, i, out, x1=None):
    x1_d = nc.dram_tensor("x1_d", [TOKENS, E], F32).ap() if x1 is None else x1
    if x1 is None:
        layer0(nc, i["L0_attn_x"], i["L0_attn_Wq"], i["L0_attn_bq"], i["L0_attn_Wk"], i["L0_attn_bk"], i["L0_attn_Wv"],
               i["L0_attn_bv"], i["L0_ffn_gate_w"], i["L0_ffn_gate_b"], i["L0_ffn_w1"], i["L0_ffn_b1"], i["L0_ffn_w2"],
               i["L0_ffn_b2"], i["ident_d"], i["strength_d"], x1_d)
    q_scr = nc.dram_tensor("q_scr", [B * HKV * G, 3, D, T], F32).ap()
    k_scr = nc.dram_tensor("k_scr", [B * HKV, 3, D, T], F32).ap()
    s_gu_scr = nc.dram_tensor("s_gu_scr", [2 * SG, 2 * INTER], F32).ap()
    z_gu_scr = nc.dram_tensor("z_gu_scr", [SG, 2 * INTER], F32).ap()
    with nc.sbuf_tensor("acc", [P, TILES, E], F32) as acc, nc.sbuf_tensor("v_all", [P, NG, T // P, 2 * D], F32) as v_all:
        with nc.sbuf_tensor("xth1", [P, KT, TOKENS], F32R) as xth, nc.sbuf_tensor("xtl1", [P, KT, TOKENS], F32R) as xtl:
            layer1_projections(nc, i["L1_attn_Wq"], i["L1_attn_Wk"], i["L1_attn_Wv"], i["ident_d"], i["rotate_d"], i["cos_d"],
                               i["sin_d"], x1_d, q_scr, k_scr, xth, xtl, v_all)
            layer1_ffn(nc, i["L1_ffn_qweight_gu"], i["L1_ffn_qzeros_gu"], i["L1_ffn_scales_gu"], i["L1_ffn_g_idx_gu"],
                       i["L1_ffn_qweight_down"], i["L1_ffn_qzeros_down"], i["L1_ffn_scales_down"], i["L1_ffn_g_idx_down"],
                       i["shift_d"], i["lane_shift_d"], i["row_d"], s_gu_scr, z_gu_scr, xth, xtl, acc)
        with nc.sbuf_tensor("ctx_sb", [P, NG, T // P, HG * D], F32) as ctx_sb:
            layer1_attention(nc, i["ident_d"], i["mask_d"], i["minus_d"], q_scr, k_scr, v_all, ctx_sb)
            layer1_output(nc, i["L1_attn_Wo"], i["ident_d"], x1_d, ctx_sb, acc, out)


def shape_constants():
    import numpy as np

    f = np.float32
    heads_per_tile = P // D
    c = {"ident_d": np.eye(P, dtype=f)}
    position = (np.arange(P)[:, None] + P * (np.arange(TILES) % (T // P))[None, :])
    text = position >= VISION
    c["strength_d"] = np.stack([text / f((T - VISION) * E), ~text / f(VISION * E)], 1).astype(f)
    inv = (f(1.0) / (f(500000.0) ** (np.arange(0, D, 2, dtype=f) / f(D)))).astype(f)
    wavelen = (f(2 * np.pi) / inv).astype(f)
    low = np.where(wavelen > f(1024.0), inv / f(32.0), inv).astype(f)
    smooth = ((f(1024) / wavelen - f(1.0)) / f(3.0)).astype(f)
    smoothed = ((f(1) - smooth) * low / f(32) + smooth * low).astype(f)
    medium = ~(wavelen < f(1024.0)) & ~(wavelen > f(256.0))
    freqs = (np.arange(T, dtype=f)[:, None] * np.where(medium, smoothed, low).astype(f)[None]).astype(f)
    emb = np.concatenate([freqs, freqs], -1)
    c["cos_d"] = np.tile(np.cos(emb).astype(f).T, (heads_per_tile, 1))
    c["sin_d"] = np.tile(np.sin(emb).astype(f).T, (heads_per_tile, 1))
    rotate = np.zeros((P, P), f)
    for m in range(P):
        first = m % D < D // 2
        rotate[m + D // 2 if first else m - D // 2, m] = -1 if first else 1
    c["rotate_d"] = rotate
    c["shift_d"] = np.tile((np.arange(PACK) * NBITS).astype(np.uint32), (P, 1))
    c["lane_shift_d"] = (np.arange(P) % PACK * NBITS).astype(np.uint32)[:, None]
    c["row_d"] = np.stack([np.arange(2 * SD) % SG, np.arange(2 * SD) % SD], 1).astype(f)
    mask = np.zeros((P, CH), f)
    mask[:, CH - P:] = np.triu(np.full((P, P), -1e30, f), 1)
    c["mask_d"] = mask
    minus = np.zeros((2, 2, 1), f)
    minus[0, 0], minus[1, 1] = -1, -1
    c["minus_d"] = minus
    return c


def kernel(**inputs):
    import numpy as np
    import concourse.bacc as bacc
    from concourse.bass_utils import run_bass_kernel_spmd

    nc = bacc.Bacc("TRN2", target_bir_lowering=False, num_devices=1)
    arrays = {name: np.ascontiguousarray(a) for name, a in {**inputs, **shape_constants()}.items()}
    handles = {name: nc.dram_tensor(name, a.shape, mybir.dt.from_np(a.dtype), kind="ExternalInput").ap() for name, a in arrays.items()}
    out = nc.dram_tensor("out", (B, T, E), F32, kind="ExternalOutput").ap()
    program(nc, handles, out)
    r = run_bass_kernel_spmd(nc, [arrays], core_ids=[0])
    return r.results[0]["out"]
```

```python
from contextlib import ExitStack

import concourse.bass as bass
from concourse import mybir

F32 = mybir.dt.float32
F32R = mybir.dt.float32r
U32 = mybir.dt.uint32
I32 = mybir.dt.int32
ALU = mybir.AluOpType
ACT = mybir.ActivationFunctionType
AX = mybir.AxisListType

P = 128
B, T, E = 2, 1024, 512
TOKENS = B * T
TILES = TOKENS // P
CH = 512
CHUNKS = TOKENS // CH
TPC = CH // P
KT = E // P
D, H, HKV = 16, 32, 8
G = H // HKV
EXPERTS = 3
EPS = 1e-5
QKV = 3 * D * HKV + EXPERTS + 1
NB = D * HKV
VISION = int(T * 0.3)


def flat(ap):
    return ap.rearrange("p a b -> p (a b)")


def three(pe, out, wh, wl, mh, ml, first, last):
    pe.matmul(out, wh, ml, start=first, stop=False)
    pe.matmul(out, wl, mh, start=False, stop=False)
    return pe.matmul(out, wh, mh, start=False, stop=last)


def layer0(nc, x, Wq, bq, Wk, bk, Wv, bv, gate_w, gate_b, w1, b1, w2, b2, ident_d, strength_d, x1_d):
    with ExitStack() as ctx:
        def sb(name, shape, dt=F32):
            return ctx.enter_context(nc.sbuf_tensor(name, shape, dt))

        def sem(name):
            return ctx.enter_context(nc.semaphore(name))

        w1h, w1l = sb("w1h", [P, EXPERTS, KT, E], F32R), sb("w1l", [P, EXPERTS, KT, E], F32R)
        w2h, w2l = sb("w2h", [P, EXPERTS, KT, E], F32R), sb("w2l", [P, EXPERTS, KT, E], F32R)
        w3h, w3l = sb("w3h", [P, KT, QKV], F32R), sb("w3l", [P, KT, QKV], F32R)
        b2p = sb("b2p", [2, EXPERTS, E], F32R)
        ones_r = sb("ones_r", [2, P], F32R)
        b1_sb = sb("b1_sb", [P, EXPERTS, KT])
        ident = sb("ident", [P, P])
        mean_var = sb("mean_var", [P, TILES, 2])
        rstd, nmr = sb("rstd", [P, TILES]), sb("nmr", [P, TILES])
        bias_row = sb("bias_row", [P, B, QKV])
        select = sb("select", [P, B, 2, EXPERTS])

        with ExitStack() as c0:
            def sb0(name, shape, dt=F32):
                return c0.enter_context(nc.sbuf_tensor(name, shape, dt))

            WB = 3
            xall = sb0("xall", [P, B, TILES // B, E])
            wst = sb0("wst", [P, WB, KT, E])
            qst = wst[:, WB - 1]
            w3f = sb0("w3f", [P, KT, QKV])
            bst = sb0("bst", [P, E + 2 * NB])
            b2st = sb0("b2st", [1, EXPERTS, E])
            b2l = sb0("b2l", [1, EXPERTS, E], F32R)
            gws = sb0("gws", [P, (E + 1) * EXPERTS])
            gbs = sb0("gbs", [P, EXPERTS])
            x0 = sb0("x0", [P, B, E])
            stats = sb0("stats", [P, TILES, 6])
            stats0 = sb0("stats0", [P, B, 6])
            mv0 = sb0("mv0", [P, B, 2])
            rstd0, nmr0 = sb0("rstd0", [P, B]), sb0("nmr0", [P, B])
            neg_half = sb0("neg_half", [P, TILES])
            veps = sb0("veps", [P, TILES + B])
            abs_sum = sb0("abs_sum", [P, TILES])
            strength = sb0("strength", [P, 2, TILES])
            weighed = sb0("weighed", [P, 2, TILES])
            ones = sb0("ones", [P, P])
            means = sb0("means", [P, 2, B])
            ratio = sb0("ratio", [P, B])
            logits0 = sb0("logits0", [P, B, EXPERTS])
            prod0 = flat(w3f[:, :, :])[:, 0:E]
            ge = sb0("ge", [P, B, 3])
            rank = sb0("rank", [P, B, EXPERTS])
            ps = c0.enter_context(nc.psum_tensor("ps0", [P, 2, TILES], F32))

            def sem0(name):
                return c0.enter_context(nc.semaphore(name))

            x_in = [sem0(f"x_in{b}") for b in range(B)]
            w_in = [sem0(f"w_in{u}") for u in range(WB)]
            small_in, qkv_in, x0_in = sem0("small_in"), sem0("qkv_in"), sem0("x0_in")
            stats_done, rstd_done, abs_done = sem0("stats_done"), sem0("rstd_done"), sem0("abs_done")
            stats0_done, rstd0_done, xn0_done = sem0("stats0_done"), sem0("rstd0_done"), sem0("xn0_done")
            weighed_done, strength_ready = sem0("weighed_done"), sem0("strength_ready")
            lo_done = [sem0(f"lo_done{u}") for u in range(WB)]
            hi_done, consts, q_summed, b2_split, b2_in = (sem0(n) for n in ("hi_done", "consts", "q_summed", "b2_split", "b2_in"))
            block = c0.enter_context(nc.Block())
            BT = TILES // B
            POOL_LOWS, DVE_LOWS = (0, 3), (1, 2, 4, 5)

            def low_parts(eng, numbers):
                for n in numbers:
                    eng.wait_ge(hi_done, n + 1)
                    e = n // 2
                    eng.tensor_tensor((w1l, w2l)[n % 2][:, e], wst[:, n % WB], (w1h, w2h)[n % 2][:, e].bitcast(F32),
                                      ALU.subtract).then_inc(lo_done[n % WB], 1)

            @block.sync
            def _(sp):
                for b in range(B):
                    sp.dma_start(xall[:, b], x[b].rearrange("(t p) e -> p t e", p=P)).then_inc(x_in[b], 16)
                for n in range(2 * EXPERTS):
                    w, e = (w1, w2)[n % 2], n // 2
                    if n == WB - 1:
                        sp.wait_ge(q_summed, 1)
                    if n >= WB:
                        sp.wait_ge(lo_done[n % WB], n // WB)
                    sp.dma_start(wst[:, n % WB], w[e].rearrange("(k p) f -> p k f", p=P)).then_inc(w_in[n % WB], 16)
                    if n == WB - 1:
                        sp.wait_ge(b2_split, 1)
                        sp.dma_start(b2p[1:2].bitcast(F32), b2l[:, :, :].bitcast(F32)).then_inc(b2_in, 16)
                sp.wait_ge(b2_in, 16)

            @block.gpsimd
            def _(pool):
                pool.memset(ones[:, :], 1.0).then_inc(consts, 1)
                pool.memset(neg_half[:, :], -0.5)
                pool.memset(ones_r[:, :].bitcast(F32), 1.0)
                pool.memset(w3f[:, :, QKV - 1:QKV], 0.0).then_inc(consts, 1)
                pool.memset(bias_row[:, :, QKV - 1:QKV], 0.0)
                pool.drain()
                def scales(ve, half, mean, var, r, m, done):
                    pool.tensor_scalar(ve, var, EPS, None, ALU.add)
                    pool.drain()
                    pool.tensor_tensor(r, ve, half, ALU.pow)
                    pool.drain()
                    pool.tensor_tensor(m, mean, r, ALU.mult)
                    pool.drain()
                    pool.tensor_scalar(m, m, -1.0, None, ALU.mult).then_inc(done, 1)

                for b in range(B):
                    if b == 1:
                        pool.wait_ge(stats0_done, 1)
                        scales(veps[:, TILES:], neg_half[:, 0:B], mv0[:, :, 0], mv0[:, :, 1], rstd0[:, :], nmr0[:, :], rstd0_done)
                    tiles = slice(b * BT, b * BT + BT)
                    pool.wait_ge(stats_done, b + 1)
                    scales(veps[:, tiles], neg_half[:, tiles], mean_var[:, tiles, 0], mean_var[:, tiles, 1], rstd[:, tiles],
                           nmr[:, tiles], rstd_done)
                low_parts(pool, POOL_LOWS)

            @block.scalar
            def _(act):
                act.dma_start(x0[:, :, :], x[:, 0:1, :].rearrange("b o e -> o b e").broadcast_to([P, B, E])).then_inc(x0_in, 16)
                act.dma_start(ident[:, :], ident_d).then_inc(qkv_in, 16)
                act.dma_start(qst, Wq.rearrange("(k p) d h -> p k (d h)", p=P)).then_inc(qkv_in, 16)
                act.dma_start(w3f[:, :, NB:2 * NB], Wk.rearrange("(k p) d h -> p k (d h)", p=P)).then_inc(qkv_in, 16)
                act.dma_start(w3f[:, :, 2 * NB:3 * NB], Wv.rearrange("(k p) d h -> p k (d h)", p=P)).then_inc(qkv_in, 16)
                act.dma_start(w3f[:, :, 3 * NB:3 * NB + EXPERTS],
                              gate_w[0:E].rearrange("(k p) e -> p k e", p=P)).then_inc(qkv_in, 16)
                act.dma_start(gws[:, :], gate_w.rearrange("(o a) e -> o (a e)", o=1).broadcast_to([P, (E + 1) * EXPERTS])).then_inc(small_in, 16)
                act.dma_start(gbs[:, :], gate_b.rearrange("(o e) -> o e", o=1).broadcast_to([P, EXPERTS])).then_inc(small_in, 16)
                for n, v in enumerate((bq, bk, bv)):
                    at = (0, E, E + NB, E + 2 * NB)
                    act.dma_start(bst[:, at[n]:at[n + 1]],
                                   v.rearrange("(o d) h -> o (d h)", o=1).broadcast_to([P, at[n + 1] - at[n]])).then_inc(small_in, 16)
                act.dma_start(strength[:, :, :], strength_d).then_inc(small_in, 16)
                act.dma_start(b2st[:, :, :], b2.rearrange("(o e) f -> o e f", o=1)).then_inc(small_in, 16)
                act.dma_start(b1_sb[:, :, :], b1.rearrange("e (k p) -> p e k", p=P), allow_slow_non_contiguous=True).then_inc(small_in, 16)
                for n in range(2 * EXPERTS):
                    if n < B:
                        act.wait_ge(rstd_done, n + 1)
                        for t in range(BT):
                            k = n * BT + t
                            act.activation(xall[:, n, t], xall[:, n, t], ACT.Abs, bias=nmr[:, k:k + 1], scale=rstd[:, k:k + 1],
                                           accum_out=abs_sum[:, k:k + 1]).then_inc(abs_done, 1)
                    act.wait_ge(w_in[n % WB], 16 * (n // WB + 1))
                    act.activation((w1h, w2h)[n % 2][:, n // 2], wst[:, n % WB], ACT.Copy).then_inc(hi_done, 1)
                    if n == 1:
                        act.wait_ge(x0_in, 16)
                        act.wait_ge(rstd0_done, 1)
                        for b in range(B):
                            act.activation(x0[:, b], x0[:, b], ACT.Identity, bias=nmr0[:, b:b + 1],
                                           scale=rstd0[:, b:b + 1]).then_inc(xn0_done, 1)

            @block.vector
            def _(dve):
                for b in range(B):
                    if b == 1:
                        dve.wait_ge(x0_in, 16)
                        for bb in range(B):
                            dve.bn_stats(stats0[:, bb], x0[:, bb])
                        dve.drain()
                        for bb in range(B):
                            dve.bn_aggr(mv0[:, bb], stats0[:, bb])
                        dve.drain().then_inc(stats0_done, 1)
                    dve.wait_ge(x_in[b], 16)
                    for t in range(b * BT, b * BT + BT):
                        dve.bn_stats(stats[:, t], xall[:, b, t - b * BT])
                    dve.drain()
                    for t in range(b * BT, b * BT + BT):
                        dve.bn_aggr(mean_var[:, t], stats[:, t])
                    dve.drain().then_inc(stats_done, 1)
                dve.wait_ge(consts, 2)
                dve.wait_ge(qkv_in, 80)
                dve.wait_ge(small_in, 128)
                dve.tensor_reduce(w3f[:, :, 0:NB], qst.rearrange("p k (d g) -> p k d g", g=G), AX.X, ALU.add).then_inc(q_summed, 1)
                for b in range(B):
                    dve.tensor_reduce(bias_row[:, b, 0:NB], bst[:, 0:E].rearrange("p (d g) -> p d g", g=G), AX.X, ALU.add)
                    dve.tensor_copy(bias_row[:, b, NB:3 * NB], bst[:, E:])
                dve.tensor_copy(b2p[0:1], b2st[:, :, :])
                dve.drain()
                dve.tensor_copy(w3h[:, :, :], w3f[:, :, :])
                dve.tensor_tensor(b2l[:, :, :], b2st[:, :, :], b2p[0:1].bitcast(F32), ALU.subtract).then_inc(b2_split, 1)
                dve.drain()
                dve.tensor_tensor(w3l[:, :, :], w3f[:, :, :], w3h[:, :, :].bitcast(F32), ALU.subtract)
                low_parts(dve, DVE_LOWS[:2])
                dve.drain()
                dve.wait_ge(xn0_done, B)
                gview = gws[:, 0:E * EXPERTS].rearrange("p (a e) -> p e a", e=EXPERTS)
                for b in range(B):
                    for e in range(EXPERTS):
                        dve.tensor_tensor_reduce(prod0, x0[:, b], gview[:, e], 1.0, 0.0, ALU.mult, ALU.add,
                                                 logits0[:, b, e:e + 1])
                        dve.drain()
                low_parts(dve, DVE_LOWS[2:])
                dve.wait_ge(abs_done, TILES)
                for k in range(2):
                    dve.tensor_tensor(weighed[:, k], strength[:, k], abs_sum[:, :], ALU.mult)
                dve.drain().then_inc(weighed_done, 1)
                dve.wait_ge(strength_ready, 1)
                dve.tensor_reduce(means[:, :, :], ps[:, :, :].rearrange("p k (b t) -> p k b t", b=B), AX.X, ALU.add)
                dve.drain()
                dve.tensor_scalar(means[:, 1], means[:, 1], 1e-8, None, ALU.add)
                dve.drain()
                dve.reciprocal(ratio[:, :], means[:, 1])
                dve.drain()
                dve.tensor_tensor(ratio[:, :], ratio[:, :], means[:, 0], ALU.mult)
                dve.drain()
                for b in range(B):
                    dve.scalar_tensor_tensor(out=bias_row[:, b, 3 * NB:3 * NB + EXPERTS], in0=gws[:, E * EXPERTS:],
                                             scalar=ratio[:, b:b + 1], in1=gbs[:, :], op0=ALU.mult, op1=ALU.add)
                dve.drain()
                dve.tensor_tensor(logits0[:, :, :], logits0[:, :, :], bias_row[:, :, 3 * NB:3 * NB + EXPERTS], ALU.add)
                dve.drain()
                for n, (i, j) in enumerate(((0, 1), (0, 2), (1, 2))):
                    dve.tensor_tensor(ge[:, :, n:n + 1], logits0[:, :, i:i + 1], logits0[:, :, j:j + 1], ALU.is_ge)
                dve.drain()
                dve.tensor_tensor(rank[:, :, 0:1], ge[:, :, 0:1], ge[:, :, 1:2], ALU.add)
                dve.tensor_tensor(rank[:, :, 1:2], ge[:, :, 0:1], ge[:, :, 2:3], ALU.subtract)
                dve.tensor_tensor(rank[:, :, 2:3], ge[:, :, 1:2], ge[:, :, 2:3], ALU.add)
                dve.drain()
                dve.tensor_scalar(rank[:, :, 0:1], rank[:, :, 0:1], -1.0, 2.0, ALU.mult, ALU.add)
                dve.tensor_scalar(rank[:, :, 1:2], rank[:, :, 1:2], 1.0, None, ALU.add)
                dve.drain()
                for i in range(2):
                    dve.tensor_scalar(select[:, :, i], rank[:, :, :], float(i), None, ALU.is_equal)
                dve.drain()

            @block.tensor
            def _(pe):
                pe.wait_ge(consts, 1)
                pe.wait_ge(weighed_done, 1)
                pe.matmul(ps[:, :, :], ones[:, :], weighed[:, :, :], start=True, stop=True).then_inc(strength_ready, 1)

        xb = sb("xb", [P, 2, TPC, E])
        xn = sb("xn", [P, TPC, E])
        xth, xtl = sb("xth", [P, KT, CH], F32R), sb("xtl", [P, KT, CH], F32R)
        af = sb("af", [P, 2, CH])
        ah, al = sb("ah", [P, 2, CH], F32R), sb("al", [P, 2, CH], F32R)
        qkv = sb("qkv", [P, TPC, QKV])
        moe = sb("moe", [P, TPC, E])
        pa, pb = sb("pa", [P, D, D, HKV]), sb("pb", [P, D, HKV, D])
        sc, at = sb("sc", [P, D, D]), sb("at", [P, D, D])
        smax, rsum = sb("smax", [P, D]), sb("rsum", [P, D])
        so = sb("so", [P, D, HKV])
        s_sb = sb("s_sb", [P, TPC, D, HKV])
        gl, gexp = sb("gl", [P, TPC, EXPERTS]), sb("gexp", [P, TPC, EXPERTS])
        gt = sb("gt", [P, 6, TPC])
        coef, coef2 = sb("coef", [P, TPC, EXPERTS]), sb("coef2", [P, TPC, EXPERTS])
        bank = ctx.enter_context(nc.psum_tensor("bank", [P, 8, 512], F32))

        xin = [sem(f"xin{u}") for u in range(2)]
        xout = [sem(f"xout{u}") for u in range(2)]
        xn_ready, tp_ready, xth_ready, xtl_ready = sem("xn_ready"), sem("tp_ready"), sem("xth_ready"), sem("xtl_ready")
        qkv_ps, qkv_ready = sem("qkv_ps"), sem("qkv_ready")
        p1_done, redA, sc_ready, exp_done, p2_done, redB = (sem(n) for n in ("p1_done", "redA", "sc_ready", "exp_done", "p2_done", "redB"))
        gl_ready, gexp_ready = sem("gl_ready"), sem("gexp_ready")
        f1_ps, act_ready, split_ready, f2_step, f2_evac = (sem(n) for n in ("f1_ps", "act_ready", "split_ready", "f2_step", "f2_evac"))
        th_ready, th_used, x1_ready = sem("th_ready"), sem("th_used"), sem("x1_ready")
        NF = EXPERTS * KT
        x1v = x1_d.rearrange("(c t p) e -> p c t e", p=P, t=TPC)
        xv = x.rearrange("b (c t p) e -> p (b c) t e", p=P, t=TPC)

        def chunk(j, k):
            return j * 2 + k, k % 2, j + k // 2

        def chunks(eng, head, body, tail):
            head(chunk(0, 0))
            body(chunk(0, 0), None, chunk(0, 1))
            with eng.Fori(0, CHUNKS // 2 - 1) as j:
                for k in (1, 2):
                    body(chunk(j, k), chunk(j, k - 1), chunk(j, k + 1))
            body(chunk(0, CHUNKS - 1), chunk(0, CHUNKS - 2), None)
            tail(chunk(0, CHUNKS - 1))

        block = ctx.enter_context(nc.Block())

        @block.sync
        def _(sp):
            sp.sem_inc(x1_ready, 1)
            for u in range(2):
                sp.dma_start(xb[:, u], xv[:, u]).then_inc(xin[u], 16)

            def body(c, u, j):
                sp.wait_ge(x1_ready, c * TPC + 1 + TPC)
                sp.dma_start(x1v[:, bass.ds(c, 1)].rearrange("p c t e -> p (c t) e"), xb[:, u]).then_inc(xout[u], 16)
                sp.wait_ge(xout[u], j * 16 + 16)
            with sp.Fori(0, CHUNKS // 2 - 1) as j:
                for u in range(2):
                    body(j * 2 + u, u, j)
                    sp.dma_start(xb[:, u], xv[:, bass.ds(j * 2 + u + 2, 1)].rearrange("p c t e -> p (c t) e")).then_inc(xin[u], 16)
            for u in range(2):
                c = CHUNKS - 2 + u
                sp.wait_ge(x1_ready, c * TPC + 1 + TPC)
                sp.dma_start(x1v[:, c], xb[:, u]).then_inc(xout[u], 16)
                sp.wait_ge(xout[u], 16 * (CHUNKS // 2))

        @block.gpsimd
        def _(pool):
            def scores(now, t):
                c = now[0]
                pool.wait_ge(qkv_ready, c * TPC + t + 1)
                pool.wait_ge(redA, c * TPC + t + 1)
                q = qkv[:, t, 0:NB].rearrange("p (d o h) -> p d o h", o=1, h=HKV).broadcast_to([P, D, D, HKV])
                k = qkv[:, t, NB:2 * NB].rearrange("p (o e h) -> p o e h", o=1, h=HKV).broadcast_to([P, D, D, HKV])
                pool.tensor_tensor(pa[:, :, :, :], q, k, ALU.mult).then_inc(p1_done, 1)

            def body(now, before, after):
                c = now[0]
                scores(now, 0)
                for t in range(TPC):
                    if t + 1 < TPC:
                        scores(now, t + 1)
                    pool.wait_ge(exp_done, c * TPC + t + 1)
                    pool.wait_ge(redB, c * TPC + t + 1)
                    a = at[:, :, :].rearrange("p d (o e) -> p d o e", o=1).broadcast_to([P, D, HKV, D])
                    v = qkv[:, t, 2 * NB:3 * NB].rearrange("p (o e h) -> p o h e", o=1, h=HKV).broadcast_to([P, D, HKV, D])
                    pool.tensor_tensor(pb[:, :, :, :], a, v, ALU.mult).then_inc(p2_done, 1)
            chunks(pool, lambda now: None, body, lambda now: None)

        @block.scalar
        def _(act):
            act.sem_inc(p2_done, 1)

            def normalize(now, t):
                c, u, turns = now
                if t == 0:
                    act.wait_ge(xin[u], turns * 16 + 16)
                    act.wait_ge(tp_ready, c * TPC + 1)
                act.activation(xn[:, t], xb[:, u, t], ACT.Identity, bias=nmr[:, bass.ds(c * TPC + t, 1)],
                               scale=rstd[:, bass.ds(c * TPC + t, 1)]).then_inc(xn_ready, 1)

            def high_parts(now):
                c = now[0]
                act.wait_ge(f1_ps, c * NF + 1)
                for t in range(TPC):
                    act.wait_ge(tp_ready, c * TPC + t + 2)
                    act.activation(xth[:, :, t * P:t * P + P], bank[:, t % 2].rearrange("p (k q) -> p k q", k=KT),
                                   ACT.Copy).then_inc(xth_ready, 1)

            def gate_tanh(now, t):
                c = now[0]
                act.wait_ge(f2_evac, (c * EXPERTS + 2) * TPC + t + 2)
                act.wait_ge(th_used, c * TPC + t + 1)
                act.activation(bank[:, t % 2], moe[:, t], ACT.Tanh, scale=0.5).then_inc(th_ready, 1)

            def head(now):
                for t in range(TPC):
                    normalize(now, t)
                high_parts(now)

            def body(now, before, after):
                c = now[0]
                act.wait_ge(gl_ready, c + 1)
                act.activation(gexp[:, :, :], gl[:, :, :], ACT.Exp).then_inc(gexp_ready, 1)
                for e in range(EXPERTS):
                    f = (ACT.Tanh, ACT.Gelu, ACT.Silu)[e]
                    for n in range(KT):
                        m = e * KT + n
                        act.wait_ge(f1_ps, c * NF + m + 2)
                        act.wait_ge(f2_step, c * NF + m + 1)
                        act.activation(af[:, m % 2], bank[:, 2 + m % 2], f, bias=b1_sb[:, e, n:n + 1])
                        act.activation(ah[:, m % 2], bank[:, 2 + m % 2], f, bias=b1_sb[:, e, n:n + 1]).then_inc(act_ready, 1)
                        if before is not None and m < TPC:
                            gate_tanh(before, m)
                        if m % 3 == 1:
                            t = m // 3
                            act.wait_ge(sc_ready, c * TPC + t + 1)
                            act.wait_ge(p2_done, c * TPC + t + 1)
                            act.activation(at[:, :, :], sc[:, :, :], ACT.Exp, scale=D ** -0.5).then_inc(exp_done, 1)
                        if after is not None and m >= NF - TPC:
                            normalize(after, m - (NF - TPC))
                if after is not None:
                    high_parts(after)

            def tail(now):
                for t in range(TPC):
                    gate_tanh(now, t)
            chunks(act, head, body, tail)

        @block.vector
        def _(dve):
            dve.sem_inc(redA, 1)
            dve.sem_inc(redB, 1)
            dve.sem_inc(f2_evac, 1)
            dve.sem_inc(th_used, 2)
            dve.sem_inc(split_ready, 1)

            def low_part(now, t):
                c = now[0]
                dve.wait_ge(xth_ready, c * TPC + t + 1)
                dve.tensor_tensor(xtl[:, :, t * P:t * P + P], bank[:, t % 2].rearrange("p (k q) -> p k q", k=KT),
                                  xth[:, :, t * P:t * P + P].bitcast(F32), ALU.subtract).then_inc(xtl_ready, 1)

            def scores(c, t):
                dve.wait_ge(p1_done, c * TPC + t + 1)
                dve.tensor_reduce(sc[:, :, :], pa[:, :, :, :], AX.X, ALU.add).then_inc(redA, 1)
                dve.drain()
                dve.tensor_reduce(smax[:, :], sc[:, :, :], AX.X, ALU.max)
                dve.drain()
                dve.tensor_tensor(sc[:, :, :], sc[:, :, :], smax[:, :].rearrange("p (d o) -> p d o", o=1).broadcast_to([P, D, D]),
                                  ALU.subtract).then_inc(sc_ready, 1)

            def sums(c, t):
                dve.wait_ge(exp_done, c * TPC + t + 1)
                dve.tensor_reduce(rsum[:, :], at[:, :, :], AX.X, ALU.add)
                dve.drain()
                dve.reciprocal(rsum[:, :], rsum[:, :])

            def mix(c, t):
                dve.wait_ge(p2_done, c * TPC + t + 2)
                dve.tensor_reduce(so[:, :, :], pb[:, :, :, :], AX.X, ALU.add).then_inc(redB, 1)
                dve.drain()
                dve.scalar_tensor_tensor(out=s_sb[:, t], in0=so[:, :, :], scalar=0.5,
                                         in1=rsum[:, :].rearrange("p (d o) -> p d o", o=1).broadcast_to([P, D, HKV]),
                                         op0=ALU.mult, op1=ALU.mult)

            def gate(now):
                c, _, b = now
                lg = qkv[:, :, 3 * NB:3 * NB + EXPERTS]
                dve.tensor_reduce(gt[:, 0], lg, AX.X, ALU.max)
                dve.drain()
                dve.tensor_tensor(gl[:, :, :], lg, gt[:, 0].rearrange("p (t o) -> p t o", o=1).broadcast_to([P, TPC, EXPERTS]),
                                  ALU.subtract).then_inc(gl_ready, 1)
                dve.wait_ge(gexp_ready, c + 1)
                dve.tensor_reduce(gt[:, 0], gexp[:, :, :], AX.X, ALU.add)
                dve.tensor_tensor(gt[:, 1], gexp[:, :, 0], gexp[:, :, 1], ALU.max)
                dve.tensor_tensor(gt[:, 2], gexp[:, :, 0], gexp[:, :, 1], ALU.min)
                dve.drain()
                dve.tensor_tensor(gt[:, 3], gt[:, 1], gexp[:, :, 2], ALU.min)
                dve.tensor_tensor(gt[:, 4], gt[:, 1], gexp[:, :, 2], ALU.max)
                dve.drain()
                dve.tensor_tensor(gt[:, 5], gt[:, 3], gt[:, 2], ALU.max)
                dve.drain()
                dve.scalar_tensor_tensor(out=gt[:, 0], in0=gt[:, 0], scalar=1e-8, in1=gt[:, 4], op0=ALU.mult, op1=ALU.add)
                dve.drain()
                dve.tensor_tensor(gt[:, 0], gt[:, 0], gt[:, 5], ALU.add)
                dve.drain()
                dve.reciprocal(gt[:, 1], gt[:, 0])
                dve.drain()
                dve.tensor_tensor(gt[:, 4], gt[:, 4], gt[:, 1], ALU.mult)
                dve.tensor_tensor(gt[:, 5], gt[:, 5], gt[:, 1], ALU.mult)
                dve.drain()
                for i, dst in enumerate((coef, coef2)):
                    val = gt[:, 4 + i].rearrange("p (t o) -> p t o", o=1).broadcast_to([P, TPC, EXPERTS])
                    chosen = flat(select[:, bass.ds(b, 1), i, :]).rearrange("p (o e) -> p o e", o=1).broadcast_to([P, TPC, EXPERTS])
                    dve.tensor_tensor(dst[:, :, :], val, chosen, ALU.mult)
                dve.drain()
                dve.tensor_tensor(coef[:, :, :], coef[:, :, :], coef2[:, :, :], ALU.add)
                dve.drain()

            def gather(c, e):
                for t in range(TPC):
                    dve.wait_ge(f2_step, c * NF + (e + 1) * KT + 3)
                    if e == 0:
                        dve.tensor_scalar(moe[:, t], bank[:, 4 + t], coef[:, t, 0:1], None, ALU.mult).then_inc(f2_evac, 1)
                    else:
                        dve.scalar_tensor_tensor(out=moe[:, t], in0=bank[:, 4 + t], scalar=coef[:, t, e:e + 1],
                                                 in1=moe[:, t], op0=ALU.mult, op1=ALU.add).then_inc(f2_evac, 1)

            def finish(now, t):
                c, u, _ = now
                dve.wait_ge(th_ready, c * TPC + t + 1)
                dve.scalar_tensor_tensor(out=moe[:, t], in0=bank[:, t % 2], scalar=1.0, in1=moe[:, t],
                                         op0=ALU.add, op1=ALU.mult).then_inc(th_used, 1)
                dve.drain()
                m4 = moe[:, t].rearrange("p (a g) -> p a g", g=G)
                s4 = s_sb[:, t].rearrange("p d (h o) -> p (d h) o", o=1).broadcast_to([P, NB, G])
                dve.tensor_tensor(m4, m4, s4, ALU.mult)
                dve.drain()
                dve.tensor_tensor(xb[:, u, t], xb[:, u, t], moe[:, t], ALU.add).then_inc(x1_ready, 1)

            def head(now):
                for t in range(TPC):
                    low_part(now, t)

            def body(now, before, after):
                c, u, b = now
                for t in range(TPC):
                    dve.wait_ge(qkv_ps, c * TPC + t + 2)
                    dve.tensor_tensor(qkv[:, t], bank[:, t % 2, 0:QKV], flat(bias_row[:, bass.ds(b, 1), :]),
                                      ALU.add).then_inc(qkv_ready, 1)
                dve.drain()
                gate(now)
                for m in range(NF):
                    e, t = m // KT, m // 3
                    dve.wait_ge(act_ready, c * NF + m + 1)
                    dve.tensor_tensor(al[:, m % 2], af[:, m % 2], ah[:, m % 2].bitcast(F32), ALU.subtract).then_inc(split_ready, 1)
                    if m % KT == 0 and e > 0:
                        gather(c, e - 1)
                    if m < TPC and before is not None:
                        finish(before, m)
                    if m == NF - 1 and after is not None:
                        low_part(after, 0)
                        low_part(after, 1)
                    (scores, sums, mix)[m % 3](c, t)
                if after is not None:
                    low_part(after, 2)
                    low_part(after, 3)
                gather(c, EXPERTS - 1)

            def tail(now):
                for t in range(TPC):
                    finish(now, t)
            chunks(dve, head, body, tail)

        @block.tensor
        def _(pe):
            pe.sem_inc(tp_ready, 1)
            pe.sem_inc(qkv_ps, 1)
            pe.sem_inc(f1_ps, 1)
            pe.sem_inc(f2_step, 3)

            def turn(now, tiles):
                c = now[0]
                for t in tiles:
                    pe.wait_ge(xn_ready, c * TPC + t + 1)
                    if t >= 2:
                        pe.wait_ge(xtl_ready, c * TPC + t - 1)
                    for k in range(KT):
                        mm = pe.transpose(bank[:, t % 2, k * P:k * P + P], xn[:, t, k * P:k * P + P], ident[:, :])
                    mm.then_inc(tp_ready, 1)

            def project(now):
                c = now[0]
                for t in range(TPC):
                    if t == 0:
                        pe.wait_ge(xtl_ready, c * TPC + TPC)
                    if t >= 2:
                        pe.wait_ge(qkv_ready, c * TPC + t - 1)
                    for k in range(KT):
                        mm = three(pe, bank[:, t % 2, 0:QKV], xth[:, k, t * P:t * P + P], xtl[:, k, t * P:t * P + P],
                                   w3h[:, k], w3l[:, k], k == 0, k == KT - 1)
                    mm.then_inc(qkv_ps, 1)

            def first_product(c, m):
                e, n = m // KT, m % KT
                if m >= 2:
                    pe.wait_ge(act_ready, c * NF + m - 1)
                for k in range(KT):
                    mm = three(pe, bank[:, 2 + m % 2], w1h[:, e, k, n * P:n * P + P], w1l[:, e, k, n * P:n * P + P],
                               xth[:, k], xtl[:, k], k == 0, k == KT - 1)
                mm.then_inc(f1_ps, 1)

            def second_product(c, m):
                e, n = m // KT, m % KT
                pe.wait_ge(split_ready, c * NF + m + 2)
                if n == 0:
                    pe.wait_ge(f2_evac, (c * EXPERTS + e) * TPC + 1)
                for t in range(TPC):
                    out = bank[:, 4 + t]
                    if n == 0:
                        pe.matmul(out, ones_r[:, :], b2p[:, e], start=True, stop=False)
                    mm = three(pe, out, ah[:, m % 2, t * P:t * P + P], al[:, m % 2, t * P:t * P + P], w2h[:, e, n], w2l[:, e, n],
                               False, n == KT - 1)
                mm.then_inc(f2_step, 1)

            def body(now, before, after):
                c = now[0]
                project(now)
                for m in range(NF):
                    first_product(c, m)
                    if m == NF - 1 and after is not None:
                        pe.wait_ge(th_used, c * TPC + 2)
                        turn(after, (0, 1))
                    if m >= 1:
                        second_product(c, m - 1)
                if after is not None:
                    turn(after, (2, 3))
                second_product(c, NF - 1)
            chunks(pe, lambda now: turn(now, range(TPC)), body, lambda now: None)


INTER = 1376
SG, SD = 4, 10
FT = (INTER + P - 1) // P
FW = [min(P, INTER - n * P) for n in range(FT)]
STEPS = [list(range(n, min(n + 2, FT))) for n in range(0, FT, 2)]
QKT = 2 * NB + E
NG = B * HKV
NBITS, PACK = 4, 8


def layer1_projections(nc, Wq, Wk, Wv, ident_d, rotate_d, cos_d, sin_d, x1_d, q_scr, k_scr, xth, xtl, v_all,
                       qz_gu, sc_gu, gi_gu, qz_d, sc_d, gi_d, shift_d, lane_shift_d, row_d, s_gu_scr, z_gu_scr, gi_scr,
                       hot_gu, hot_d, sd, zd, lane_shift, lent):
    with ExitStack() as ctx:
        def sb(name, shape, dt=F32):
            return ctx.enter_context(nc.sbuf_tensor("c_" + name, shape, dt))

        def sem(name):
            return ctx.enter_context(nc.semaphore("c_" + name))

        OT = QKT // P
        ROT = OT - 1
        ident, rotate = sb("ident", [P, P]), sb("rotate", [P, P])
        cos, sin = sb("cos", [P, T]), sb("sin", [P, T])
        wn = lent[:, 0:OT]
        SF, ZR, ZC = SG * 2 * INTER // P, SG * 2 * INTER // P, P // PACK
        sg, sgh, sgl = sb("sg", [P, SF]), sb("sgh", [P, SF], F32R), sb("sgl", [P, SF], F32R)
        zg, zu, zf = sb("zg", [ZR, ZC], U32), sb("zu", [ZR, ZC, PACK], U32), sb("zf", [ZR, ZC * PACK])
        zdp, zdu = sb("zdp", [SD, E // PACK], U32), sb("zdu", [SD, E // PACK, PACK], U32)
        sdn, sdl = lent[0:SD, OT], sb("sdl", [SD, E], F32R)
        shift, row = sb("shift", [P, PACK], U32), sb("row", [2 * SD, 2])
        IG, IR, IC = E // P, ZR, INTER // ZR
        idx, idf, neg = sb("idx", [P, IG + IC], I32), sb("idf", [P, IG + IC]), sb("neg", [P, IG + IC])
        idb = lent[0:2 * SD, OT + 1:OT + 5].rearrange("p a b -> p (a b)")[:, 0:E + INTER]
        wth, wtl = sb("wth", [P, KT, QKT], F32R), sb("wtl", [P, KT, QKT], F32R)
        xb, xn = sb("xb", [P, 2, TPC, E]), sb("xn", [P, TPC, E])
        stats, mv = sb("stats", [P, TPC, 6]), sb("mv", [P, TPC, 2])
        neg_half, veps = sb("neg_half", [P, TPC]), sb("veps", [P, TPC])
        rstd, nmr = sb("rstd", [P, TPC]), sb("nmr", [P, TPC])
        qf, qc, qs = sb("qf", [P, 2, CH]), sb("qc", [P, 2, CH]), sb("qs", [P, 2, CH])
        qh, ql = sb("qh", [P, 2, CH], F32R), sb("ql", [P, 2, CH], F32R)
        bank = ctx.enter_context(nc.psum_tensor("c_bank", [P, 8, 512], F32))
        w_in, ident_in, table_in = sem("w_in"), sem("ident_in"), sem("table_in")
        s_in, s_made, s_out, idb_in = sem("s_in"), sem("s_made"), sem("s_out"), sem("idb_in")
        xin = [sem(f"xin{u}") for u in range(2)]
        q_out = [sem(f"q_out{u}") for u in range(2)]
        w_tp, w_hi, w_lo = sem("w_tp"), sem("w_hi"), sem("w_lo")
        stats_done, stats_seen, rstd_done, xn_ready = sem("stats_done"), sem("stats_seen"), sem("rstd_done"), sem("xn_ready")
        tp_ready, xth_ready, xtl_ready = sem("tp_ready"), sem("xth_ready"), sem("xtl_ready")
        proj_ps, qf_ready, rot_ps, qc_ready, rope_ready = (sem(n) for n in ("proj_ps", "qf_ready", "rot_ps", "qc_ready", "rope_ready"))
        qh_ready, ql_ready, q_free, v_tp, v_ready = (sem(n) for n in ("qh_ready", "ql_ready", "q_free", "v_tp", "v_ready"))
        x1v = x1_d.rearrange("(c t p) e -> p c t e", p=P, t=TPC)

        def before(c, m, n):
            return c * n + 2 + max(0, m - 1)

        def chunks(eng, head, body):
            chunk = lambda j, k: (j * 2 + k, k % 2, j + k // 2)
            head(chunk(0, 0))
            with eng.Fori(0, CHUNKS // 2 - 1) as j:
                for k in range(2):
                    body(chunk(j, k), chunk(j, k + 1))
            body(chunk(0, CHUNKS - 2), chunk(0, CHUNKS - 1))
            body(chunk(0, CHUNKS - 1), None)

        block = ctx.enter_context(nc.Block())

        @block.sync
        def _(sp):
            sp.sem_inc(q_free, 2)
            sp.dma_start(wn[:, 0:KT], Wq.rearrange("(o p) e -> p o e", p=P)).then_inc(w_in, 16)
            sp.dma_start(wn[:, KT], Wk).then_inc(w_in, 16)
            sp.dma_start(wn[:, KT + 1], Wv).then_inc(w_in, 16)
            sp.wait_ge(w_in, 48)
            for u in range(2):
                sp.dma_start(xb[:, u], x1v[:, u]).then_inc(xin[u], 16)

            sp.wait_ge(s_made, 1)
            sp.dma_start(gi_scr[0:E].rearrange("(p c) -> p c", p=P), idf[:, 0:IG]).then_inc(s_out, 16)
            sp.dma_start(gi_scr[E:].rearrange("(p c) -> p c", p=IR), idf[0:IR, IG:]).then_inc(s_out, 16)
            sp.wait_ge(s_out, 32)
            sp.dma_start(idb, gi_scr.rearrange("(o k) -> o k", o=1).broadcast_to([2 * SD, E + INTER])).then_inc(idb_in, 16)
            spread = lambda a, n: a.rearrange("g f -> (g f)").rearrange("(p c) -> p c", p=n)
            sp.dma_start(spread(s_gu_scr[0:SG], P), sgh[:, :].bitcast(F32)).then_inc(s_out, 16)
            sp.dma_start(spread(s_gu_scr[SG:], P), sgl[:, :].bitcast(F32)).then_inc(s_out, 16)
            sp.dma_start(spread(z_gu_scr, ZR), zf[:, :]).then_inc(s_out, 16)
            sp.dma_start(sd[SD:].bitcast(F32), sdl[:, :].bitcast(F32)).then_inc(s_out, 16)
            sp.wait_ge(s_out, 96)

            def store(c, u, b):
                for m in range(ROT):
                    sp.wait_ge(ql_ready, c * ROT + m + 1)
                    heads = P // D
                    if m < ROT - 1:
                        dst, parts = q_scr[bass.ds(b * (HKV * G) + m * heads, heads)], (qh, ql, qh)
                    else:
                        dst, parts = k_scr[bass.ds(b * HKV, HKV)], (qh, qh, ql)
                    for n, part in enumerate(parts):
                        sp.dma_start(dst[:, n, :, u * CH:u * CH + CH], part[:, m % 2].bitcast(F32)).then_inc(q_out[m % 2], 16)
                    for k in ([m - 1] if m else []) + ([m] if m == ROT - 1 else []):
                        each = (ROT + 1 - k % 2) // 2
                        sp.wait_ge(q_out[k % 2], (c * each + k // 2 + 1) * 48)
                        sp.sem_inc(q_free, 1)

            def reload(c, u):
                sp.wait_ge(xn_ready, c * TPC + TPC)
                sp.dma_start(xb[:, u], x1v[:, bass.ds(c + 2, 1)].rearrange("p c t e -> p (c t) e")).then_inc(xin[u], 16)

            with sp.Fori(0, CHUNKS // 2 - 1) as b:
                for u in range(2):
                    reload(b * 2 + u, u)
                    store(b * 2 + u, u, b)
            for u in range(2):
                store(CHUNKS - 2 + u, u, CHUNKS // 2 - 1)

        @block.gpsimd
        def _(pool):
            pool.sem_inc(qc_ready, 2)
            pool.memset(v_all[:, :, :, D:], 0.0)
            pool.memset(neg_half[:, :], -0.5)
            pool.drain()
            pool.memset(v_all[:, :, :, D:D + 1], 1.0)
            pool.drain()

            def scales(now):
                c = now[0]
                pool.wait_ge(stats_done, c + 1)
                pool.sem_inc(stats_seen, 1)
                pool.tensor_scalar(veps[:, :], mv[:, :, 1], EPS, None, ALU.add)
                pool.drain()
                pool.wait_ge(tp_ready, c * TPC + 1)
                pool.tensor_tensor(rstd[:, :], veps[:, :], neg_half[:, :], ALU.pow)
                pool.drain()
                pool.tensor_tensor(nmr[:, :], mv[:, :, 0], rstd[:, :], ALU.mult)
                pool.drain()
                pool.tensor_scalar(nmr[:, :], nmr[:, :], -1.0, None, ALU.mult).then_inc(rstd_done, 1)

            def body(now, after):
                c, u, b = now
                pool.wait_ge(table_in, 32)
                for m in range(ROT):
                    pool.wait_ge(qf_ready, c * OT + m + 3)
                    pool.wait_ge(rope_ready, before(c, m, ROT))
                    pool.tensor_tensor(qc[:, m % 2], qf[:, m % 2], cos[:, u * CH:u * CH + CH], ALU.mult).then_inc(qc_ready, 1)
                    if m == 1 and after is not None:
                        scales(after)
            chunks(pool, scales, body)

        @block.scalar
        def _(act):
            act.dma_start(ident[:, :], ident_d).then_inc(ident_in, 16)
            act.dma_start(rotate[:, :], rotate_d).then_inc(ident_in, 16)
            sp_in = lambda out, a: act.dma_start(out, a).then_inc(s_in, 16)
            flat_gu = lambda a, n: a.rearrange("g f -> (g f)").rearrange("(p c) -> p c", p=n)
            sp_in(sg[:, :], flat_gu(sc_gu, P))
            sp_in(zg[:, :], flat_gu(qz_gu, ZR))
            sp_in(sdn, sc_d)
            sp_in(zdp[:, :], qz_d)
            sp_in(shift[:, :], shift_d)
            sp_in(row[:, :], row_d)
            sp_in(lane_shift[:, :], lane_shift_d)
            sp_in(idx[:, 0:IG], gi_gu.rearrange("(p c) -> p c", p=P))
            sp_in(idx[0:IR, IG:], gi_d.rearrange("(p c) -> p c", p=IR))
            act.sem_inc(qf_ready, 2)
            act.wait_ge(w_in, 48)
            act.dma_start(cos[:, :], cos_d).then_inc(table_in, 16)
            act.dma_start(sin[:, :], sin_d).then_inc(table_in, 16)
            for o in range(OT):
                act.wait_ge(w_tp, o + 1)
                act.activation(wth[:, :, o * P:o * P + P], bank[:, o % 2].rearrange("p (k q) -> p k q", k=KT),
                               ACT.Copy).then_inc(w_hi, 1)

            def normalize(now, tiles):
                c, u, b = now
                act.wait_ge(xin[u], b * 16 + 16)
                act.wait_ge(rstd_done, c + 1)
                act.wait_ge(tp_ready, c * TPC + 1)
                for t in tiles:
                    act.activation(xn[:, t], xb[:, u, t], ACT.Identity, bias=nmr[:, t:t + 1],
                                   scale=rstd[:, t:t + 1]).then_inc(xn_ready, 1)

            def high_parts(now, tiles):
                c = now[0]
                for t in tiles:
                    act.wait_ge(tp_ready, c * TPC + t + 2)
                    act.activation(xth[:, :, bass.ds((c * TPC + t) * P, P)], bank[:, t % 2].rearrange("p (k q) -> p k q", k=KT),
                                   ACT.Copy).then_inc(xth_ready, 1)

            def head(now):
                normalize(now, range(TPC))
                high_parts(now, range(TPC))

            def body(now, after):
                c, u, b = now
                for m in range(OT):
                    act.wait_ge(proj_ps, c * OT + m + 1)
                    if m == 1:
                        act.wait_ge(v_tp, c + 1)
                    else:
                        act.wait_ge(qc_ready, c * ROT + 2 + max(0, m - 1))
                        act.wait_ge(rot_ps, c * ROT + 2 + max(0, m - 1))
                    act.activation(qf[:, m % 2], bank[:, 2 + m % 2], ACT.Copy).then_inc(qf_ready, 1)
                    if m >= 1:
                        k = m - 1
                        act.wait_ge(rope_ready, c * ROT + k + 3)
                        act.wait_ge(q_free, before(c, k, ROT))
                        act.activation(qh[:, k % 2], qs[:, k % 2], ACT.Copy).then_inc(qh_ready, 1)
                    if m in (OT - 4, OT - 3) and after is not None:
                        normalize(after, (0, 1) if m == OT - 4 else (2, 3))
                    if m in (OT - 2, OT - 1) and after is not None:
                        high_parts(after, (0, 1) if m == OT - 2 else (2, 3))
            chunks(act, head, body)

        @block.vector
        def _(dve):
            dve.sem_inc(rope_ready, 2)
            dve.sem_inc(v_ready, 1)
            for o in range(OT):
                dve.wait_ge(w_hi, o + 1)
                dve.tensor_tensor(wtl[:, :, o * P:o * P + P], bank[:, o % 2].rearrange("p (k q) -> p k q", k=KT),
                                  wth[:, :, o * P:o * P + P].bitcast(F32), ALU.subtract).then_inc(w_lo, 1)

            def statistics(now):
                c, u, b = now
                dve.wait_ge(xin[u], b * 16 + 16)
                dve.wait_ge(tp_ready, c * TPC + 1)
                for t in range(TPC):
                    dve.bn_stats(stats[:, t], xb[:, u, t])
                dve.drain()
                for t in range(TPC):
                    dve.bn_aggr(mv[:, t], stats[:, t])
                dve.drain().then_inc(stats_done, 1)

            def small_arrays():
                dve.wait_ge(s_in, 9 * 16)
                dve.tensor_copy(idf[:, 0:IG], idx[:, 0:IG])
                dve.tensor_copy(idf[0:IR, IG:], idx[0:IR, IG:])
                dve.tensor_copy(sgh[:, :], sg[:, :])
                dve.tensor_copy(sd[0:SD], sdn)
                for packed, out, rows in ((zg, zu, ZR), (zdp, zdu, SD)):
                    n = packed.shape[1]
                    dve.tensor_tensor(out[:, :, :], packed[:, :].rearrange("p (c o) -> p c o", o=1).broadcast_to([rows, n, PACK]),
                                      shift[0:rows, :].rearrange("p (o i) -> p o i", o=1).broadcast_to([rows, n, PACK]),
                                      ALU.logical_shift_right)
                dve.drain()
                dve.tensor_tensor(sgl[:, :], sg[:, :], sgh[:, :].bitcast(F32), ALU.subtract)
                dve.tensor_tensor(sdl[:, :], sdn, sd[0:SD].bitcast(F32), ALU.subtract)
                for out in (zu, zdu):
                    dve.tensor_scalar(out[:, :, :], out[:, :, :], 15, None, ALU.bitwise_and)
                groups = ((slice(0, P), slice(0, IG), SG), (slice(0, IR), slice(IG, IG + IC), SD))
                for rows, at, n in groups:
                    dve.tensor_scalar(neg[rows, at], idf[rows, at], 0.0, float(n), ALU.is_lt, ALU.mult)
                dve.drain()
                dve.tensor_scalar(zf[:, :], zu[:, :, :].rearrange("p c i -> p (c i)"), 1.0, None, ALU.add)
                dve.tensor_scalar(zd[:, :], zdu[:, :, :].rearrange("p c i -> p (c i)"), 1.0, None, ALU.add)
                for rows, at, n in groups:
                    dve.tensor_tensor(idf[rows, at], idf[rows, at], neg[rows, at], ALU.add)
                dve.drain()
                for rows, at, n in groups:
                    dve.tensor_scalar(idf[rows, at], idf[rows, at], 0.0, float(n - 1), ALU.max, ALU.min)
                dve.drain().then_inc(s_made, 1)

            def low_parts(now, tiles):
                c = now[0]
                for t in tiles:
                    dve.wait_ge(xth_ready, c * TPC + t + 1)
                    at = bass.ds((c * TPC + t) * P, P)
                    dve.tensor_tensor(xtl[:, :, at], bank[:, t % 2].rearrange("p (k q) -> p k q", k=KT),
                                      xth[:, :, at].bitcast(F32), ALU.subtract).then_inc(xtl_ready, 1)

            def head(now):
                statistics(now)
                small_arrays()
                low_parts(now, range(TPC))
                dve.wait_ge(table_in, 32)

            def body(now, after):
                c, u, b = now
                for m in range(ROT):
                    dve.wait_ge(rot_ps, c * ROT + m + 3)
                    dve.tensor_tensor(qs[:, m % 2], bank[:, 4 + m % 2], sin[:, u * CH:u * CH + CH], ALU.mult)
                    dve.drain()
                    dve.wait_ge(qc_ready, c * ROT + m + 3)
                    dve.tensor_tensor(qs[:, m % 2], qs[:, m % 2], qc[:, m % 2], ALU.add).then_inc(rope_ready, 1)
                    dve.wait_ge(qh_ready, c * ROT + m + 1)
                    dve.tensor_tensor(ql[:, m % 2], qs[:, m % 2], qh[:, m % 2].bitcast(F32), ALU.subtract).then_inc(ql_ready, 1)
                    if m == 0 and after is not None:
                        statistics(after)
                    if m in (ROT - 2, ROT - 1) and after is not None:
                        low_parts(after, (0, 1) if m == ROT - 2 else (2, 3))
                dve.wait_ge(v_tp, c + 2)
                for t in range(TPC):
                    last = dve.tensor_copy(v_all[:, bass.ds(b * HKV, HKV), u * TPC + t, 0:D],
                                           bank[:, 6, t * P:t * P + P].rearrange("p (g d) -> p g d", d=D))
                last.then_inc(v_ready, 1)
            chunks(dve, head, body)
            dve.wait_ge(idb_in, 16)
            dve.tensor_scalar(hot_gu[:, :], idb[0:2 * SG, 0:E], row[0:2 * SG, 0:1], None, ALU.is_equal)
            dve.tensor_scalar(hot_d[:, :], idb[:, E:], row[:, 1:2], None, ALU.is_equal)

        @block.tensor
        def _(pe):
            pe.sem_inc(tp_ready, 1)
            pe.sem_inc(rot_ps, 2)
            pe.sem_inc(v_tp, 1)
            pe.wait_ge(w_in, 48)
            pe.wait_ge(ident_in, 32)
            for o in range(OT):
                if o >= 2:
                    pe.wait_ge(w_lo, o - 1)
                for k in range(KT):
                    mm = pe.transpose(bank[:, o % 2, k * P:k * P + P], wn[:, o, k * P:k * P + P], ident[:, :])
                mm.then_inc(w_tp, 1)
            pe.wait_ge(w_lo, OT)

            def turn(now, tiles):
                c = now[0]
                for t in tiles:
                    pe.wait_ge(xn_ready, c * TPC + t + 1)
                    if t >= 2:
                        pe.wait_ge(xtl_ready, c * TPC + t - 1)
                    for k in range(KT):
                        mm = pe.transpose(bank[:, t % 2, k * P:k * P + P], xn[:, t, k * P:k * P + P], ident[:, :])
                    mm.then_inc(tp_ready, 1)

            def body(now, after):
                c, u, b = now
                pe.wait_ge(xtl_ready, c * TPC + TPC)
                tokens = bass.ds(c * CH, CH)
                for m in range(OT + 1):
                    if m < OT:
                        pe.wait_ge(qf_ready, before(c, m, OT))
                        for k in range(KT):
                            mm = three(pe, bank[:, 2 + m % 2], wth[:, k, m * P:m * P + P], wtl[:, k, m * P:m * P + P],
                                       xth[:, k, tokens], xtl[:, k, tokens], k == 0, k == KT - 1)
                        mm.then_inc(proj_ps, 1)
                    if m >= 1:
                        k = m - 1
                        pe.wait_ge(qf_ready, c * OT + k + 3)
                        if k < ROT:
                            pe.wait_ge(rope_ready, before(c, k, ROT))
                            pe.matmul(bank[:, 4 + k % 2], rotate[:, :], qf[:, k % 2], start=True, stop=True).then_inc(rot_ps, 1)
                        else:
                            pe.wait_ge(v_ready, c + 1)
                            for t in range(TPC):
                                mm = pe.transpose(bank[:, 6, t * P:t * P + P], qf[:, k % 2, t * P:t * P + P], ident[:, :])
                            mm.then_inc(v_tp, 1)
                    if m in (OT - 2, OT - 1) and after is not None:
                        turn(after, (0, 1) if m == OT - 2 else (2, 3))
            chunks(pe, lambda now: turn(now, range(TPC)), body)


def layer1_ffn(nc, qw_gu, qw_d, hot_gu, hot_d, sd, zd, lane_shift, s_gu_scr, z_gu_scr, xth, xtl, acc):
    with ExitStack() as ctx:
        def sb(name, shape, dt=F32):
            return ctx.enter_context(nc.sbuf_tensor("d_" + name, shape, dt))

        def sem(name):
            return ctx.enter_context(nc.semaphore("d_" + name))

        W = 2 * P
        sz, zz = sb("sz", [2 * SG, 2, 2, W], F32R), sb("zz", [SG, 2, 2, W], F32R)
        hot = sb("hot", [2 * SD, 3, P], F32R)
        qw = sb("qw", [P, 2, 2 * W], U32)
        wq = sb("wq", [P, 2 * W], U32)
        wf = sb("wf", [P, 2 * W])
        wgh, wgl = sb("wgh", [P, 2, KT, 2, W], F32R), sb("wgl", [P, 2, KT, 2, W], F32R)
        wdh, wdl = sb("wdh", [P, 2, 2, E], F32R), sb("wdl", [P, 2, 2, E], F32R)
        hs = sb("hs", [P, 2, CH])
        hh, hl = sb("hh", [P, 2, CH], F32R), sb("hl", [P, 2, CH], F32R)
        bank = ctx.enter_context(nc.psum_tensor("d_bank", [P, 8, 512], F32))
        sz_in, qw_in2 = sem("sz_in"), sem("qw_in2")
        qw_in = [sem(f"qw_in{u}") for u in range(2)]
        hot_ready, row_ps, unpacked, w_ready = sem("hot_ready"), sem("row_ps"), sem("unpacked"), sem("w_ready")
        f1_ps, silu_ready, h_ready, hh_ready, hl_ready = (sem(n) for n in ("f1_ps", "silu_ready", "h_ready", "hh_ready", "hl_ready"))
        f2_tile, f2_ps, acc_ready = sem("f2_tile"), sem("f2_ps"), sem("acc_ready")

        def piece_number(s, b, n):
            return b * 3 + (6 * s + n)

        PIECES = [(0, "gu"), (1, "gu"), (2, "down")]

        def tile(s, b, u, n):
            return (b * 2 + u) * len(STEPS[s]) + (CHUNKS * sum(len(STEPS[k]) for k in range(s)) + n)

        def slot(s, u, n):
            return n if len(STEPS[s]) == 2 else u

        qgv = qw_gu.rearrange("r (h f) -> r h f", h=2)
        block = ctx.enter_context(nc.Block())

        def each_pair(eng, body):
            for s in range(-1, len(STEPS)):
                with eng.Fori(0, CHUNKS // 2) as b:
                    body(s, b)

        @block.sync
        def _(sp):
            def body(s, b):
                if s + 1 == len(STEPS):
                    return
                tiles = STEPS[s + 1]
                f0, w = tiles[0] * P, sum(FW[n] for n in tiles)
                for n, kind in PIECES:
                    number = piece_number(s + 1, b, n)
                    sp.wait_ge(unpacked, number + (1 if n == 0 else 0))
                    dst = qw[:, (n if kind == "gu" else 0)]
                    if kind == "gu":
                        src = qgv[bass.ds((b * 2 + n) * (P // PACK), P // PACK), :, f0:f0 + w]
                        for h in range(2):
                            sp.dma_start(dst[:, h * W:h * W + w],
                                         src[:, h].rearrange("r (o f) -> r o f", o=1).broadcast_to([P // PACK, PACK, w])).then_inc(qw_in[n], 16)
                    else:
                        rows = FW[tiles[0]] // PACK
                        at = b * (P // PACK) + f0 // PACK if len(tiles) > 1 else f0 // PACK
                        src = qw_d[bass.ds(at, rows), :] if len(tiles) > 1 else qw_d[at:at + rows, :]
                        sp.dma_start(dst[0:rows * PACK, :],
                                     src.rearrange("r (o f) -> r o f", o=1).broadcast_to([rows, PACK, E])).then_inc(qw_in2, 16)

            def scales(s):
                if s > 0:
                    sp.wait_ge(w_ready, 6 * s + 1)
                tiles = STEPS[s]
                f0, w = tiles[0] * P, sum(FW[n] for n in tiles)
                for scr, dst in ((s_gu_scr, sz), (z_gu_scr, zz)):
                    sp.dma_start(dst[:, s % 2, :, 0:w].bitcast(F32), scr.rearrange("r (h f) -> r h f", h=2)[:, :, f0:f0 + w]).then_inc(sz_in, 16)

            sp.sem_inc(unpacked, 1)
            scales(0)
            with sp.Fori(0, CHUNKS // 2) as b:
                body(-1, b)
            for s in range(len(STEPS) - 1):
                scales(s + 1)
                with sp.Fori(0, CHUNKS // 2) as b:
                    body(s, b)

        @block.vector
        def _(dve):
            dve.sem_inc(h_ready, 2)
            dve.sem_inc(hl_ready, 2)
            dve.sem_inc(w_ready, 1)
            dve.sem_inc(acc_ready, 1)

            def pick(s, b):
                tiles = STEPS[s]
                rows = FW[tiles[0]]
                for n in range(2):
                    dve.tensor_copy(hot[0:2 * SG, n], hot_gu[:, bass.ds((b * 2 + n) * P, P)]).then_inc(hot_ready, 1)
                at = bass.ds(b * P + tiles[0] * P, P) if len(tiles) > 1 else slice(tiles[0] * P, tiles[0] * P + rows)
                dve.tensor_copy(hot[:, 2, 0:rows], hot_d[:, at]).then_inc(hot_ready, 1)

            def piece(s, b, n, kind):
                tiles = STEPS[s]
                w = sum(FW[k] for k in tiles)
                number = piece_number(s, b, n)
                rows = P if kind == "gu" else FW[tiles[0]]
                if kind == "gu":
                    dve.wait_ge(qw_in[n], (b + (2 * s + 1)) * 32)
                    v3 = lambda a: a.rearrange("p (h f) -> p h f", h=2)[0:rows, :, 0:w]
                    src, into = qw[:, n], (wgh[:, s % 2, bass.ds(b * 2 + n, 1)], wgl[:, s % 2, bass.ds(b * 2 + n, 1)])
                    into = [a.rearrange("p k h f -> p (k h) f")[:, :, 0:w] for a in into]
                else:
                    dve.wait_ge(qw_in2, (b + (2 * s + 1)) * 16)
                    v3 = lambda a: a[0:rows]
                    k = bass.ds(b, 1) if len(tiles) > 1 else slice(0, 1)
                    src, into = qw[:, 0], [flat(a[:, s % 2, k])[0:rows] for a in (wdh, wdl)]
                first = 2 * (n % 2)
                dve.tensor_scalar(v3(wq[:, :]), v3(src), lane_shift[0:rows, 0:1], 15, ALU.logical_shift_right,
                                  ALU.bitwise_and).then_inc(unpacked, 1)
                dve.drain()
                dve.wait_ge(row_ps, number + 1)
                dve.tensor_tensor(v3(wf[:, :]), v3(wq[:, :]), v3(bank[:, first + 1]), ALU.subtract)
                dve.drain()
                dve.tensor_tensor(v3(wf[:, :]), v3(wf[:, :]), v3(bank[:, first]), ALU.mult)
                dve.drain()
                dve.tensor_copy(into[0], v3(wf[:, :]))
                dve.drain()
                dve.tensor_tensor(into[1], v3(wf[:, :]), into[0].bitcast(F32), ALU.subtract).then_inc(w_ready, 1)

            def product(s, b, u, n):
                k, v, rows = tile(s, b, u, n), slot(s, u, n), FW[STEPS[s][n]]
                dve.wait_ge(silu_ready, k + 1)
                dve.tensor_tensor(hs[0:rows, v], hs[0:rows, v], bank[0:rows, 2 * v + 1], ALU.mult).then_inc(h_ready, 1)
                dve.wait_ge(hh_ready, k + 1)
                dve.tensor_tensor(hl[0:rows, v], hs[0:rows, v], hh[0:rows, v].bitcast(F32), ALU.subtract).then_inc(hl_ready, 1)

            def gather(s, b, u):
                for t in range(TPC):
                    dve.wait_ge(f2_ps, (b * 2 + u) * TPC + (s * TILES + t + 2))
                    a = flat(acc[:, bass.ds((b * 2 + u) * TPC + t, 1), :])
                    if s == 0:
                        dve.tensor_copy(a, bank[:, 4 + t]).then_inc(acc_ready, 1)
                    else:
                        dve.tensor_tensor(a, a, bank[:, 4 + t], ALU.add).then_inc(acc_ready, 1)

            def body(s, b):
                if s == -1:
                    dve.wait_ge(sz_in, 32)
                    pick(0, b)
                    for n, kind in PIECES:
                        piece(0, b, n, kind)
                    return
                two, making = len(STEPS[s]) == 2, s + 1 < len(STEPS)
                if making:
                    pick(s + 1, b)
                product(s, b, 0, 0)
                if making:
                    piece(s + 1, b, *PIECES[0])
                if two:
                    product(s, b, 0, 1)
                if making:
                    piece(s + 1, b, *PIECES[1])
                product(s, b, 1, 0)
                gather(s, b, 0)
                if making:
                    piece(s + 1, b, *PIECES[2])
                if two:
                    product(s, b, 1, 1)
                gather(s, b, 1)
            each_pair(dve, body)

        @block.scalar
        def _(act):
            def body(s, b):
                if s == -1:
                    return
                for u in range(2):
                    for n in range(len(STEPS[s])):
                        k, v, rows = tile(s, b, u, n), slot(s, u, n), FW[STEPS[s][n]]
                        act.wait_ge(f1_ps, k + 1)
                        act.wait_ge(hl_ready, k + 1)
                        act.activation(hs[0:rows, v], bank[0:rows, 2 * v], ACT.Silu).then_inc(silu_ready, 1)
                        act.wait_ge(h_ready, k + 3)
                        if n + 1 < len(STEPS[s]):
                            act.wait_ge(f2_tile, b * 2 + (s * CHUNKS + u + 1))
                        else:
                            act.wait_ge(f2_ps, (b * 2 + u) * TPC + (s * TILES + 1))
                        act.activation(hh[0:rows, v], hs[0:rows, v], ACT.Copy).then_inc(hh_ready, 1)
            each_pair(act, body)

        @block.tensor
        def _(pe):
            pe.sem_inc(f2_ps, 1)
            pe.sem_inc(f2_tile, 1)

            def piece(s, b, n, kind):
                tiles = STEPS[s]
                w = sum(FW[k] for k in tiles)
                number = piece_number(s, b, n)
                first = 2 * (n % 2)
                pe.wait_ge(hot_ready, number + 1)
                pe.wait_ge(w_ready, number + (1 if n == 0 else 0))
                if kind == "gu":
                    out = [bank[:, first + k].rearrange("p (h f) -> p h f", h=2)[:, :, 0:w] for k in range(2)]
                    pe.matmul(out[0], hot[0:2 * SG, n], sz[:, s % 2, :, 0:w], start=True, stop=True)
                    pe.matmul(out[1], hot[0:SG, n], zz[:, s % 2, :, 0:w], start=True, stop=True).then_inc(row_ps, 1)
                else:
                    rows = FW[tiles[0]]
                    pe.matmul(bank[0:rows, first], hot[:, n, 0:rows], sd[:, :], start=True, stop=True)
                    pe.matmul(bank[0:rows, first + 1], hot[0:SD, n, 0:rows], zd[:, :], start=True, stop=True).then_inc(row_ps, 1)

            def gate_up(s, b, u, n, between=lambda: None):
                k, v, rows = tile(s, b, u, n), slot(s, u, n), FW[STEPS[s][n]]
                now = bass.ds((b * 2 + u) * CH, CH)
                pe.wait_ge(h_ready, k + 1)
                pe.wait_ge(w_ready, piece_number(s + 1, b, 0) + (n + 2 if u == 1 else 1) if s + 1 < len(STEPS)
                           else 6 * len(STEPS) + 1)
                for h in range(2):
                    if h == 1:
                        between()
                    for c in range(KT):
                        mm = three(pe, bank[0:rows, 2 * v + h], wgh[:, s % 2, c, h, n * P:n * P + rows],
                                   wgl[:, s % 2, c, h, n * P:n * P + rows], xth[:, c, now], xtl[:, c, now], c == 0, c == KT - 1)
                mm.then_inc(f1_ps, 1)

            def down(s, b, u, n):
                k, v, rows = tile(s, b, u, n), slot(s, u, n), FW[STEPS[s][n]]
                if n == 0:
                    pe.wait_ge(acc_ready, (b * 2 + u) * TPC + s * TILES + 1)
                pe.wait_ge(hl_ready, k + 3)
                last = n == len(STEPS[s]) - 1
                for t in range(TPC):
                    mm = three(pe, bank[:, 4 + t], hh[0:rows, v, t * P:t * P + P], hl[0:rows, v, t * P:t * P + P],
                               wdh[0:rows, s % 2, n], wdl[0:rows, s % 2, n], n == 0, last)
                    if last:
                        mm.then_inc(f2_ps, 1)
                if not last:
                    mm.then_inc(f2_tile, 1)

            def body(s, b):
                if s == -1:
                    pe.wait_ge(sz_in, 32)
                    for n, kind in PIECES:
                        piece(0, b, n, kind)
                    return
                two, making = len(STEPS[s]) == 2, s + 1 < len(STEPS)
                if making:
                    pe.wait_ge(sz_in, 32 * (s + 2))
                gate_up(s, b, 0, 0)

                def first_piece():
                    if making:
                        pe.wait_ge(h_ready, tile(s, b, 0, 0) + 3)
                        piece(s + 1, b, *PIECES[0])
                if two:
                    gate_up(s, b, 0, 1, first_piece)
                if two:
                    down(s, b, 0, 0)
                if making:
                    pe.wait_ge(h_ready, tile(s, b, 0, 1) + 3)
                    piece(s + 1, b, *PIECES[1])
                gate_up(s, b, 1, 0)
                down(s, b, 0, len(STEPS[s]) - 1)
                if making:
                    pe.wait_ge(h_ready, tile(s, b, 1, 0) + 3)
                    piece(s + 1, b, *PIECES[2])
                if two:
                    gate_up(s, b, 1, 1)
                    down(s, b, 1, 0)
                down(s, b, 1, len(STEPS[s]) - 1)
            each_pair(pe, body)


HG = G
QB = T // P
HALF = T // CH
QPH = CH // P
PART = 3 * D
M_ROW = 2 * PART
STACKS = 3
UNITS = [(0, k) for k in range(QPH)] + [(1, k) for k in (0, 4, 5, 6, 7, 1, 2, 3)]
NU, NC = len(UNITS), 2 * len(UNITS)
HEAD = 3
ITEMS = [(h, q, at, min(CH, (q + 1) * P - at)) for h in range(HG) for q in range(QB) for at in range(0, (q + 1) * P, CH)]
TURN_MAXIMA = 19
TURN_FIRST_HALF = 10
LOADED = 4 * 16
LEAST = -3.0e38
SPARE = 3


def beside(c):
    cost = [w + 96 for *_, w in ITEMS]
    upto = lambda x: sum(sum(cost[:s + 1]) <= sum(cost) * x / NC + 1e-6 for s in range(len(ITEMS)))
    at = (c - TURN_MAXIMA) % NC
    return range(upto(at), upto(at + 1))


EARLY = beside(NC - 1).stop


def tasks(ahead):
    out = []
    for c in range(NC):
        if c < TURN_MAXIMA and ahead >= 1:
            out += [(c, "items", s) for s in beside(c)]
        if c == HEAD - 1:
            out.append((c, "turn the group before", None))
        if c == TURN_FIRST_HALF:
            out.append((c, "turn half", None))
        if c >= TURN_MAXIMA and ahead >= 2:
            out += [(c, "early", s) for s in beside(c)]
        if c == TURN_MAXIMA and ahead >= 1:
            out.append((c, "turn maxima", None))
    return out


def layer1_attention(nc, ident_d, mask_d, fixed_d, q_scr, k_scr, v_all, ctx_sb):
    with ExitStack() as ctx:
        def sb(name, shape, dt=F32):
            return ctx.enter_context(nc.sbuf_tensor("f_" + name, shape, dt))

        def sem(name):
            return ctx.enter_context(nc.semaphore("f_" + name))

        ident, mask = sb("ident", [P, P]), sb("mask", [P, CH])
        fixed = sb("fixed", [P, 2, 1])
        qst = sb("qst", [P, STACKS, 2, T], F32R)
        kst = sb("kst", [P, STACKS, 2, T], F32R)
        vst = sb("vst", [P, STACKS, QB, 2 * D])
        prob = sb("prob", [P, 2, HG, CH])
        mx = sb("mx", [P, STACKS, 2, 2, QB])
        mx_first = sb("mx_first", [P, 2, 2, QB])
        mt = sb("mt", [HG * QB, STACKS, P], F32R)
        ctxt = sb("ctxt", [P, HALF, CH])
        rden = sb("rden", [P, QPH, HG])
        bank = ctx.enter_context(nc.psum_tensor("f_bank", [P, 8, 512], F32))
        spare = [bank[:, 0], bank[:, 1], bank[:, 7]]
        score_bank = [bank[:, 2:4], bank[:, 4:6]]
        sum_bank = bank[:, 6]
        const_in, cleared = sem("const_in"), sem("cleared")
        fixed_in = sem("fixed_in")
        item_seen, diag_seen = sem("item_seen"), sem("diag_seen")
        qk_in = [sem(f"qk_in{u}") for u in range(STACKS)]
        m_in = [sem(f"m_in{u}") for u in range(STACKS)]
        spare_ps, spare_free, mx_ready = (sem(n) for n in ("spare_ps", "spare_free", "mx_ready"))
        st_ps, exp_done, masked, av_done, vst_ready = (sem(n) for n in ("st_ps", "exp_done", "masked", "av_done", "vst_ready"))
        ctxt_ready = sem("ctxt_ready")
        NI = len(ITEMS)
        ROUNDS = (NG - 1) // STACKS

        def span(h, k):
            return max(0, k * P - h * CH)

        def diagonal(h, k):
            return k * P >= h * CH

        DIAG = 2 * sum(diagonal(*unit) for unit in UNITS)

        FULL = tasks(2)
        FIRST_USES = NI + 1 + EARLY

        def ahead_of(n):
            return min(2, NG - 1 - n) if isinstance(n, int) else 2

        def use(n, at):
            return n * len(FULL) + (FIRST_USES - 1 + at - (EARLY if ahead_of(n) == 0 else 0))

        def use_of(n, name):
            return use(n, [t for _, t, _ in tasks(ahead_of(n))].index(name))

        def group(j, k):
            return j * STACKS + k, k % STACKS, j + k // STACKS

        def groups(eng, step, tail):
            def run(c, j, k, first=False):
                todo = []
                n = j * STACKS + k
                for at, (cc, task, s) in enumerate(tasks(ahead_of(n))):
                    if cc == c and not (first and task == "turn the group before"):
                        at += 1 if first else 0
                        bank_at = use(k, at) if isinstance(n, int) else use(0, at) + k * len(FULL)
                        todo.append((use(n, at), bank_at % SPARE, task, s))
                step(c, group(j, k), todo, None if first else group(j, k - 1), group(j, k + 1), group(j, k + 2))

            assert len(FULL) % SPARE == 0
            for c in range(HEAD):
                run(c, 0, 0, True)
            with eng.Fori(0, ROUNDS - 1) as j:
                for k in range(STACKS):
                    for c in range(HEAD, NC):
                        run(c, j, k)
                    for c in range(HEAD):
                        run(c, j, k + 1)
            for n in range((ROUNDS - 1) * STACKS, NG):
                for c in range(HEAD if n == (ROUNDS - 1) * STACKS else 0, NC):
                    run(c, 0, n)
            tail(group(0, NG - 1), use(NG - 1, len(tasks(0))))

        block = ctx.enter_context(nc.Block())

        @block.sync
        def _(sp):
            def load(g):
                n, u, _ = g
                for par in range(2):
                    r = slice(par * PART, par * PART + PART)
                    sp.dma_start(kst[r, u, par].bitcast(F32), k_scr[bass.ds(n, 1)].rearrange("n c d t -> (n c d) t")).then_inc(qk_in[u], 16)
                    src = q_scr[bass.ds(n * HG, HG)].rearrange("(i p) c d t -> p (c d) i t", p=2)[par]
                    sp.dma_start(qst[r, u].bitcast(F32), src).then_inc(qk_in[u], 16)

            def maxima(g, first=False):
                n, u, _ = g
                sp.wait_ge(spare_free, (NI if first else use_of(n - 1, "turn maxima")) + 1 + SPARE)
                for par in range(2):
                    sp.dma_start(qst[M_ROW + par:M_ROW + par + 1, u].rearrange("o i (b q) -> o (i b) q", q=P).bitcast(F32),
                                 mt[par * 2 * QB:(par + 1) * 2 * QB, u].bitcast(F32)).then_inc(m_in[u], 16)

            def step(g, after, third):
                maxima(after)
                if third is not None:
                    sp.wait_ge(st_ps, g[0] * NC + NC)
                    load(third)

            sp.dma_start(fixed[:, :, :], fixed_d).then_inc(fixed_in, 16)
            for u in range(STACKS):
                sp.wait_ge(cleared, u + 1)
                load(group(0, u))
            maxima(group(0, 0), True)
            with sp.Fori(0, ROUNDS - 1) as j:
                for k in range(STACKS):
                    step(group(j, k), group(j, k + 1), group(j, k + STACKS))
            for k in range(STACKS):
                step(group(ROUNDS - 1, k), group(ROUNDS - 1, k + 1), group(ROUNDS - 1, k + STACKS) if k == 0 else None)

        @block.gpsimd
        def _(pool):
            def values(g):
                n, u, _ = g
                pool.tensor_copy(vst[:, u].rearrange("p b d -> p (b d)"),
                                 v_all[:, bass.ds(n, 1)].rearrange("p n b d -> p (n b d)")).then_inc(vst_ready, 1)

            def step(c, g, todo, before, after, second):
                n = g[0]
                h, k = UNITS[c // 2]
                if diagonal(h, k):
                    pool.wait_ge(exp_done, n * NC + (c + 3))
                    pool.sem_inc(diag_seen, 1)
                    p = prob[:, c // 2 % 2, c % 2 * 2:c % 2 * 2 + 2, span(h, k):span(h, k) + P]
                    pool.affine_select(out=p, in_=p, compare_op=ALU.is_ge, fill=0.0, base=0,
                                       pattern=[[0, 2], [1, P]], channel_multiplier=-1).then_inc(masked, 1)
                if c == HEAD and ahead_of(n) > 0:
                    pool.wait_ge(av_done, n * NU + 2)
                    values(after)
            values(group(0, 0))
            groups(pool, step, lambda *last: None)

        @block.scalar
        def _(act):
            act.dma_start(ident[:, :], ident_d).then_inc(const_in, 16)
            act.dma_start(mask[:, :], mask_d).then_inc(const_in, 16)
            act.sem_inc(exp_done, 2)
            act.sem_inc(ctxt_ready, 1)

            def turn(n, h):
                act.wait_ge(av_done, n * NU + (QPH if h == 0 else NU) + 2)
                act.wait_ge(spare_ps, (use_of(n - 1, "turn half") if h == 0 else use_of(n, "turn the group before")) + 1)
                act.activation(ctxt[:, h], sum_bank, ACT.Copy).then_inc(ctxt_ready, 1)

            def step(c, g, todo, before, after, second):
                n = g[0]
                lo = span(*UNITS[c // 2])
                if any(task == "turn the group before" for _, _, task, _ in todo):
                    turn(before[0], 1)
                if c == 2 * QPH + 2:
                    turn(n, 0)
                if c % 2 == 0:
                    act.wait_ge(av_done, n * NU + c // 2 + 1)
                act.wait_ge(st_ps, n * NC + c + 1)
                act.activation(prob[:, c // 2 % 2, c % 2 * 2:c % 2 * 2 + 2, lo:], score_bank[c % 2][:, :, lo:], ACT.Exp,
                               scale=D ** -0.5).then_inc(exp_done, 1)
            groups(act, step, lambda g, number: turn(g[0], 1))

        @block.vector
        def _(dve):
            dve.wait_ge(fixed_in, 16)
            for u in range(STACKS):
                dve.tensor_copy(kst[:, u], fixed[:, :, :].broadcast_to([P, 2, T])).then_inc(cleared, 1)
            dve.sem_inc(spare_free, SPARE)
            dve.wait_ge(const_in, 32)

            def item(g, s, number, v):
                u = g[1]
                h, q, at, w = ITEMS[s]
                sc = spare[v][:, 0:w]
                dve.wait_ge(spare_ps, number + 1)
                if at + w == (q + 1) * P:
                    dve.sem_inc(item_seen, 1)
                    dve.tensor_tensor_reduce(sc, sc, mask[:, CH - w:CH], 1.0, LEAST, ALU.add, ALU.max,
                                             mx[:, u, h % 2, h // 2, q:q + 1]).then_inc(spare_free, 1)
                else:
                    dve.tensor_reduce(mx_first[:, h % 2, h // 2, q:q + 1], sc, AX.X, ALU.max).then_inc(spare_free, 1)
                if s == NI - 1:
                    dve.drain()
                    more = mx[:, u, :, :, QPH:]
                    dve.tensor_tensor(more, more, mx_first[:, :, :, QPH:], ALU.max).then_inc(mx_ready, 1)
                    dve.drain()

            def maxima(g, number, v):
                u = g[1]
                dve.wait_ge(spare_ps, number + 1)
                dve.tensor_copy(mt[:, u], spare[v][0:HG * QB, 0:P]).then_inc(spare_free, 1)

            def normalize(g, h, number, v):
                n = g[0]
                dve.drain()
                dve.wait_ge(spare_ps, number + 1)
                turned = spare[v].rearrange("p (b h d) -> p b h d", h=HG, d=2 * D)
                dve.reciprocal(rden[:, :, :], turned[:, :, :, D])
                dve.drain()
                dve.tensor_tensor(ctx_sb[:, bass.ds(n, 1), h * QPH:(h + 1) * QPH].rearrange("p n b (h d) -> p (n b) h d", d=D),
                                  turned[:, :, :, 0:D], rden[:, :, :].rearrange("p b (h o) -> p b h o", o=1).broadcast_to([P, QPH, HG, D]),
                                  ALU.mult).then_inc(spare_free, 1)

            def step(c, g, todo, before, after, second):
                for number, v, task, s in todo:
                    if task == "items":
                        item(after, s, number, v)
                    elif task == "early":
                        item(second, s, number, v)
                    elif task == "turn maxima":
                        maxima(after, number, v)
                    elif task == "turn half":
                        normalize(g, 0, number, v)
                    else:
                        normalize(before, 1, number, v)

            for s in range(NI):
                item(group(0, 0), s, s, s % SPARE)
            maxima(group(0, 0), NI, NI % SPARE)
            for s in range(EARLY):
                item(group(0, 1), s, NI + 1 + s, (NI + 1 + s) % SPARE)
            groups(dve, step, lambda g, number: normalize(g, 1, number, number % SPARE))

        @block.tensor
        def _(pe):
            pe.sem_inc(av_done, 2)

            def item(g, s, number, v):
                _, u, turns = g
                h, q, at, w = ITEMS[s]
                if s == 0:
                    pe.wait_ge(qk_in[u], turns * LOADED + LOADED)
                pe.wait_ge(spare_free, number + 1)
                pe.matmul(spare[v][:, 0:w], qst[0:M_ROW, u, h // 2, q * P:q * P + P],
                          kst[0:M_ROW, u, h % 2, at:at + w], start=True, stop=True).then_inc(spare_ps, 1)

            def maxima(g, number, v):
                n, u, _ = g
                pe.wait_ge(spare_free, number + 1)
                pe.wait_ge(mx_ready, n + 1)
                pe.transpose(spare[v][0:HG * QB, 0:P], mx[:, u].rearrange("p a b c -> p (a b c)"), ident[:, :]).then_inc(spare_ps, 1)

            def scores(g, c):
                n, u, turns = g
                h, k = UNITS[c // 2]
                lo = span(h, k)
                if c == 0:
                    pe.wait_ge(m_in[u], turns * (16 * 2) + 16 * 2)
                pe.wait_ge(exp_done, n * NC + c + 1)
                for hh in range(2):
                    mm = pe.matmul(score_bank[c % 2][:, hh, lo:], kst[0:M_ROW + 2, u, hh, k * P:k * P + P],
                                   qst[0:M_ROW + 2, u, c % 2, h * CH + lo:(h + 1) * CH], start=True, stop=True)
                mm.then_inc(st_ps, 1)

            def weighed(g, i):
                n, u, _ = g
                h, k = UNITS[i]
                last = [kk for hh, kk in UNITS if hh == h][-1]
                pe.wait_ge(exp_done, n * NC + (2 * i + 4))
                if diagonal(h, k):
                    pe.wait_ge(masked, n * DIAG + 2 * sum(diagonal(*unit) for unit in UNITS[:i + 1]))
                if i == 0:
                    pe.wait_ge(vst_ready, n + 1)
                if k == 0:
                    pe.wait_ge(ctxt_ready, n * HALF + h + 1)
                lo = span(h, k)
                for hh in range(HG):
                    mm = pe.matmul(sum_bank[2 * D * hh:2 * D * (hh + 1), lo:], vst[:, u, k], prob[:, i % 2, hh, lo:],
                                   start=(k == 0), stop=(k == last))
                mm.then_inc(av_done, 1)

            def turn(g, h, number, v):
                n = g[0]
                pe.wait_ge(spare_free, number + 1)
                pe.wait_ge(ctxt_ready, n * HALF + h + 2)
                for b in range(QPH):
                    mm = pe.transpose(spare[v][:, b * P:b * P + P], ctxt[:, h, b * P:b * P + P], ident[:, :])
                mm.then_inc(spare_ps, 1)

            def step(c, g, todo, before, after, second):
                scores(g, c)

                def run(part):
                    for number, v, task, s in part:
                        if task == "items":
                            item(after, s, number, v)
                        elif task == "early":
                            item(second, s, number, v)
                        elif task == "turn maxima":
                            maxima(after, number, v)
                        elif task == "turn half":
                            turn(g, 0, number, v)
                        else:
                            turn(before, 1, number, v)
                run(todo[:1])
                if c > 1 and c % 2 == 1:
                    weighed(g, c // 2 - 1)
                elif c == 1 and before is not None:
                    weighed(before, NU - 1)
                run(todo[1:])

            def tail(g, number):
                weighed(g, NU - 1)
                turn(g, 1, number, number % SPARE)
            pe.wait_ge(const_in, 32)
            pe.wait_ge(cleared, STACKS)
            for s in range(NI):
                item(group(0, 0), s, s, s % SPARE)
            maxima(group(0, 0), NI, NI % SPARE)
            for s in range(EARLY):
                item(group(0, 1), s, NI + 1 + s, (NI + 1 + s) % SPARE)
            groups(pe, step, tail)


def layer1_output(nc, Wo, ident_d, x1_d, ctx_sb, acc, out):
    with ExitStack() as ctx:
        def sb(name, shape, dt=F32):
            return ctx.enter_context(nc.sbuf_tensor("g_" + name, shape, dt))

        def sem(name):
            return ctx.enter_context(nc.semaphore("g_" + name))

        ident = sb("ident", [P, P])
        wn = sb("wn", [P, KT, E])
        woh, wol = sb("woh", [P, KT, E], F32R), sb("wol", [P, KT, E], F32R)
        x1 = sb("x1", [P, TILES, E])
        th = sb("th", [P, 2, E])
        ct = sb("ct", [P, 2, E])
        cth, ctl = sb("cth", [P, 2, KT, P], F32R), sb("ctl", [P, 2, KT, P], F32R)
        bank = ctx.enter_context(nc.psum_tensor("g_bank", [P, 8, 512], F32))
        w_in, x_in = sem("w_in"), sem("x_in")
        w_tp, w_hi, w_lo = sem("w_tp"), sem("w_hi"), sem("w_lo")
        ct_ready, ct_tp, cth_ready, ctl_ready, proj_ps, out_ready = (
            sem(n) for n in ("ct_ready", "ct_tp", "cth_ready", "ctl_ready", "proj_ps", "out_ready"))
        read_ps, th_ready, th_used = sem("read_ps"), sem("th_ready"), sem("th_used")
        y_out = [sem(f"y_out{u}") for u in range(2)]
        k4 = lambda a: a.rearrange("p (k q) -> p k q", k=KT)
        outv = out.rearrange("b (t p) e -> p (b t) e", p=P)

        def tiles(eng, body):
            with eng.Fori(0, TILES // 2) as j:
                for u in range(2):
                    body(j * 2 + u, u, j)

        block = ctx.enter_context(nc.Block())

        def ahead(eng, first, second):
            first(0, 0)
            with eng.Fori(0, TILES // 2 - 1) as j:
                for u in range(2):
                    first(j * 2 + u + 1, 1 - u)
                    second(j * 2 + u, u)
            first(TILES - 1, 1)
            second(TILES - 2, 0)
            second(TILES - 1, 1)

        @block.sync
        def _(sp):
            sp.dma_start(wn[:, :, :], Wo.rearrange("(o p) e -> p o e", p=P)).then_inc(w_in, 16)
            sp.dma_start(ident[:, :], ident_d).then_inc(w_in, 16)
            sp.dma_start(x1[:, :, :], x1_d.rearrange("(t p) e -> p t e", p=P)).then_inc(x_in, 16)

            def body(t, u, j):
                sp.wait_ge(out_ready, t + 1)
                sp.dma_start(outv[:, bass.ds(t, 1)].rearrange("p t e -> p (t e)"),
                             x1[:, bass.ds(t, 1)].rearrange("p t e -> p (t e)")).then_inc(y_out[u], 16)
            tiles(sp, body)
            for u in range(2):
                sp.wait_ge(y_out[u], 16 * (TILES // 2))

        @block.gpsimd
        def _(pool):
            pool.sem_inc(ct_tp, 2)
            with pool.Fori(0, B) as b:
                for qb in range(QB):
                    pool.wait_ge(ct_tp, b * QB + qb + 1)
                    pool.tensor_copy(ct[:, qb % 2].rearrange("p (g d) -> p g d", g=HKV),
                                     ctx_sb[:, bass.ds(b * HKV, HKV), qb]).then_inc(ct_ready, 1)

        @block.scalar
        def _(act):
            for o in range(KT):
                act.wait_ge(w_tp, o + 1)
                act.activation(woh[:, :, o * P:o * P + P], k4(bank[:, o % 2]), ACT.Copy).then_inc(w_hi, 1)

            def body(t, u, j):
                act.wait_ge(ct_tp, t + 3)
                act.wait_ge(proj_ps, t + 1)
                act.activation(cth[:, u], k4(bank[:, u]), ACT.Copy).then_inc(cth_ready, 1)
                act.wait_ge(th_used, t + 1)
                act.activation(th[:, u], flat(acc[:, bass.ds(t, 1)]), ACT.Tanh, scale=0.5).then_inc(th_ready, 1)
            tiles(act, body)

        @block.vector
        def _(dve):
            for o in range(KT):
                dve.wait_ge(w_hi, o + 1)
                dve.tensor_tensor(wol[:, :, o * P:o * P + P], k4(bank[:, o % 2]), woh[:, :, o * P:o * P + P].bitcast(F32),
                                  ALU.subtract).then_inc(w_lo, 1)
            dve.sem_inc(ctl_ready, 2)
            dve.wait_ge(x_in, 16)

            def low_part(t, u):
                dve.wait_ge(cth_ready, t + 1)
                dve.tensor_tensor(ctl[:, u], k4(bank[:, u]), cth[:, u].bitcast(F32), ALU.subtract).then_inc(ctl_ready, 1)

            def finish(t, u):
                a = flat(acc[:, bass.ds(t, 1)])
                x = flat(x1[:, bass.ds(t, 1)])
                dve.wait_ge(th_ready, t + 1)
                dve.scalar_tensor_tensor(out=a, in0=th[:, u], scalar=1.0, in1=a, op0=ALU.add, op1=ALU.mult).then_inc(th_used, 1)
                dve.drain()
                dve.wait_ge(proj_ps, t + 3)
                dve.scalar_tensor_tensor(out=a, in0=bank[:, 2 + u], scalar=0.5, in1=a, op0=ALU.mult, op1=ALU.mult).then_inc(read_ps, 1)
                dve.drain()
                dve.tensor_tensor(x, x, a, ALU.add).then_inc(out_ready, 1)
            dve.sem_inc(read_ps, 2)
            dve.sem_inc(th_used, 2)
            ahead(dve, low_part, finish)

        @block.tensor
        def _(pe):
            pe.sem_inc(proj_ps, 2)
            pe.wait_ge(w_in, 32)
            for o in range(KT):
                if o >= 2:
                    pe.wait_ge(w_lo, o - 1)
                for k in range(KT):
                    mm = pe.transpose(bank[:, o % 2, k * P:k * P + P], wn[:, o, k * P:k * P + P], ident[:, :])
                mm.then_inc(w_tp, 1)
            pe.wait_ge(w_lo, KT)

            def turn(t, u):
                pe.wait_ge(ct_ready, t + 1)
                pe.wait_ge(ctl_ready, t + 1)
                for k in range(KT):
                    mm = pe.transpose(bank[:, u, k * P:k * P + P], ct[:, u, k * P:k * P + P], ident[:, :])
                mm.then_inc(ct_tp, 1)

            def product(t, u):
                pe.wait_ge(ctl_ready, t + 3)
                pe.wait_ge(read_ps, t + 1)
                for k in range(KT):
                    mm = three(pe, bank[:, 2 + u], cth[:, u, k], ctl[:, u, k], woh[:, k], wol[:, k], k == 0, k == KT - 1)
                mm.then_inc(proj_ps, 1)

            ahead(pe, turn, product)


def program(nc, i, out, x1=None):
    x1_d = nc.dram_tensor("x1_d", [TOKENS, E], F32).ap() if x1 is None else x1
    if x1 is None:
        layer0(nc, i["L0_attn_x"], i["L0_attn_Wq"], i["L0_attn_bq"], i["L0_attn_Wk"], i["L0_attn_bk"], i["L0_attn_Wv"],
               i["L0_attn_bv"], i["L0_ffn_gate_w"], i["L0_ffn_gate_b"], i["L0_ffn_w1"], i["L0_ffn_b1"], i["L0_ffn_w2"],
               i["L0_ffn_b2"], i["ident_d"], i["strength_d"], x1_d)
    q_scr = nc.dram_tensor("q_scr", [B * HKV * G, 3, D, T], F32).ap()
    k_scr = nc.dram_tensor("k_scr", [B * HKV, 3, D, T], F32).ap()
    s_gu_scr = nc.dram_tensor("s_gu_scr", [2 * SG, 2 * INTER], F32).ap()
    z_gu_scr = nc.dram_tensor("z_gu_scr", [SG, 2 * INTER], F32).ap()
    gi_scr = nc.dram_tensor("gi_scr", [E + INTER], F32).ap()
    with nc.sbuf_tensor("acc", [P, TILES, E], F32) as acc, nc.sbuf_tensor("v_all", [P, NG, T // P, 2 * D], F32) as v_all:
        with ExitStack() as ctx:
            def sb(name, shape, dt):
                return ctx.enter_context(nc.sbuf_tensor(name, shape, dt))

            xth, xtl = sb("xth1", [P, KT, TOKENS], F32R), sb("xtl1", [P, KT, TOKENS], F32R)
            hot_gu, hot_d = sb("hot_gu", [2 * SG, E], F32R), sb("hot_d", [2 * SD, INTER], F32R)
            sd, zd = sb("sd", [2 * SD, E], F32R), sb("zd", [SD, E], F32R)
            lane_shift = sb("lane_shift", [P, 1], U32)
            layer1_projections(nc, i["L1_attn_Wq"], i["L1_attn_Wk"], i["L1_attn_Wv"], i["ident_d"], i["rotate_d"], i["cos_d"],
                               i["sin_d"], x1_d, q_scr, k_scr, xth, xtl, v_all, i["L1_ffn_qzeros_gu"], i["L1_ffn_scales_gu"],
                               i["L1_ffn_g_idx_gu"], i["L1_ffn_qzeros_down"], i["L1_ffn_scales_down"], i["L1_ffn_g_idx_down"],
                               i["shift_d"], i["lane_shift_d"], i["row_d"], s_gu_scr, z_gu_scr, gi_scr, hot_gu, hot_d, sd, zd,
                               lane_shift, acc)
            layer1_ffn(nc, i["L1_ffn_qweight_gu"], i["L1_ffn_qweight_down"], hot_gu, hot_d, sd, zd, lane_shift, s_gu_scr,
                       z_gu_scr, xth, xtl, acc)
        with nc.sbuf_tensor("ctx_sb", [P, NG, T // P, HG * D], F32) as ctx_sb:
            layer1_attention(nc, i["ident_d"], i["mask_d"], i["fixed_d"], q_scr, k_scr, v_all, ctx_sb)
            layer1_output(nc, i["L1_attn_Wo"], i["ident_d"], x1_d, ctx_sb, acc, out)


def shape_constants():
    import numpy as np

    f = np.float32
    heads_per_tile = P // D
    c = {"ident_d": np.eye(P, dtype=f)}
    position = (np.arange(P)[:, None] + P * (np.arange(TILES) % (T // P))[None, :])
    text = position >= VISION
    c["strength_d"] = np.stack([text / f((T - VISION) * E), ~text / f(VISION * E)], 1).astype(f)
    inv = (f(1.0) / (f(500000.0) ** (np.arange(0, D, 2, dtype=f) / f(D)))).astype(f)
    wavelen = (f(2 * np.pi) / inv).astype(f)
    low = np.where(wavelen > f(1024.0), inv / f(32.0), inv).astype(f)
    smooth = ((f(1024) / wavelen - f(1.0)) / f(3.0)).astype(f)
    smoothed = ((f(1) - smooth) * low / f(32) + smooth * low).astype(f)
    medium = ~(wavelen < f(1024.0)) & ~(wavelen > f(256.0))
    freqs = (np.arange(T, dtype=f)[:, None] * np.where(medium, smoothed, low).astype(f)[None]).astype(f)
    emb = np.concatenate([freqs, freqs], -1)
    c["cos_d"] = np.tile(np.cos(emb).astype(f).T, (heads_per_tile, 1))
    c["sin_d"] = np.tile(np.sin(emb).astype(f).T, (heads_per_tile, 1))
    rotate = np.zeros((P, P), f)
    for m in range(P):
        first = m % D < D // 2
        rotate[m + D // 2 if first else m - D // 2, m] = -1 if first else 1
    c["rotate_d"] = rotate
    c["shift_d"] = np.tile((np.arange(PACK) * NBITS).astype(np.uint32), (P, 1))
    c["lane_shift_d"] = (np.arange(P) % PACK * NBITS).astype(np.uint32)[:, None]
    c["row_d"] = np.stack([np.arange(2 * SD) % SG, np.arange(2 * SD) % SD], 1).astype(f)
    mask = np.zeros((P, CH), f)
    mask[:, CH - P:] = np.triu(np.full((P, P), -1e30, f), 1)
    c["mask_d"] = mask
    fixed = np.zeros((P, 2, 1), f)
    fixed[M_ROW, 0], fixed[M_ROW + 1, 1] = -1, -1
    c["fixed_d"] = fixed
    return c


def kernel(**inputs):
    import numpy as np
    import concourse.bacc as bacc
    from concourse.bass_utils import run_bass_kernel_spmd

    nc = bacc.Bacc("TRN2", target_bir_lowering=False, num_devices=1)
    arrays = {name: np.ascontiguousarray(a) for name, a in {**inputs, **shape_constants()}.items()}
    handles = {name: nc.dram_tensor(name, a.shape, mybir.dt.from_np(a.dtype), kind="ExternalInput").ap() for name, a in arrays.items()}
    out = nc.dram_tensor("out", (B, T, E), F32, kind="ExternalOutput").ap()
    program(nc, handles, out)
    r = run_bass_kernel_spmd(nc, [arrays], core_ids=[0])
    return r.results[0]["out"]
```
